# Optimizing a Trainium2 kernel written in Bass

```python
import numpy as np
import jax
import jax.numpy as jnp

def _softmax(x, axis=-1):
    return jax.nn.softmax(x, axis=axis)

def _gelu(x):
    return jax.nn.gelu(x, approximate=True)

def _silu(x):
    return jax.nn.silu(x)

def _sigmoid(x):
    return jax.nn.sigmoid(x)

def _layernorm(x, axis=-1, eps=1e-05):
    m = jnp.mean(x, axis=axis, keepdims=True)
    v = jnp.var(x, axis=axis, keepdims=True)
    return (x - m) / jnp.sqrt(v + eps)

def _scatter_add(tgt, idx, src, axis=0):
    return tgt.at[idx].add(src)

def _segment_sum(src, seg, n):
    return jax.ops.segment_sum(src, seg, n)
kernel_name = 'mk_seq_postln_d2_jaxref_r8_4bdee6'

def setup_inputs(seed: int=0):
    np.random.seed(seed)
    _w = jnp.asarray

    def _L0_attn_setup():
        import jax, jax.numpy as jnp
        import numpy as np
        EMBED_DIM = 128
        NUM_HEADS = 16
        HEAD_SIZE = EMBED_DIM // NUM_HEADS
        MAX_EMBED_DIM = 256
        MAX_HEAD_SIZE = 128
        B, T = (4, 256)
        key = jax.random.key(seed)
        kx, kq, kk, kv = jax.random.split(key, 4)
        x = jax.random.normal(kx, (B, T, MAX_EMBED_DIM), dtype=jnp.float32)
        Wq = jax.random.normal(kq, (NUM_HEADS, MAX_HEAD_SIZE, MAX_EMBED_DIM), dtype=jnp.float32) * 0.02
        Wk = jax.random.normal(kk, (NUM_HEADS, MAX_HEAD_SIZE, MAX_EMBED_DIM), dtype=jnp.float32) * 0.02
        Wv = jax.random.normal(kv, (NUM_HEADS, MAX_HEAD_SIZE, MAX_EMBED_DIM), dtype=jnp.float32) * 0.02
        return {'x': x, 'Wq': Wq, 'Wk': Wk, 'Wv': Wv}
    _L0_attn_in = _L0_attn_setup()

    def _L0_ffn_setup():
        import jax, jax.numpy as jnp
        import numpy as np
        NUM_EXPERTS = 16
        C = 1.0
        key = jax.random.key(seed)
        k1, k2, k3 = jax.random.split(key, 3)
        b, s, h = (4, 256, 256)
        return {'x': jax.random.normal(k1, (b, s, h), dtype=jnp.float32), 'router_w': jax.random.normal(k2, (h, NUM_EXPERTS), dtype=jnp.float32) * 0.02, 'router_b': jnp.zeros((NUM_EXPERTS,), dtype=jnp.float32), 'expert_w': jax.random.normal(k3, (h, h), dtype=jnp.float32) * 0.02, 'expert_b': jnp.zeros((h,), dtype=jnp.float32)}
    _L0_ffn_in = _L0_ffn_setup()

    def _L1_attn_setup():
        import jax, jax.numpy as jnp
        import numpy as np
        B, T, C = (4, 512, 256)

        def _scan_op(a, bb):
            g_i, v_i = a
            g_j, v_j = bb
            return (g_j * g_i, g_j * v_i + v_j)
        key = jax.random.key(seed)
        k1, k2 = jax.random.split(key)
        x = jax.random.normal(k1, (B, T, C), dtype=jnp.float32)
        W = jax.random.normal(k2, (2 * C, C), dtype=jnp.float32) * (1.0 / np.sqrt(C))
        b = jnp.zeros((2 * C,), dtype=jnp.float32)
        return {'x': x, 'W': W, 'b': b}
    _L1_attn_in = _L1_attn_setup()

    def _L1_ffn_setup():
        import jax, jax.numpy as jnp
        import numpy as np
        B, S, D = (4, 256, 256)
        E, F, K = (8, 128, 2)
        SF = 128
        EPS = 1e-06

        def _rmsnorm(x, w, eps=EPS):
            var = jnp.mean(x * x, axis=-1, keepdims=True)
            return x * jax.lax.rsqrt(var + eps) * w
        key = jax.random.key(seed)
        ks = jax.random.split(key, 9)
        g = lambda k, shape, scale: jax.random.normal(k, shape, jnp.float32) * scale
        return {'x': g(ks[0], (B, S, D), 1.0), 'rms_weight': jnp.ones((D,), jnp.float32), 'router_w': g(ks[1], (D, E), 0.02), 'w_gate': g(ks[2], (E, D, F), 0.02), 'w_up': g(ks[3], (E, D, F), 0.02), 'w_down': g(ks[4], (E, F, D), 0.02), 'sw_gate': g(ks[5], (D, SF), 0.02), 'sw_up': g(ks[6], (D, SF), 0.02), 'sw_down': g(ks[7], (SF, D), 0.02)}
    _L1_ffn_in = _L1_ffn_setup()
    _d = {'L0_attn_x': _L0_attn_in['x'], 'L0_attn_Wq': _L0_attn_in['Wq'], 'L0_attn_Wk': _L0_attn_in['Wk'], 'L0_attn_Wv': _L0_attn_in['Wv'], 'L0_ffn_router_w': _L0_ffn_in['router_w'], 'L0_ffn_router_b': _L0_ffn_in['router_b'], 'L0_ffn_expert_w': _L0_ffn_in['expert_w'], 'L0_ffn_expert_b': _L0_ffn_in['expert_b'], 'L1_attn_W': _L1_attn_in['W'], 'L1_attn_b': _L1_attn_in['b'], 'L1_ffn_rms_weight': _L1_ffn_in['rms_weight'], 'L1_ffn_router_w': _L1_ffn_in['router_w'], 'L1_ffn_w_gate': _L1_ffn_in['w_gate'], 'L1_ffn_w_up': _L1_ffn_in['w_up'], 'L1_ffn_w_down': _L1_ffn_in['w_down'], 'L1_ffn_sw_gate': _L1_ffn_in['sw_gate'], 'L1_ffn_sw_up': _L1_ffn_in['sw_up'], 'L1_ffn_sw_down': _L1_ffn_in['sw_down']}
    _x0 = _d['L0_attn_x']
    _d['L0_attn_x'] = jax.random.normal(jax.random.fold_in(jax.random.key(seed), 1), (8, 256, 256), dtype=_x0.dtype)
    del _x0
    return _d

def reference(L0_attn_x, L0_attn_Wq, L0_attn_Wk, L0_attn_Wv, L0_ffn_router_w, L0_ffn_router_b, L0_ffn_expert_w, L0_ffn_expert_b, L1_attn_W, L1_attn_b, L1_ffn_rms_weight, L1_ffn_router_w, L1_ffn_w_gate, L1_ffn_w_up, L1_ffn_w_down, L1_ffn_sw_gate, L1_ffn_sw_up, L1_ffn_sw_down):

    def _L0_attn_ref(x, Wq, Wk, Wv):
        import jax, jax.numpy as jnp
        import numpy as np
        EMBED_DIM = 128
        NUM_HEADS = 16
        HEAD_SIZE = EMBED_DIM // NUM_HEADS
        MAX_EMBED_DIM = 256
        MAX_HEAD_SIZE = 128
        B, T = (4, 256)
        Bx, Tx, _ = x.shape
        xs = x[:, :, :EMBED_DIM]
        wq = Wq[:, :HEAD_SIZE, :EMBED_DIM]
        wk = Wk[:, :HEAD_SIZE, :EMBED_DIM]
        wv = Wv[:, :HEAD_SIZE, :EMBED_DIM]
        q = jnp.einsum('bte,hde->bhtd', xs, wq)
        k = jnp.einsum('bte,hde->bhtd', xs, wk)
        v = jnp.einsum('bte,hde->bhtd', xs, wv)
        scale = jnp.asarray(HEAD_SIZE, x.dtype) ** (-0.5)
        wei = jnp.einsum('bhtd,bhsd->bhts', q, k) * scale
        causal = jnp.tril(jnp.ones((Tx, Tx), dtype=bool))
        wei = jnp.where(causal, wei, jnp.asarray(-jnp.inf, wei.dtype))
        wei = jax.nn.softmax(wei, axis=-1)
        out = jnp.einsum('bhts,bhsd->bhtd', wei, v)
        out = out.transpose(0, 2, 1, 3).reshape(Bx, Tx, NUM_HEADS * HEAD_SIZE)
        pad = MAX_EMBED_DIM - NUM_HEADS * HEAD_SIZE
        return jnp.pad(out, ((0, 0), (0, 0), (0, pad)))

    def _L0_ffn_ref(x, router_w, router_b, expert_w, expert_b):
        import jax, jax.numpy as jnp
        import numpy as np
        NUM_EXPERTS = 16
        C = 1.0
        b, s, h = x.shape
        bs = b * s
        k = min(int(bs * C / NUM_EXPERTS), bs)
        xf = x.reshape(bs, h)
        logits = xf @ router_w + router_b
        S = jax.nn.softmax(logits, axis=-1)
        G, idx = jax.lax.top_k(S.T, k)
        tokens = xf[idx]
        out = jnp.einsum('ekh,hd->ekd', tokens, expert_w) + expert_b
        weighted = G[..., None] * out
        y = jnp.zeros((bs, h), dtype=x.dtype).at[idx.reshape(-1)].add(weighted.reshape(-1, h))
        return y.reshape(b, s, h)

    def _L1_attn_ref(x, W, b):
        import jax, jax.numpy as jnp
        import numpy as np
        B, T, C = (4, 512, 256)

        def _scan_op(a, bb):
            g_i, v_i = a
            g_j, v_j = bb
            return (g_j * g_i, g_j * v_i + v_j)
        params = jnp.einsum('btc,dc->btd', x, W) + b
        gates, values = jnp.split(params, 2, axis=-1)
        gates = jax.nn.sigmoid(gates)
        values = jnp.tanh(values)
        _, hidden = jax.lax.associative_scan(_scan_op, (gates, values), axis=1)
        return hidden

    def _L1_ffn_ref(x, rms_weight, router_w, w_gate, w_up, w_down, sw_gate, sw_up, sw_down):
        import jax, jax.numpy as jnp
        import numpy as np
        B, S, D = (4, 256, 256)
        E, F, K = (8, 128, 2)
        SF = 128
        EPS = 1e-06

        def _rmsnorm(x, w, eps=EPS):
            var = jnp.mean(x * x, axis=-1, keepdims=True)
            return x * jax.lax.rsqrt(var + eps) * w
        b, s, d = x.shape
        e = router_w.shape[1]
        h = _rmsnorm(x, rms_weight)
        ht = h.reshape(-1, d)
        t = ht.shape[0]
        logits = ht @ router_w
        probs = jax.nn.softmax(logits, axis=-1)
        topv, topi = jax.lax.top_k(probs, K)
        topv = topv / jnp.sum(topv, axis=-1, keepdims=True)
        w_dense = jnp.zeros((t, e), ht.dtype).at[jnp.arange(t)[:, None], topi].set(topv)
        g = jnp.einsum('td,edf->tef', ht, w_gate)
        u = jnp.einsum('td,edf->tef', ht, w_up)
        eo = jnp.einsum('tef,efd->ted', jax.nn.silu(g) * u, w_down)
        moe = jnp.einsum('te,ted->td', w_dense, eo)
        sh = jax.nn.silu(ht @ sw_gate) * (ht @ sw_up) @ sw_down
        return (moe + sh).reshape(b, s, d)
    x = L0_attn_x
    x = _layernorm(x + _L0_attn_ref(x, L0_attn_Wq, L0_attn_Wk, L0_attn_Wv), axis=-1)
    x = _layernorm(x + _L0_ffn_ref(x, L0_ffn_router_w, L0_ffn_router_b, L0_ffn_expert_w, L0_ffn_expert_b), axis=-1)
    x = _layernorm(x + _L1_attn_ref(x, L1_attn_W, L1_attn_b), axis=-1)
    x = _layernorm(x + _L1_ffn_ref(x, L1_ffn_rms_weight, L1_ffn_router_w, L1_ffn_w_gate, L1_ffn_w_up, L1_ffn_w_down, L1_ffn_sw_gate, L1_ffn_sw_up, L1_ffn_sw_down), axis=-1)
    return x

_drawn_inputs = setup_inputs


def setup_inputs(seed=0):
    import zlib

    import numpy as np

    out = dict(_drawn_inputs(seed))
    spreads = {'L0_ffn_router_b': (0.0, 0.8),
     'L0_ffn_expert_b': (0.0, 0.491),
     'L1_attn_b': (0.0, 0.1),
     'L1_ffn_rms_weight': (1.0, 0.6)}
    factors = {'L0_attn_Wq': 8.0,
     'L0_attn_Wk': 8.0,
     'L1_ffn_router_w': 7.259,
     'L1_ffn_w_gate': 6.31,
     'L1_ffn_w_up': 6.267,
     'L1_ffn_w_down': 6.26,
     'L1_ffn_sw_gate': 4.564,
     'L1_ffn_sw_up': 4.452,
     'L1_ffn_sw_down': 4.471}
    for name, (base, spread) in spreads.items():
        noise = np.random.default_rng([zlib.crc32(name.encode()), seed]).standard_normal(out[name].shape)
        drawn = base * np.exp(spread * noise) if base else spread * noise
        out[name] = jnp.asarray(drawn.astype(out[name].dtype))
    for name, factor in factors.items():
        out[name] = (out[name] * factor).astype(out[name].dtype)
    return out
```

```python
from contextlib import ExitStack

import concourse.bass as bass
from concourse import mybir

F32 = mybir.dt.float32
BF16 = mybir.dt.bfloat16
I32 = mybir.dt.int32
ACT = mybir.ActivationFunctionType
ALU = mybir.AluOpType
AX = mybir.AxisListType

P = 128
NB, T, C = 8, 256, 256
TT = T // P
NT = NB * TT
HC = 128
NH, HD = 16, 8
PAIRS = NH // 2
SLOTS = 6
KS = SLOTS * HD
KM = KS + 3
VW = 32
NEG = -1.0e30
SCALE = float(HD) ** -0.5
LN_EPS = 1e-5
E0 = 16
TOP = NB * T // E0
BITS = 30
E1, TOP1 = 8, 2
FF = 128
RMS_EPS = 1e-6
Q = 4
QT = NT // Q
QN = QT * P
MISC = 12


def program(nc, x_in, Wq, Wk, Wv, r0_w, r0_b, e0_w, e0_b, W1, b1, rms_w, r1_w, w_gate, w_up, w_down,
            sw_gate, sw_up, sw_down, out):
    with ExitStack() as whole:
        def keep(name, shape, dt=F32):
            return whole.enter_context(nc.sbuf_tensor(name, shape, dt))

        m = Kept()
        m.x = keep("x", [P, NT, C])
        m.xT = keep("xT", [P, 2, NB * T])
        m.sg = keep("sg", [P, NT, E0])
        m.ident = keep("ident", [P, P])
        m.half_neg = keep("half_neg", [P, NT])
        m.same = keep("same", [P, NB, E0])
        m.before = keep("before", [P, NB, E0])
        m.ones = keep("ones", [P, P])
        m.e0w = keep("e0w", [P, 2, C])
        m.e0b = keep("e0b", [1, C])
        m.w1_nat = keep("w1_nat", [P, 4, C])
        m.b1 = keep("b1s", [P, 4])
        m.rms = keep("rms", [P, 2])
        m.r1w = keep("r1w", [P, 2, E1])
        m.wg = keep("wg", [P, E1 + 1, 2, FF])
        m.wu = keep("wu", [P, E1 + 1, 2, FF])
        m.wd = keep("wd", [FF, E1 + 1, C])
        attention(nc, m, x_in, Wq, Wk, Wv, r0_w, r0_b, e0_w, e0_b, W1, b1, rms_w, r1_w, w_gate, w_up, w_down,
                  sw_gate, sw_up, sw_down)
        rest_of_layers(nc, m, out)


class Kept:
    pass


def attention(nc, m, x_in, Wq, Wk, Wv, r0_w, r0_b, e0_w, e0_b, W1, b1, rms_w, r1_w, w_gate, w_up, w_down,
              sw_gate, sw_up, sw_down):
    with ExitStack() as ctx:
        x, xT, sg, ident, half_neg = m.x, m.xT, m.sg, m.ident, m.half_neg

        def sb(name, shape, dt=F32):
            return ctx.enter_context(nc.sbuf_tensor(name, shape, dt))

        def psum(name, shape, dt=F32):
            return ctx.enter_context(nc.psum_tensor(name, shape, dt))

        def sem(name):
            return ctx.enter_context(nc.semaphore(name))

        def at_least(eng, s, n):
            if n > 0:
                eng.wait_ge(s, n)

        w_nat = sb("w_nat", [P, 3, P])
        wT = sb("wT", [P, 3 * P])
        ident_b = sb("ident_b", [P, P], BF16)
        causal = sb("causal", [P, 4, P], BF16)
        in_T = sb("in_T", [P, 2, T])
        stack = sb("stack", [P, 2, TT, NH, 64], BF16)
        rest = sb("rest", [P, TT, 2 * P])
        rest_b = sb("rest_b", [P, TT, 2 * P], BF16)
        kT = sb("kT", [P, 2, PAIRS, T], BF16)
        qT = sb("qT", [P, 2, 2, PAIRS, T], BF16)
        vaug = sb("vaug", [P, 3, TT, NH, VW])
        mx = sb("mx", [P, TT, 2, PAIRS])
        nmr = sb("nmr", [P, TT, 2, PAIRS])
        nm = sb("nm", [P, TT, 2, 3, PAIRS], BF16)
        nmT = sb("nmT", [2 * 3 * PAIRS, T], BF16)
        probs = sb("probs", [P, 2, 6, 512])
        oT = sb("oT", [P, 2, 2, 2, T])
        rden = sb("rden", [P, NH])
        attn = sb("attn", [P, TT, 2, PAIRS, HD])
        bst = sb("bst", [P, TT, 6])
        mv = sb("mv", [P, TT, 2])
        rstd = sb("rstd", [P, TT])
        shift = sb("shift", [P, TT])
        rb0 = sb("rb0", [P, E0])
        r0w = sb("r0w", [P, 2, E0])
        lg = sb("lg", [P, TT, E0])
        lgm = sb("lgm", [P, TT])

        misc = [psum(f"misc{i}", [P, 512]) for i in range(2)]
        abank = [psum(f"abank{i}", [P, 512]) for i in range(2)]
        bbank = [psum(f"bbank{i}", [P, 512]) for i in range(3)]
        obank = psum("obank", [P, 512])

        ld_w = sem("ld_w")
        ld_x = [sem(f"ld_x{b}") for b in range(NB)]
        consts = sem("consts")
        wT_ps, wT_sb = sem("wT_ps"), sem("wT_sb")
        inT_ps, inT_sb = sem("inT_ps"), sem("inT_sb")
        qkv_ps, part_a, part_r, part_b, parts = sem("qkv_ps"), sem("part_a"), sem("part_r"), sem("part_b"), sem("parts")
        fill_ps, k_sb, q_sb = sem("fill_ps"), sem("k_sb"), sem("q_sb")
        a_ps, a_max = sem("a_ps"), sem("a_max")
        nm_tok, nmT_ps, nmT_sb, nm_rows = sem("nm_tok"), sem("nmT_ps"), sem("nmT_sb"), sem("nm_rows")
        b_ps, b_exp, b_cut, pv_ps, o_sb = sem("b_ps"), sem("b_exp"), sem("b_cut"), sem("pv_ps"), sem("o_sb")
        ot_ps = sem("ot_ps")
        ln_mv, ln_rs, ln_x = sem("ln_mv"), sem("ln_rs"), sem("ln_x")
        xT_ps, xT_sb = sem("xT_ps"), sem("xT_sb")
        lg_ps, lg_in, lg_sub, lg_exp, s_tok = sem("lg_ps"), sem("lg_in"), sem("lg_sub"), sem("lg_exp"), sem("s_tok")
        o_div, added, filled = sem("o_div"), sem("added"), sem("filled")
        dve_c, act_c, pool_c = sem("dve_c"), sem("act_c"), sem("pool_c")
        ld_later, masks = sem("ld_later"), sem("masks")

        def uses(s):
            nxt, now, cur, prev = 0 <= s + 1 < NB, 0 <= s < NB, 0 <= s - 1 < NB, 0 <= s - 2 < NB
            return [cur, now, now, prev, prev, nxt, nxt, nxt, nxt, nxt, prev, prev]

        NMT, FILL2, FILL3, OT0, OT1, INT, QKV0, QKV1, FILL0, FILL1, XT, LG = range(MISC)
        fills = [FILL0, FILL1, FILL2, FILL3]
        emptied = {NMT: (-1, nmT_sb, 1, 1), OT0: (-2, o_div, 2, 1), OT1: (-2, o_div, 2, 2), INT: (1, inT_sb, 1, 1),
                   QKV0: (1, part_r, 2, 1), QKV1: (1, part_r, 2, 2), XT: (-2, xT_sb, 1, 1),
                   LG: (-2, lg_in, 1, 1), FILL0: (1, q_sb, 8, 2), FILL1: (1, q_sb, 8, 4),
                   FILL2: (0, q_sb, 8, 6), FILL3: (0, q_sb, 8, 8)}

        def chunk(k):
            u, c = divmod(k, 6)
            js = range(4) if c < 2 else (range(0, 2) if c < 4 else range(2, 4))
            return u, c, c % 2, [4 * u + j for j in js]

        def fill_view(b, f):
            return misc[fills[f] % 2][:, :].bitcast(BF16).rearrange("p (a r t) -> p a r t", a=2, r=2)

        block = ctx.enter_context(nc.Block())

        @block.sync
        def _(sp):
            sp.dma_start(x[:, 0:TT, :], x_in[0].rearrange("(n p) c -> p n c", p=P)).then_inc(ld_x[0], 16)
            for i, w in enumerate((Wq, Wk, Wv)):
                sp.dma_start(w_nat[:, i, :], w[:, 0:HD, 0:HC]).then_inc(ld_w, 16)
            sp.dma_start(r0w[:, :, :], r0_w.rearrange("(k p) e -> p k e", p=P)).then_inc(ld_w, 16)
            sp.dma_start(rb0[:, :], r0_b.partition_broadcast(P)).then_inc(ld_w, 16)
            for b in range(1, NB):
                sp.dma_start(x[:, TT * b:TT * (b + 1), :],
                             x_in[b].rearrange("(n p) c -> p n c", p=P)).then_inc(ld_x[b], 16)
            later = [(m.e0w[:, :, :], e0_w.rearrange("(k p) c -> p k c", p=P)), (m.e0b[:, :], e0_b.unsqueeze(0)),
                     (m.w1_nat[:, :, :], W1.rearrange("(n p) c -> p n c", p=P)),
                     (m.b1[:, :], b1.rearrange("(n p) -> p n", p=P)),
                     (m.rms[:, :], rms_w.rearrange("(k p) -> p k", p=P)),
                     (m.r1w[:, :, :], r1_w.rearrange("(k p) e -> p k e", p=P)),
                     (m.wg[:, 0, :, :], sw_gate.rearrange("(k p) f -> p k f", p=P)),
                     (m.wu[:, 0, :, :], sw_up.rearrange("(k p) f -> p k f", p=P)), (m.wd[:, 0, :], sw_down),
                     (m.wg[:, 1:, :, :], w_gate.rearrange("e (k p) f -> p e k f", p=P)),
                     (m.wu[:, 1:, :, :], w_up.rearrange("e (k p) f -> p e k f", p=P)),
                     (m.wd[:, 1:, :], w_down.rearrange("e f c -> f e c"))]
            for dst, src in later:
                sp.dma_start(dst, src, allow_slow_non_contiguous=True).then_inc(ld_later, 16)
            for b in range(NB):
                sp.wait_ge(nmT_sb, b + 1)
                for par in range(2):
                    sp.dma_start(qT[64 * par + KS:64 * par + KM, b % 2, par, :, :],
                                 nmT[24 * par:24 * par + 24, :]
                                 ).then_inc(nm_rows, 16)
            sp.wait_ge(ld_later, 16 * len(later))

        N_LDW = 16 * (3 + 2)

        @block.gpsimd
        def _(pool):
            pool.memset(ident[:, :], 0.0).then_inc(pool_c, 1)
            pool.memset(ident_b[:, :], 0.0).then_inc(pool_c, 1)
            pool.memset(causal[:, :, :], 0.0).then_inc(pool_c, 1)
            pool.memset(half_neg[:, :], -0.5).then_inc(pool_c, 1)
            pool.wait_ge(pool_c, 4)
            for one in (ident, ident_b):
                pool.affine_select(out=one[:, :], in_=one[:, :], compare_op=ALU.not_equal, fill=1.0, base=0,
                                   pattern=[[-1, P]], channel_multiplier=1).then_inc(consts, 1)
            pool.affine_select(out=causal[:, :, :], in_=causal[:, :, :], compare_op=ALU.is_ge, fill=NEG, base=0,
                               pattern=[[0, 4], [-1, P]], channel_multiplier=1).then_inc(consts, 1)

            pool.memset(m.ones[:, :], 1.0).then_inc(pool_c, 1)
            pool.memset(m.same[:, 0, :], 0.0).then_inc(masks, 1)
            for c in range(NB):
                pool.wait_ge(masks, c + 1)
                pool.affine_select(out=m.same[:, 0, :], in_=m.same[:, 0, :], compare_op=ALU.not_equal, fill=1.0,
                                   base=-E0 * c, pattern=[[-1, E0]], channel_multiplier=1).then_inc(masks, 1)
            pool.wait_ge(masks, NB + 1)
            pool.tensor_copy(m.same[:, 1:, :], m.same[:, 0:1, :].to_broadcast([P, NB - 1, E0])).then_inc(masks, 1)
            pool.wait_ge(masks, NB + 2)
            pool.affine_select(out=m.before[:, :, :], in_=m.same[:, :, :], compare_op=ALU.is_gt, fill=0.0, base=0,
                               pattern=[[E0, NB], [0, E0]], channel_multiplier=-1).then_inc(masks, 1)

            def cut(b, u, lo, hi):
                pool.wait_ge(b_exp, 12 * b + 6 * u + hi)
                w = P if lo == 0 else T
                part = probs[:, u, lo:hi, :].rearrange("p c (h t) -> p (c h) t", t=w)[:, :, 0:P]
                pool.affine_select(out=part, in_=part, compare_op=ALU.is_ge, fill=0.0, base=0,
                                   pattern=[[0, 8], [1, P]], channel_multiplier=-1).then_inc(b_cut, 1)

            def add_attn(b):
                for t in range(TT):
                    pool.wait_ge(o_div, TT * b + t + 1)
                    xv = x[:, TT * b + t, 0:HC].rearrange("p (r a d) -> p a r d", a=2, d=HD)
                    pool.tensor_tensor(xv, xv, attn[:, t, :, :, :], ALU.add).then_inc(added, 1)

            def normalise(b):
                pool.wait_ge(ln_mv, b + 1)
                pool.tensor_tensor(rstd[:, :], mv[:, :, 1], half_neg[:, 0:TT], ALU.pow).then_inc(ln_rs, 1)
                pool.wait_ge(ln_rs, 2 * b + 1)
                pool.tensor_tensor(shift[:, :], mv[:, :, 0], rstd[:, :], ALU.mult).then_inc(ln_rs, 1)
                pool.wait_ge(ln_rs, 2 * b + 2)
                for t in range(TT):
                    xv = x[:, TT * b + t, :]
                    pool.tensor_scalar(xv, xv, rstd[:, t:t + 1], shift[:, t:t + 1], ALU.mult, ALU.subtract
                                       ).then_inc(ln_x, 1)

            for s in range(-1, NB + 2):
                nxt, cur, prev = 0 <= s + 1 < NB, 0 <= s - 1 < NB, 0 <= s - 2 < NB
                if prev:
                    add_attn(s - 2)
                if cur:
                    cut(s - 1, 0, 0, 2)
                if prev:
                    normalise(s - 2)
                if cur:
                    cut(s - 1, 0, 2, 6)
                    cut(s - 1, 1, 0, 2)
                    cut(s - 1, 1, 2, 6)
        N_CONST = 3

        @block.scalar
        def _(act):
            act.wait_ge(wT_ps, 1)
            act.copy(wT[:, :], misc[0][:, 0:3 * P]).then_inc(wT_sb, 1)

            def nmT_out(b):
                act.wait_ge(nmT_ps, b + 1)
                at_least(act, nm_rows, 32 * b)
                act.copy(nmT[:, :], misc[NMT % 2][:, :].bitcast(BF16)[0:48, 0:T]).then_inc(nmT_sb, 1)

            def inT_out(b):
                act.wait_ge(inT_ps, b + 1)
                act.copy(in_T[:, b % 2, :], misc[INT % 2][:, 0:T]).then_inc(inT_sb, 1)

            def qkv_out(b, t):
                act.wait_ge(qkv_ps, TT * b + t + 1)
                bank = misc[(QKV0 + t) % 2]
                if b == 0 and t == 0:
                    act.wait_ge(filled, 6)
                if b >= 3 and t == 0:
                    act.wait_ge(pv_ps, 2 * (b - 2))
                act.copy(vaug[:, b % 3, t, :, 0:HD],
                         bank[:, 2 * P:3 * P].rearrange("p (h d) -> p h d", d=HD)).then_inc(act_c, 1)
                if b >= 1 and t == 0:
                    act.wait_ge(fill_ps, 4 * b)
                act.copy(stack[:, :, t, :, 0:HD],
                         bank[:, 0:2 * P].rearrange("p (a h d) -> p a h d", a=2, d=HD)).then_inc(part_a, 1)

            def exps(b, k):
                n = 12 * b + k
                u = k // 6
                act.wait_ge(b_ps, n + 1)
                if k % 6 == 0:
                    at_least(act, pv_ps, 2 * b + u - 1)
                act.activation(probs[:, u, k % 6, :], bbank[n % 3][:, :], ACT.Exp, scale=SCALE).then_inc(b_exp, 1)

            def o_out(b, u):
                act.wait_ge(pv_ps, 2 * b + u + 1)
                if u == 0:
                    at_least(act, ot_ps, TT * (b - 1))
                act.copy(oT[:, b % 2, u, :, :], obank[:, :].rearrange("p (a t) -> p a t", a=2)).then_inc(o_sb, 1)

            def xT_out(b):
                act.wait_ge(xT_ps, b + 1)
                act.copy(xT[:, :, b * T:(b + 1) * T],
                         misc[XT % 2][:, :].rearrange("p (k t) -> p k t", k=2)).then_inc(xT_sb, 1)

            def fill_out(b, f):
                act.wait_ge(fill_ps, 4 * b + f + 1)
                if b >= 2:
                    act.wait_ge(b_ps, 12 * (b - 2) + 6 * (f // 2) + 6)
                act.copy(kT[:, b % 2, 2 * f:2 * f + 2, :], fill_view(b, f)[:, 1]).then_inc(k_sb, 1)

            def lg_out(b):
                act.wait_ge(lg_sub, b + 1)
                act.activation(sg[:, TT * b:TT * (b + 1), :], lg[:, :, :], ACT.Exp).then_inc(lg_exp, 1)

            for s in range(-1, NB + 2):
                nxt, now, cur, prev = 0 <= s + 1 < NB, 0 <= s < NB, 0 <= s - 1 < NB, 0 <= s - 2 < NB
                if cur:
                    nmT_out(s - 1)
                if now:
                    fill_out(s, 2)
                if prev:
                    o_out(s - 2, 1)
                if now:
                    fill_out(s, 3)
                for k in range(3, 12):
                    if cur:
                        exps(s - 1, k - 3)
                    if nxt and k == 3:
                        inT_out(s + 1)
                    if nxt and k in (4, 5):
                        qkv_out(s + 1, k - 4)
                    if nxt and k in (10, 11):
                        fill_out(s + 1, k - 10)
                if cur:
                    exps(s - 1, 9)
                    o_out(s - 1, 0)
                if prev:
                    xT_out(s - 2)
                if cur:
                    exps(s - 1, 10)
                    exps(s - 1, 11)
                if prev:
                    lg_out(s - 2)

        @block.vector
        def _(dve):
            ticks = [0]

            def tick(ins):
                ticks[0] += 1
                ins.then_inc(dve_c, 1)
                return ticks[0]

            dve.memset(vaug[:, :, :, :, :].rearrange("p a t h d -> p (a t h) d"), 0.0).then_inc(filled, 1)
            for par in range(2):
                other = slice(64 - 64 * par, P - 64 * par)
                dve.memset(qT[other, :, par, :, :].bitcast(F32), 0.0).then_inc(filled, 1)
            dve.memset(stack[:, :, :, :, :].rearrange("p a t h d -> p (a t h) d"), 0.0).then_inc(filled, 1)
            dve.wait_ge(filled, 4)
            dve.memset(vaug[:, :, :, :, HD:HD + 1].rearrange("p a t h d -> p (a t h) d"), 1.0).then_inc(filled, 1)
            dve.memset(stack[:, 1, :, :, KS:KM].rearrange("p t h d -> p (t h) d"), 1.0).then_inc(filled, 1)

            def maxima(b, k):
                n = 12 * b + k
                u, c, par, pairs = chunk(k)
                t = 0 if c < 2 else 1
                dve.wait_ge(a_ps, n + 1)
                if k == 0:
                    at_least(dve, nm_tok, b)
                dve.tensor_reduce(mx[:, t, par, pairs[0]:pairs[-1] + 1],
                                  abank[n % 2][:, :].rearrange("p (h s) -> p h s", h=len(pairs)), AX.X,
                                  ALU.max).then_inc(a_max, 1)

            def neg_max(b):
                dve.wait_ge(a_max, 12 * (b + 1))
                at_least(dve, nmT_ps, b)
                v = tick(dve.tensor_scalar(nm[:, :, :, 0, :], mx[:, :, :, :], -1.0, None, ALU.mult))
                for i in range(2):
                    dve.wait_ge(dve_c, v)
                    src = mx if i == 0 else nmr
                    v = tick(dve.scalar_tensor_tensor(
                        nmr[:, :, :, :].rearrange("p t a r -> p (t a) r"),
                        src[:, :, :, :].rearrange("p t a r -> p (t a) r"), -1.0 if i == 0 else 1.0,
                        nm[:, :, :, i, :].rearrange("p t a r -> p (t a) r"), ALU.mult, ALU.subtract))
                    dve.wait_ge(dve_c, v)
                    w = dve.tensor_copy(nm[:, :, :, i + 1, :], nmr[:, :, :, :])
                    if i == 0:
                        v = tick(w)
                    else:
                        w.then_inc(nm_tok, 1)

            def qk_rest(b, t):
                dve.wait_ge(part_a, TT * b + t + 1)
                at_least(dve, parts, TT * (b - 1) + t + 1)
                dve.tensor_tensor(rest[:, t, :].rearrange("p (a h d) -> p a h d", a=2, d=HD),
                                  misc[(QKV0 + t) % 2][:, 0:2 * P].rearrange("p (a h d) -> p a h d", a=2, d=HD),
                                  stack[:, :, t, :, 0:HD], ALU.subtract).then_inc(part_r, 1)

            def qk_parts(b, t):
                q, k = stack[:, 0, t, :, :], stack[:, 1, t, :, :]
                first = stack[:, :, t, :, 0:HD]
                dve.wait_ge(part_r, TT * b + t + 1)
                dve.tensor_copy(rest_b[:, t, :], rest[:, t, :]).then_inc(part_b, 1)
                dve.tensor_copy(q[:, :, HD:3 * HD].rearrange("p h (i d) -> p h i d", i=2),
                                     first[:, 0].unsqueeze(2).to_broadcast([P, NH, 2, HD]))
                dve.tensor_copy(k[:, :, 3 * HD:4 * HD], first[:, 1])
                dve.tensor_copy(k[:, :, 5 * HD:6 * HD], first[:, 1])
                dve.wait_ge(part_b, TT * b + t + 1)
                sec = rest_b[:, t, :].rearrange("p (a h d) -> p a h d", a=2, d=HD)
                rst = rest[:, t, :].rearrange("p (a h d) -> p a h d", a=2, d=HD)
                dve.tensor_copy(stack[:, :, t, :, 4 * HD:5 * HD], sec)
                dve.tensor_copy(q[:, :, 3 * HD:4 * HD], sec[:, 0])
                dve.tensor_copy(k[:, :, HD:2 * HD], sec[:, 1])
                dve.tensor_tensor(q[:, :, 5 * HD:6 * HD], rst[:, 0], sec[:, 0], ALU.subtract)
                dve.tensor_tensor(k[:, :, 2 * HD:3 * HD], rst[:, 1], sec[:, 1], ALU.subtract).then_inc(parts, 1)

            def fill_out(b, f):
                dve.wait_ge(fill_ps, 4 * b + f + 1)
                if b >= 2:
                    dve.wait_ge(b_ps, 12 * (b - 2) + 6 * (f // 2) + 6)
                for par in range(2):
                    rows = slice(64 * par, 64 * par + 64)
                    dve.wait_ge(k_sb, 4 * b + f + 1)
                    dve.tensor_copy(qT[rows, b % 2, par, 2 * f:2 * f + 2, :], fill_view(b, f)[rows, 0]
                                    ).then_inc(q_sb, 1)

            def residual(b, t):
                tile = TT * b + t
                o = misc[(OT0 + t) % 2][:, :].rearrange("p (g w) -> p g w", w=VW)
                dve.wait_ge(ot_ps, tile + 1)
                at_least(dve, o_div, tile)
                v = tick(dve.reciprocal(rden[:, :], o[:, :, HD]))
                dve.wait_ge(dve_c, v)
                at_least(dve, added, tile - 1)
                dve.tensor_tensor(attn[:, t, :, :, :].rearrange("p a r d -> p (a r) d"), o[:, :, 0:HD],
                                  rden[:, :].unsqueeze(2).to_broadcast([P, NH, HD]), ALU.mult
                                  ).then_inc(o_div, 1)

            def statistics(b):
                for t in range(TT):
                    dve.wait_ge(added, TT * b + t + 1)
                    v = tick(dve.bn_stats(bst[:, t, :], x[:, TT * b + t, :]))
                at_least(dve, ln_x, TT * b)
                for t in range(TT):
                    dve.wait_ge(dve_c, v)
                    v = tick(dve.bn_aggr(mv[:, t, :], bst[:, t, :]))
                dve.wait_ge(dve_c, v)
                dve.tensor_scalar(mv[:, :, 1], mv[:, :, 1], LN_EPS, None, ALU.add).then_inc(ln_mv, 1)

            def softmax_a(b):
                dve.wait_ge(lg_ps, b + 1)
                at_least(dve, lg_exp, b)
                dve.tensor_tensor(lg[:, :, :], misc[LG % 2][:, 0:TT * E0].rearrange("p (t e) -> p t e", e=E0),
                                  rb0[:, :].unsqueeze(1).to_broadcast([P, TT, E0]), ALU.add
                                  ).then_inc(lg_in, 1)
                dve.wait_ge(lg_in, b + 1)
                v = tick(dve.tensor_reduce(lgm[:, :], lg[:, :, :], AX.X, ALU.max))
                dve.wait_ge(dve_c, v)
                dve.tensor_tensor(lg[:, :, :], lg[:, :, :], lgm[:, :].unsqueeze(2).to_broadcast([P, TT, E0]),
                                  ALU.subtract).then_inc(lg_sub, 1)

            def softmax_b(b):
                dve.wait_ge(lg_exp, b + 1)
                sv = sg[:, TT * b:TT * (b + 1), :]
                v = tick(dve.tensor_reduce(lgm[:, :], sv, AX.X, ALU.add))
                dve.wait_ge(dve_c, v)
                v = tick(dve.reciprocal(lgm[:, :], lgm[:, :]))
                dve.wait_ge(dve_c, v)
                dve.tensor_tensor(sv, sv, lgm[:, :].unsqueeze(2).to_broadcast([P, TT, E0]), ALU.mult
                                  ).then_inc(s_tok, 1)

            for s in range(-1, NB + 2):
                nxt, now, prev = 0 <= s + 1 < NB, 0 <= s < NB, 0 <= s - 2 < NB
                for k in range(12):
                    if now:
                        maxima(s, k)
                    if now and k in (0, 1):
                        fill_out(s, 2 + k)
                    if prev and k in (2, 3):
                        residual(s - 2, k - 2)
                    if nxt and k in (4, 5):
                        qk_rest(s + 1, k - 4)
                    if prev and k == 5:
                        statistics(s - 2)
                    if nxt and k in (6, 7):
                        qk_parts(s + 1, k - 6)
                    if nxt and k in (10, 11):
                        fill_out(s + 1, k - 10)
                if now:
                    neg_max(s)
                if prev:
                    softmax_a(s - 2)
                    softmax_b(s - 2)

        @block.tensor
        def _(pe):
            pe.wait_ge(consts, N_CONST)
            pe.wait_ge(ld_w, N_LDW)
            for i in range(3):
                mm = pe.transpose(misc[0][:, i * P:(i + 1) * P], w_nat[:, i, :], ident[:, :])
            mm.then_inc(wT_ps, 1)
            pe.wait_ge(wT_sb, 1)

            def scores_a(b, k):
                n = 12 * b + k
                u, c, par, pairs = chunk(k)
                bank = abank[n % 2]
                if c == 0:
                    pe.wait_ge(k_sb, 4 * b + 2 * u + 2)
                    pe.wait_ge(q_sb, 8 * b + 4 * u + 4)
                at_least(pe, a_max, n - 1)
                w = P if c < 2 else T
                t = 0 if c < 2 else 1
                pe.matmul(bank[:, :].rearrange("p (h s) -> p h s", h=len(pairs))[:, :, w - P:w], ident_b[:, :],
                          causal[:, 0:len(pairs), :], start=True, stop=False, skip_group_check=True)
                for j, pair in enumerate(pairs):
                    mm = pe.matmul(bank[:, j * w:(j + 1) * w], qT[:, b % 2, par, pair, t * P:(t + 1) * P],
                                   kT[:, b % 2, pair, 0:w], start=False, stop=True, skip_group_check=True)
                mm.then_inc(a_ps, 1)

            def scores_b(b, k):
                n = 12 * b + k
                u, c, par, pairs = chunk(k)
                bank = bbank[n % 3]
                if k == 0:
                    pe.wait_ge(nm_rows, 32 * (b + 1))
                at_least(pe, b_exp, n - 2)
                w, t0, s0 = (P, P, P) if c < 2 else (T, 0, 0)
                for j, pair in enumerate(pairs):
                    mm = pe.matmul(bank[:, j * w:(j + 1) * w], kT[:, b % 2, pair, s0:s0 + P],
                                   qT[:, b % 2, par, pair, t0:T], start=True, stop=True)
                mm.then_inc(b_ps, 1)

            def values(b, u):
                pe.wait_ge(b_cut, 4 * b + 2 * u + 2)
                at_least(pe, o_sb, 2 * b + u)
                for par in range(2):
                    for j in range(4):
                        h = 8 * u + 2 * j + par
                        pe.matmul(obank[32 * j:32 * j + 32, par * T:(par + 1) * T], vaug[:, b % 3, 0, h, :],
                                  probs[:, u, 2 + 2 * (j // 2) + par, (j % 2) * T:(j % 2 + 1) * T],
                                  start=True, stop=False)
                    for j in range(4):
                        h = 8 * u + 2 * j + par
                        mm = pe.matmul(obank[32 * j:32 * j + 32, par * T + P:(par + 1) * T], vaug[:, b % 3, 1, h, :],
                                       probs[:, u, par, j * P:(j + 1) * P], start=False, stop=True)
                mm.then_inc(pv_ps, 1)

            def free_bank(s, n):
                if (s, n) in ((-1, INT), (-1, QKV0)):
                    return pe.wait_ge(wT_sb, 1)
                a, m = max((a, m) for a in (s - 1, s) for m in range(n % 2, MISC, 2) if uses(a)[m] and (a, m) < (s, n))
                ahead, read, per_sequence, nth = emptied[m]
                pe.wait_ge(read, per_sequence * (a + ahead) + nth)

            def nm_rows_T(b):
                free_bank(b + 1, NMT)
                pe.wait_ge(nm_tok, b + 1)
                for t in range(TT):
                    mm = pe.transpose(misc[NMT % 2][:, :].bitcast(BF16)[0:48, t * P:(t + 1) * P],
                                      nm[:, t, :, :, :].rearrange("p a i r -> p (a i r)"), ident_b[:, :])
                mm.then_inc(nmT_ps, 1)

            def o_T(b, t):
                free_bank(b + 2, OT0 + t)
                if t == 0:
                    pe.wait_ge(o_sb, 2 * (b + 1))
                for par in range(2):
                    for u in range(2):
                        g = par * 2 + u
                        mm = pe.transpose(misc[(OT0 + t) % 2][:, g * P:(g + 1) * P],
                                          oT[:, b % 2, u, par, t * P:(t + 1) * P], ident[:, :])
                mm.then_inc(ot_ps, 1)

            def in_tr(b):
                free_bank(b - 1, INT)
                pe.wait_ge(ld_x[b], 16)
                for t in range(TT):
                    mm = pe.transpose(misc[INT % 2][:, t * P:(t + 1) * P], x[:, TT * b + t, 0:HC], ident[:, :])
                mm.then_inc(inT_ps, 1)

            def qkv(b, t):
                free_bank(b - 1, QKV0 + t)
                pe.wait_ge(inT_sb, b + 1)
                pe.matmul(misc[(QKV0 + t) % 2][:, 0:3 * P], in_T[:, b % 2, t * P:(t + 1) * P], wT[:, :],
                          start=True, stop=True).then_inc(qkv_ps, 1)

            def fill(b, f):
                free_bank(b - 1 if f < 2 else b, fills[f])
                pe.wait_ge(parts, TT * (b + 1))
                view = misc[fills[f] % 2][:, :].bitcast(BF16).rearrange("p (a r t n) -> p a r t n", a=2, r=2, t=TT)
                for a in range(2):
                    for r in range(2):
                        for t in range(TT):
                            pair = 2 * f + r
                            mm = pe.transpose(view[:, a, r, t, :],
                                              stack[:, a, t, 2 * pair:2 * pair + 2, :].rearrange("p h d -> p (h d)"),
                                              ident_b[:, :])
                mm.then_inc(fill_ps, 1)

            def x_T(b):
                free_bank(b + 2, XT)
                pe.wait_ge(ln_x, TT * (b + 1))
                for k in range(2):
                    for t in range(TT):
                        mm = pe.transpose(misc[XT % 2][:, (k * TT + t) * P:(k * TT + t + 1) * P],
                                          x[:, TT * b + t, k * P:(k + 1) * P], ident[:, :])
                mm.then_inc(xT_ps, 1)

            def logits(b):
                free_bank(b + 2, LG)
                pe.wait_ge(xT_sb, b + 1)
                for t in range(TT):
                    for k in range(2):
                        mm = pe.matmul(misc[LG % 2][:, t * E0:(t + 1) * E0],
                                       xT[:, k, (TT * b + t) * P:(TT * b + t + 1) * P], r0w[:, k, :],
                                       start=(k == 0), stop=(k == 1))
                mm.then_inc(lg_ps, 1)

            for s in range(-1, NB + 2):
                nxt, now, cur, prev = 0 <= s + 1 < NB, 0 <= s < NB, 0 <= s - 1 < NB, 0 <= s - 2 < NB
                for k in range(12):
                    if now:
                        scores_a(s, k)
                    if cur and k >= 3:
                        scores_b(s - 1, k - 3)
                    if cur and k == 0:
                        nm_rows_T(s - 1)
                    if prev and k == 0:
                        values(s - 2, 1)
                    if now and k in (0, 1):
                        fill(s, 2 + k)
                    if prev and k in (1, 2):
                        o_T(s - 2, k - 1)
                    if nxt and k == 3:
                        in_tr(s + 1)
                    if nxt and k in (4, 5):
                        qkv(s + 1, k - 4)
                    if nxt and k in (10, 11):
                        fill(s + 1, k - 10)
                if cur:
                    scores_b(s - 1, 9)
                    values(s - 1, 0)
                if prev:
                    x_T(s - 2)
                if cur:
                    scores_b(s - 1, 10)
                    scores_b(s - 1, 11)
                if prev:
                    logits(s - 2)


def rest_of_layers(nc, m, out):
    with ExitStack() as ctx:
        x, xT, sg, ident, half_neg = m.x, m.xT, m.sg, m.ident, m.half_neg

        def sb(name, shape, dt=F32):
            return ctx.enter_context(nc.sbuf_tensor(name, shape, dt))

        def psum(name, shape, dt=F32):
            return ctx.enter_context(nc.psum_tensor(name, shape, dt))

        def sem(name):
            return ctx.enter_context(nc.semaphore(name))

        def at_least(eng, s, n):
            if n > 0:
                eng.wait_ge(s, n)

        prob = sb("prob", [P, 2, P])
        over = sb("over", [P, 2, P])
        tie = sb("tie", [P, 2, P])
        nth = sb("nth", [P, 2, P])
        cand = sb("cand", [P, 1], I32)
        flip = sb("flip", [P, 1], I32)
        cnt = sb("cnt", [P, 3])
        lim = sb("lim", [P, 2])
        tot = sb("tot", [P, 5])
        gsum = sb("gsum", [P, NT])
        y0 = sb("y0", [P, NT, C])
        w1T = sb("w1T", [P, 2, 2 * C])
        b1h = sb("b1h", [P, 2])
        gate = sb("gate", [P, 2, NB * T])
        val = sb("val", [P, 2, NB * T])
        hid = sb("hid", [P, 2, NB * T])
        bst = sb("bst2", [P, NT, 6])
        mv = sb("mv2", [P, NT, 2])
        rstd = sb("rstd2", [P, NT])
        shift = sb("shift2", [P, NT])
        sq = sb("sq", [P, C])
        ss = sb("ss", [P, NT])
        rr = sb("rr", [P, NT])
        xr = sb("xr", [P, QT, C])
        hT = sb("hT", [P, 2, NB * T])
        lg1 = sb("lg1", [P, QT, E1])
        red = sb("red", [P, QT])
        p1 = sb("p1", [P, QT, E1])
        top = sb("top", [P, QT, E1])
        w1 = sb("w1", [P, NT, E1])
        sil = sb("sil", [P, 2, QN])
        act_in = sb("act_in", [P, 2, QN])

        tr = [psum(f"tr{i}", [P, 512]) for i in range(2)]
        mm = [psum(f"mm{i}", [P, 512]) for i in range(4)]
        dn = [psum(f"dn{i}", [P, 512]) for i in range(2)]

        pr_ps, pr_sb, w1_ps, w1_sb = sem("pr_ps"), sem("pr_sb"), sem("w1_ps"), sem("w1_sb")
        cand_ok, counted, totals = sem("cand_ok"), sem("counted"), sem("totals")
        y0_ps, y0_sb = sem("y0_ps"), sem("y0_sb")
        chosen, g_ps, g_sb = sem("chosen"), sem("g_ps"), sem("g_sb")
        ln_mv = [sem(f"ln{i}_mv") for i in range(3)]
        ln_rs = sem("ln_rs2")
        ln_x = [sem(f"ln{i}_x") for i in range(3)]
        x2_ps, x2_sb = sem("x2_ps"), sem("x2_sb")
        z_ps, z_sb, g_ok, scanned, h_ps, h_add = (sem("z_ps"), sem("z_sb"), sem("g_ok"), sem("scanned"),
                                                  sem("h_ps"), sem("h_add"))
        sq_ok, ms_ok, xr_ok, xr_ps, hT_ok = sem("sq_ok"), sem("ms_ok"), sem("xr_ok"), sem("xr_ps"), sem("hT_ok")
        lg_ps, lg_rd, lg_sub, lg_exp, w_ok = sem("lg1_ps"), sem("lg1_rd"), sem("lg1_sub"), sem("lg1_exp"), sem("w_ok")
        gu_ps, sil_ok, act_ok, dn_ps, dn_add = sem("gu_ps"), sem("sil_ok"), sem("act_ok"), sem("dn_ps"), sem("dn_add")
        dve_c, act_c, pool_c = sem("dve_c2"), sem("act_c2"), sem("pool_c2")
        stored = sem("stored")
        EX = E1 + 1

        block = ctx.enter_context(nc.Block())

        @block.sync
        def _(sp):
            for q in range(Q):
                sp.wait_ge(ln_x[2], QT * (q + 1))
                for h in range(2):
                    sp.dma_start(out[2 * q + h].rearrange("(n p) c -> p n c", p=P),
                                 x[:, QT * q + TT * h:QT * q + TT * (h + 1), :]).then_inc(stored, 16)
            sp.wait_ge(stored, 16 * NB)

        @block.gpsimd
        def _(pool):
            rs = [0]

            def normalise(i, q):
                n0, n1 = QT * q, QT * (q + 1)
                pool.wait_ge(ln_mv[i], q + 1)
                pool.tensor_tensor(rstd[:, n0:n1], mv[:, n0:n1, 1], half_neg[:, 0:QT], ALU.pow).then_inc(ln_rs, 1)
                pool.wait_ge(ln_rs, rs[0] + 1)
                pool.tensor_tensor(shift[:, n0:n1], mv[:, n0:n1, 0], rstd[:, n0:n1], ALU.mult).then_inc(ln_rs, 1)
                pool.wait_ge(ln_rs, rs[0] + 2)
                rs[0] += 2
                for n in range(n0, n1):
                    pool.tensor_scalar(x[:, n, :], x[:, n, :], rstd[:, n:n + 1], shift[:, n:n + 1], ALU.mult,
                                       ALU.subtract).then_inc(ln_x[i], 1)

            def sigmoid(q):
                for k in range(2):
                    pool.wait_ge(z_sb, 4 * q + k + 1)
                    gv = gate[:, k, QN * q:QN * (q + 1)]
                    pool.tensor_scalar(gv, gv, 0.5, 0.5, ALU.mult, ALU.add).then_inc(g_ok, 1)

            def over_rms(q):
                n0, n1 = QT * q, QT * (q + 1)
                pool.wait_ge(ms_ok, q + 1)
                pool.tensor_tensor(rr[:, n0:n1], ss[:, n0:n1], half_neg[:, 0:QT], ALU.pow).then_inc(pool_c, 1)
                pool.wait_ge(pool_c, q + 1)
                at_least(pool, xr_ps, 2 * q)
                for n in range(n0, n1):
                    pool.tensor_scalar(xr[:, n - n0, :], x[:, n, :], rr[:, n:n + 1], None, ALU.mult
                                       ).then_inc(xr_ok, 1)

            for s in range(Q + 2):
                if s < Q:
                    normalise(0, s)
                    sigmoid(s)
                if 0 <= s - 1 < Q:
                    normalise(1, s - 1)
                if 0 <= s - 2 < Q:
                    over_rms(s - 2)
            for q in range(Q):
                normalise(2, q)

        @block.scalar
        def _(act):
            for k in range(2):
                act.wait_ge(w1_ps, k + 1)
                act.copy(w1T[:, k, :], mm[k][:, :]).then_inc(w1_sb, 1)
            act.mul(b1h[:, :], m.b1[:, 0:2], 0.5).then_inc(act_c, 1)
            for i in range(NT // 2):
                act.wait_ge(y0_ps, i + 1)
                act.copy(y0[:, 2 * i:2 * i + 2, :], mm[i % 4][:, :].rearrange("p (n c) -> p n c", n=2)
                         ).then_inc(y0_sb, 1)
            act.wait_ge(act_c, 1)

            def x2_out(q):
                for k in range(2):
                    act.wait_ge(x2_ps, 2 * q + k + 1)
                    act.copy(xT[:, k, QN * q:QN * (q + 1)], tr[k][:, :]).then_inc(x2_sb, 1)

            def squash(q):
                for d in range(4):
                    act.wait_ge(z_ps, 4 * q + d + 1)
                    if d < 2:
                        act.activation(gate[:, d, QN * q:QN * (q + 1)], mm[d][:, :], ACT.Tanh, bias=b1h[:, d:d + 1],
                                       scale=0.5).then_inc(z_sb, 1)
                    else:
                        act.activation(val[:, d - 2, QN * q:QN * (q + 1)], mm[d][:, :], ACT.Tanh,
                                       bias=m.b1[:, d:d + 1]).then_inc(z_sb, 1)

            def squares(q):
                for n in range(QT * q, QT * (q + 1)):
                    act.wait_ge(ln_x[1], n + 1)
                    at_least(act, sq_ok, n)
                    act.activation(sq[:, :], x[:, n, :], ACT.Square, accum_out=ss[:, n:n + 1]).then_inc(sq_ok, 1)

            def hT_out(q):
                for k in range(2):
                    act.wait_ge(xr_ps, 2 * q + k + 1)
                    act.activation(hT[:, k, QN * q:QN * (q + 1)], tr[k][:, :], ACT.Copy,
                                   scale=m.rms[:, k:k + 1]).then_inc(hT_ok, 1)

            def lg_out(q):
                act.wait_ge(lg_sub, q + 1)
                act.activation(p1[:, :, :], lg1[:, :, :], ACT.Exp).then_inc(lg_exp, 1)

            for s in range(Q + 2):
                if s < Q:
                    x2_out(s)
                    squash(s)
                if 0 <= s - 1 < Q:
                    squares(s - 1)
                if 0 <= s - 2 < Q:
                    hT_out(s - 2)
                    lg_out(s - 2)
            for i in range(Q * EX):
                act.wait_ge(gu_ps, 2 * i + 1)
                at_least(act, act_ok, i - 1)
                act.activation(sil[:, i % 2, :], mm[2 * (i % 2)][:, :], ACT.Silu).then_inc(sil_ok, 1)

        @block.vector
        def _(dve):
            ticks = [0]

            def tick(ins):
                ticks[0] += 1
                ins.then_inc(dve_c, 1)
                return ticks[0]

            dve.wait_ge(pr_ps, 1)
            dve.tensor_copy(prob[:, :, :], tr[0][:, 0:2 * P].rearrange("p (j t) -> p j t", j=2)).then_inc(pr_sb, 1)
            dve.memset(cand[:, :], 1 << (BITS - 1)).then_inc(cand_ok, 1)
            dve.wait_ge(pr_sb, 1)
            for r in range(BITS):
                bit = 1 << (BITS - 1 - r)
                dve.wait_ge(cand_ok, r + 1)
                at_least(dve, totals, r)
                dve.tensor_scalar(over[:, :, :].rearrange("p j t -> p (j t)"),
                                  prob[:, :, :].rearrange("p j t -> p (j t)"), cand[:, :].bitcast(F32), None,
                                  ALU.is_ge, ALU.add, accum_out=cnt[:, 0:1]).then_inc(counted, 1)
                dve.wait_ge(totals, r + 1)
                v = tick(dve.tensor_scalar(flip[:, :], tr[1][:, r % 2:r % 2 + 1], float(TOP), float(bit), ALU.is_lt,
                                           ALU.mult))
                dve.wait_ge(dve_c, v)
                dve.scalar_tensor_tensor(cand[:, :], flip[:, :], bit >> 1, cand[:, :], ALU.bitwise_xor,
                                         ALU.bitwise_xor).then_inc(cand_ok, 1)
            dve.wait_ge(cand_ok, BITS + 1)
            dve.tensor_scalar(over[:, :, :].rearrange("p j t -> p (j t)"),
                              prob[:, :, :].rearrange("p j t -> p (j t)"), cand[:, :].bitcast(F32), None, ALU.is_gt,
                              ALU.add, accum_out=cnt[:, 0:1])
            for j in range(2):
                w = dve.tensor_scalar(tie[:, j, :], prob[:, j, :], cand[:, :].bitcast(F32), None, ALU.is_equal,
                                      ALU.add, accum_out=cnt[:, 1 + j:2 + j])
            w.then_inc(counted, 1)
            dve.wait_ge(counted, BITS + 1)
            for j in range(2):
                v = tick(dve.tensor_tensor_scan(nth[:, j, :], m.ones[:, :], tie[:, j, :], 0.0, ALU.mult, ALU.add))
            dve.wait_ge(totals, BITS + 1)
            v = tick(dve.tensor_copy(tot[:, :], tr[1][:, 2:7]))
            dve.wait_ge(dve_c, v)
            v = tick(dve.tensor_scalar(lim[:, 0:1], tot[:, 0:1], -1.0, float(TOP), ALU.mult, ALU.add))
            dve.wait_ge(dve_c, v)
            v = tick(dve.tensor_tensor(lim[:, 1:2], lim[:, 0:1], tot[:, 1:2], ALU.subtract))
            dve.wait_ge(dve_c, v)
            v = tick(dve.tensor_tensor(lim[:, :], lim[:, :], tot[:, 3:5], ALU.subtract))
            dve.wait_ge(dve_c, v)
            for j in range(2):
                v = tick(dve.scalar_tensor_tensor(tie[:, j, :], nth[:, j, :], lim[:, j:j + 1], tie[:, j, :],
                                                  ALU.is_le, ALU.mult))
            dve.wait_ge(dve_c, v)
            v = tick(dve.tensor_tensor(over[:, :, :], over[:, :, :], tie[:, :, :], ALU.add))
            dve.wait_ge(dve_c, v)
            dve.tensor_tensor(over[:, :, :], over[:, :, :], prob[:, :, :], ALU.mult).then_inc(chosen, 1)
            dve.wait_ge(g_ps, 1)
            dve.tensor_reduce(gsum[:, :].rearrange("p (j c) -> p j c", j=2),
                              tr[0][:, 0:2 * P].rearrange("p (j c e) -> p j c e", j=2, e=E0), AX.X, ALU.add
                              ).then_inc(g_sb, 1)
            dve.wait_ge(g_sb, 1)

            def statistics(i, q):
                n0, n1 = QT * q, QT * (q + 1)
                v = 0
                for n in range(n0, n1):
                    v = tick(dve.bn_stats(bst[:, n, :], x[:, n, :]))
                for n in range(n0, n1):
                    dve.wait_ge(dve_c, v - (n1 - 1 - n) if n == n0 else v)
                    w = tick(dve.bn_aggr(mv[:, n, :], bst[:, n, :]))
                dve.wait_ge(dve_c, w)
                dve.tensor_scalar(mv[:, n0:n1, 1], mv[:, n0:n1, 1], LN_EPS, None, ALU.add).then_inc(ln_mv[i], 1)

            def add_experts(q):
                dve.wait_ge(y0_sb, QT // 2 * (q + 1))
                for n in range(QT * q, QT * (q + 1)):
                    v = tick(dve.scalar_tensor_tensor(x[:, n, :], y0[:, n, :], gsum[:, n:n + 1], x[:, n, :],
                                                      ALU.mult, ALU.add))
                dve.wait_ge(dve_c, v)
                statistics(0, q)

            def recur(q):
                dve.wait_ge(g_ok, 2 * (q + 1))
                dve.wait_ge(z_sb, 4 * (q + 1))
                for k in range(2):
                    for h in range(2):
                        at = slice(QN * q + T * h, QN * q + T * (h + 1))
                        w = dve.tensor_tensor_scan(hid[:, k, at], gate[:, k, at], val[:, k, at], 0.0, ALU.mult,
                                                   ALU.add)
                    w.then_inc(scanned, 1)

            def add_hidden(q):
                for i in range(2):
                    dve.wait_ge(h_ps, 2 * q + i + 1)
                    xv = x[:, QT * q + 2 * i:QT * q + 2 * i + 2, :]
                    dve.tensor_tensor(xv, xv, tr[i][:, :].rearrange("p (n c) -> p n c", n=2), ALU.add
                                      ).then_inc(h_add, 1)
                dve.wait_ge(h_add, 2 * (q + 1))
                statistics(1, q)

            def mean_square(q):
                n0, n1 = QT * q, QT * (q + 1)
                dve.wait_ge(sq_ok, n1)
                dve.tensor_scalar(ss[:, n0:n1], ss[:, n0:n1], 1.0 / C, RMS_EPS, ALU.mult, ALU.add).then_inc(ms_ok, 1)

            def route(q):
                wide = [P, QT, E1]
                dve.wait_ge(lg_ps, q + 1)
                at_least(dve, w_ok, q)
                z = mm[0][:, 0:QT * E1].rearrange("p (n e) -> p n e", e=E1)
                v = tick(dve.tensor_reduce(red[:, :], z, AX.X, ALU.max))
                dve.wait_ge(dve_c, v)
                dve.tensor_tensor(lg1[:, :, :], z, red[:, :].unsqueeze(2).to_broadcast(wide), ALU.subtract
                                  ).then_inc(lg_sub, 1)
                dve.wait_ge(lg_exp, q + 1)
                v = tick(dve.tensor_reduce(red[:, :], p1[:, :, :], AX.X, ALU.add))
                dve.wait_ge(dve_c, v)
                v = tick(dve.reciprocal(red[:, :], red[:, :]))
                dve.wait_ge(dve_c, v)
                v = tick(dve.tensor_tensor(p1[:, :, :], p1[:, :, :], red[:, :].unsqueeze(2).to_broadcast(wide),
                                           ALU.mult))
                dve.wait_ge(dve_c, v)
                for n in range(QT):
                    v = tick(dve.max(top[:, n, :], p1[:, n, :]))
                dve.wait_ge(dve_c, v)
                v = tick(dve.tensor_tensor(red[:, :], top[:, :, 0], top[:, :, 1], ALU.add))
                v = tick(dve.memset(top[:, :, TOP1:], -1.0))
                dve.wait_ge(dve_c, v)
                v = tick(dve.reciprocal(red[:, :], red[:, :]))
                wv = w1[:, QT * q:QT * (q + 1), :]
                for n in range(QT):
                    v = tick(dve.match_replace(out=w1[:, QT * q + n, :], in_to_replace=top[:, n, :],
                                               in_values=p1[:, n, :], imm_value=0.0))
                dve.wait_ge(dve_c, v)
                v = tick(dve.tensor_tensor(wv, p1[:, :, :], wv, ALU.subtract))
                dve.wait_ge(dve_c, v)
                dve.tensor_tensor(wv, wv, red[:, :].unsqueeze(2).to_broadcast(wide), ALU.mult).then_inc(w_ok, 1)

            for s in range(Q + 2):
                if s < Q:
                    add_experts(s)
                    recur(s)
                if 0 <= s - 1 < Q:
                    add_hidden(s - 1)
                    mean_square(s - 1)
                if 0 <= s - 2 < Q:
                    route(s - 2)

            def gated(i):
                dve.wait_ge(sil_ok, i + 1)
                dve.wait_ge(gu_ps, 2 * (i + 1))
                at_least(dve, dn_ps, 2 * (i - 1))
                dve.tensor_tensor(act_in[:, i % 2, :], sil[:, i % 2, :], mm[2 * (i % 2) + 1][:, :], ALU.mult
                                  ).then_inc(act_ok, 1)

            def add_down(q, e):
                i = EX * q + e
                for t in range(QT):
                    n = QT * q + t
                    if t % 2 == 0:
                        dve.wait_ge(dn_ps, 2 * i + t // 2 + 1)
                    if e > 0:
                        dve.wait_ge(dn_add, QT * (i - 1) + t + 1)
                    d = dn[t // 2][:, (t % 2) * C:(t % 2 + 1) * C]
                    if e == 0:
                        w = dve.tensor_tensor(x[:, n, :], x[:, n, :], d, ALU.add)
                    else:
                        w = dve.scalar_tensor_tensor(x[:, n, :], d, w1[:, n, e - 1:e], x[:, n, :], ALU.mult, ALU.add)
                    w.then_inc(dn_add, 1)

            dve.wait_ge(w_ok, Q)
            for i in range(Q * EX + 1):
                if i < Q * EX:
                    gated(i)
                if i > 0:
                    q, e = divmod(i - 1, EX)
                    add_down(q, e)
                    if e == EX - 1:
                        dve.wait_ge(dn_add, QT * i)
                        statistics(2, q)

        @block.tensor
        def _(pe):
            for j in range(2):
                w = pe.transpose(tr[0][:, j * P:(j + 1) * P],
                                 sg[:, NB * j:NB * (j + 1), :].rearrange("p c e -> p (c e)"), ident[:, :])
            w.then_inc(pr_ps, 1)
            for k in range(2):
                for d in range(4):
                    w = pe.transpose(mm[k][:, d * P:(d + 1) * P], m.w1_nat[:, d, k * P:(k + 1) * P], ident[:, :])
                w.then_inc(w1_ps, 1)

            def y0_piece(k):
                n, part = divmod(k, 3)
                i = n // 2
                dst = mm[i % 4][:, (n % 2) * C:(n % 2 + 1) * C]
                if n % 2 == 0 and part == 0:
                    pe.wait_ge(w1_sb, 2)
                    at_least(pe, y0_sb, i - 3)
                if part == 0:
                    pe.matmul(dst, m.ones[0:1, :], m.e0b[:, :], start=True, stop=False)
                else:
                    w = pe.matmul(dst, xT[:, part - 1, n * P:(n + 1) * P], m.e0w[:, part - 1, :], start=False,
                                  stop=(part == 2))
                    if part == 2 and n % 2 == 1:
                        w.then_inc(y0_ps, 1)

            same = m.same[:, :, :].rearrange("p c e -> p (c e)")
            before = m.before[:, :, :].rearrange("p c e -> p (c e)")
            for r in range(BITS):
                pe.wait_ge(counted, r + 1)
                at_least(pe, cand_ok, r)
                pe.matmul(tr[1][:, r % 2:r % 2 + 1], same, cnt[:, 0:1], start=True, stop=True).then_inc(totals, 1)
                for k in range(2 * r, 2 * r + 2):
                    if k < 3 * NT:
                        y0_piece(k)
            pe.wait_ge(counted, BITS + 1)
            pe.matmul(tr[1][:, 2:5], same, cnt[:, :], start=True, stop=True)
            pe.matmul(tr[1][:, 5:7], before, cnt[:, 1:3], start=True, stop=True).then_inc(totals, 1)
            pe.wait_ge(chosen, 1)
            for j in range(2):
                w = pe.transpose(tr[0][:, j * P:(j + 1) * P], over[:, j, :], ident[:, :])
            w.then_inc(g_ps, 1)

            def x2_T(q):
                pe.wait_ge(ln_x[0], QT * (q + 1))
                if q == 0:
                    pe.wait_ge(g_sb, 1)
                for k in range(2):
                    if q == 1:
                        pe.wait_ge(x2_sb, k + 1)
                    if q >= 2:
                        at_least(pe, h_add, 2 * (q - 2) + k + 1)
                    if q >= 3:
                        at_least(pe, hT_ok, 2 * (q - 3) + k + 1)
                    for t in range(QT):
                        w = pe.transpose(tr[k][:, t * P:(t + 1) * P], x[:, QT * q + t, k * P:(k + 1) * P],
                                         ident[:, :])
                    w.then_inc(x2_ps, 1)

            def linear(q):
                for d in range(4):
                    for k in range(2):
                        if d == 0:
                            pe.wait_ge(x2_sb, 2 * q + k + 1)
                        if k == 0:
                            at_least(pe, z_sb, 4 * (q - 1) + d + 1)
                            if q == 0:
                                pe.wait_ge(y0_sb, NT // 2)
                            if q >= 3 and d == 0:
                                pe.wait_ge(lg_sub, q - 2)
                        w = pe.matmul(mm[d][:, :], w1T[:, k, d * P:(d + 1) * P], xT[:, k, QN * q:QN * (q + 1)],
                                      start=(k == 0), stop=(k == 1))
                    w.then_inc(z_ps, 1)

            def hidden_T(q):
                pe.wait_ge(scanned, 2 * (q + 1))
                pe.wait_ge(x2_sb, 2 * min(q + 2, Q))
                for i in range(2):
                    if q >= 2:
                        pe.wait_ge(hT_ok, 2 * (q - 2) + i + 1)
                    for t in range(2):
                        for k in range(2):
                            n = QT * q + 2 * i + t
                            w = pe.transpose(tr[i][:, (2 * t + k) * P:(2 * t + k + 1) * P],
                                             hid[:, k, n * P:(n + 1) * P], ident[:, :])
                    w.then_inc(h_ps, 1)

            def h_T(q):
                pe.wait_ge(xr_ok, QT * (q + 1))
                pe.wait_ge(h_add, 2 * min(q + 2, Q))
                for k in range(2):
                    for t in range(QT):
                        w = pe.transpose(tr[k][:, t * P:(t + 1) * P], xr[:, t, k * P:(k + 1) * P], ident[:, :])
                    w.then_inc(xr_ps, 1)

            def logits(q):
                pe.wait_ge(hT_ok, 2 * (q + 1))
                pe.wait_ge(z_sb, 4 * min(q + 3, Q))
                at_least(pe, lg_sub, q)
                for t in range(QT):
                    for k in range(2):
                        n = QT * q + t
                        w = pe.matmul(mm[0][:, t * E1:(t + 1) * E1], hT[:, k, n * P:(n + 1) * P], m.r1w[:, k, :],
                                      start=(k == 0), stop=(k == 1))
                w.then_inc(lg_ps, 1)

            for s in range(Q + 2):
                if s < Q:
                    x2_T(s)
                    linear(s)
                if 0 <= s - 1 < Q:
                    hidden_T(s - 1)
                if 0 <= s - 2 < Q:
                    h_T(s - 2)
                    logits(s - 2)

            def gate_up(q, e):
                i = EX * q + e
                if i == 0:
                    pe.wait_ge(lg_sub, Q)
                at_least(pe, sil_ok, i - 1)
                at_least(pe, act_ok, i - 1)
                for j, weights in enumerate((m.wg, m.wu)):
                    for k in range(2):
                        w = pe.matmul(mm[2 * (i % 2) + j][:, :], weights[:, e, k, :], hT[:, k, QN * q:QN * (q + 1)],
                                      start=(k == 0), stop=(k == 1))
                    w.then_inc(gu_ps, 1)

            def down(q, e):
                i = EX * q + e
                pe.wait_ge(act_ok, i + 1)
                for t in range(QT):
                    if t % 2 == 0:
                        at_least(pe, dn_add, QT * (i - 1) + t + 2)
                    w = pe.matmul(dn[t // 2][:, (t % 2) * C:(t % 2 + 1) * C], act_in[:, i % 2, t * P:(t + 1) * P],
                                  m.wd[:, e, :], start=True, stop=True)
                    if t % 2 == 1:
                        w.then_inc(dn_ps, 1)

            for i in range(Q * EX + 1):
                if i < Q * EX:
                    gate_up(*divmod(i, EX))
                if i > 0:
                    down(*divmod(i - 1, EX))


INPUTS = ["L0_attn_x", "L0_attn_Wq", "L0_attn_Wk", "L0_attn_Wv", "L0_ffn_router_w", "L0_ffn_router_b",
          "L0_ffn_expert_w", "L0_ffn_expert_b", "L1_attn_W", "L1_attn_b", "L1_ffn_rms_weight", "L1_ffn_router_w",
          "L1_ffn_w_gate", "L1_ffn_w_up", "L1_ffn_w_down", "L1_ffn_sw_gate", "L1_ffn_sw_up", "L1_ffn_sw_down"]


def kernel(**inputs):
    import numpy as np
    import concourse.bacc as bacc
    from concourse.bass_utils import run_bass_kernel_spmd

    nc = bacc.Bacc("TRN2", target_bir_lowering=False, num_devices=1)
    arrays, args = {}, []
    for name in INPUTS:
        a = np.ascontiguousarray(inputs[name])
        arrays[f"in_{name}"] = a
        args.append(nc.dram_tensor(f"in_{name}", a.shape, mybir.dt.from_np(a.dtype), kind="ExternalInput").ap())
    out = nc.dram_tensor("out", (NB, T, C), F32, kind="ExternalOutput").ap()
    program(nc, *args, out)
    return run_bass_kernel_spmd(nc, [arrays], core_ids=[0]).results[0]["out"]
```

```python
from contextlib import ExitStack

import concourse.bass as bass
from concourse import mybir

F32 = mybir.dt.float32
BF16 = mybir.dt.bfloat16
I32 = mybir.dt.int32
ACT = mybir.ActivationFunctionType
ALU = mybir.AluOpType
AX = mybir.AxisListType

P = 128
NB, T, C = 8, 256, 256
TT = T // P
NT = NB * TT
HC = 128
NH, HD = 16, 8
PAIRS = NH // 2
SLOTS = 6
KS = SLOTS * HD
KM = KS + 3
VW = 32
NEG = -1.0e30
SCALE = float(HD) ** -0.5
LN_EPS = 1e-5
E0 = 16
TOP = NB * T // E0
BITS = 30
E1, TOP1 = 8, 2
FF = 128
RMS_EPS = 1e-6
Q = 4
QT = NT // Q
QN = QT * P
ON_DVE = QT // 2
BEGIN = (0, 1, 2, 16)
FIRST_EXPERT = 12
MISC = 12


def program(nc, x_in, Wq, Wk, Wv, r0_w, r0_b, e0_w, e0_b, W1, b1, rms_w, r1_w, w_gate, w_up, w_down,
            sw_gate, sw_up, sw_down, out):
    with ExitStack() as whole:
        def keep(name, shape, dt=F32):
            return whole.enter_context(nc.sbuf_tensor(name, shape, dt))

        m = Kept()
        m.x = keep("x", [P, NT, C])
        m.xT = keep("xT", [P, 2, NB * T])
        m.sg = keep("sg", [P, NT, E0])
        m.ident = keep("ident", [P, P])
        m.half_neg = keep("half_neg", [P, NT])
        m.same = keep("same", [P, NB, E0])
        m.before = keep("before", [P, NB, E0])
        m.ones = keep("ones", [P, P])
        m.e0w = keep("e0w", [P, 2, C])
        m.e0b = keep("e0b", [P, C])
        m.w1_nat = keep("w1_nat", [P, 4, C])
        m.b1 = keep("b1s", [P, 4])
        m.rms = keep("rms", [P, 2])
        m.r1w = keep("r1w", [P, 2, E1])
        m.wg = keep("wg", [P, E1 + 1, 2, FF])
        m.wu = keep("wu", [P, E1 + 1, 2, FF])
        m.wd = keep("wd", [FF, E1 + 1, C])
        attention(nc, m, x_in, Wq, Wk, Wv, r0_w, r0_b, e0_w, e0_b, W1, b1, rms_w, r1_w, w_gate, w_up, w_down,
                  sw_gate, sw_up, sw_down)
        rest_of_layers(nc, m, out)


class Kept:
    pass


def attention(nc, m, x_in, Wq, Wk, Wv, r0_w, r0_b, e0_w, e0_b, W1, b1, rms_w, r1_w, w_gate, w_up, w_down,
              sw_gate, sw_up, sw_down):
    with ExitStack() as ctx:
        x, xT, sg, ident, half_neg = m.x, m.xT, m.sg, m.ident, m.half_neg

        def sb(name, shape, dt=F32):
            return ctx.enter_context(nc.sbuf_tensor(name, shape, dt))

        def psum(name, shape, dt=F32):
            return ctx.enter_context(nc.psum_tensor(name, shape, dt))

        def sem(name):
            return ctx.enter_context(nc.semaphore(name))

        def at_least(eng, s, n):
            if n > 0:
                eng.wait_ge(s, n)

        w_nat = sb("w_nat", [P, 3, P])
        wT = sb("wT", [P, 3 * P])
        ident_b = sb("ident_b", [P, P], BF16)
        causal = sb("causal", [P, 4, P], BF16)
        in_T = sb("in_T", [P, 2, T])
        stack = sb("stack", [P, 2, TT, NH, 64], BF16)
        rest = sb("rest", [P, TT, 2 * P])
        rest_b = sb("rest_b", [P, TT, 2 * P], BF16)
        kT = sb("kT", [P, 2, PAIRS, T], BF16)
        qT = sb("qT", [P, 2, 2, PAIRS, T], BF16)
        vaug = sb("vaug", [P, 3, TT, NH, VW])
        mx = sb("mx", [P, TT, 2, PAIRS])
        nmr = sb("nmr", [P, TT, 2, PAIRS])
        nm = sb("nm", [P, TT, 2, 3, PAIRS], BF16)
        nmT = sb("nmT", [2 * 3 * PAIRS, T], BF16)
        probs = sb("probs", [P, 2, 6, 512])
        oT = sb("oT", [P, 2, 2, 2, T])
        rden = sb("rden", [P, NH])
        attn = sb("attn", [P, TT, 2, PAIRS, HD])
        bst = sb("bst", [P, TT, 6])
        mv = sb("mv", [P, TT, 2])
        rstd = sb("rstd", [P, TT])
        shift = sb("shift", [P, TT])
        rb0 = sb("rb0", [P, E0])
        r0w = sb("r0w", [P, 2, E0])
        lg = sb("lg", [P, TT, E0])
        lgm = sb("lgm", [P, TT])

        misc = [psum(f"misc{i}", [P, 512]) for i in range(2)]
        abank = [psum(f"abank{i}", [P, 512]) for i in range(2)]
        bbank = [psum(f"bbank{i}", [P, 512]) for i in range(3)]
        obank = psum("obank", [P, 512])

        ld_w = sem("ld_w")
        ld_x = [sem(f"ld_x{b}") for b in range(NB)]
        consts = sem("consts")
        wT_ps, wT_sb = sem("wT_ps"), sem("wT_sb")
        inT_ps, inT_sb = sem("inT_ps"), sem("inT_sb")
        qkv_ps, part_a, part_r, part_b, parts = sem("qkv_ps"), sem("part_a"), sem("part_r"), sem("part_b"), sem("parts")
        fill_ps, k_sb, q_sb = sem("fill_ps"), sem("k_sb"), sem("q_sb")
        a_ps, a_max = sem("a_ps"), sem("a_max")
        nm_tok, nmT_ps, nmT_sb, nm_rows = sem("nm_tok"), sem("nmT_ps"), sem("nmT_sb"), sem("nm_rows")
        b_ps, b_exp, b_cut, pv_ps, o_sb = sem("b_ps"), sem("b_exp"), sem("b_cut"), sem("pv_ps"), sem("o_sb")
        ot_ps = sem("ot_ps")
        ln_mv, ln_rs, ln_x = sem("ln_mv"), sem("ln_rs"), sem("ln_x")
        xT_ps, xT_sb = sem("xT_ps"), sem("xT_sb")
        lg_ps, lg_in, lg_sub, lg_exp, s_tok = sem("lg_ps"), sem("lg_in"), sem("lg_sub"), sem("lg_exp"), sem("s_tok")
        o_div, added, filled = sem("o_div"), sem("added"), sem("filled")
        dve_c, act_c, pool_c = sem("dve_c"), sem("act_c"), sem("pool_c")
        ld_later, masks = sem("ld_later"), sem("masks")

        def uses(s):
            nxt, now, cur, prev = 0 <= s + 1 < NB, 0 <= s < NB, 0 <= s - 1 < NB, 0 <= s - 2 < NB
            return [cur, now, now, prev, prev, nxt, nxt, nxt, nxt, nxt, prev, prev]

        NMT, FILL2, FILL3, OT0, OT1, INT, QKV0, QKV1, FILL0, FILL1, XT, LG = range(MISC)
        fills = [FILL0, FILL1, FILL2, FILL3]
        emptied = {NMT: (-1, nmT_sb, 1, 1), OT0: (-2, o_div, 2, 1), OT1: (-2, o_div, 2, 2), INT: (1, inT_sb, 1, 1),
                   QKV0: (1, part_r, 2, 1), QKV1: (1, part_r, 2, 2), XT: (-2, xT_sb, 1, 1),
                   LG: (-2, lg_in, 1, 1), FILL0: (1, q_sb, 8, 2), FILL1: (1, q_sb, 8, 4),
                   FILL2: (0, q_sb, 8, 6), FILL3: (0, q_sb, 8, 8)}

        def chunk(k):
            u, c = divmod(k, 6)
            js = range(4) if c < 2 else (range(0, 2) if c < 4 else range(2, 4))
            return u, c, c % 2, [4 * u + j for j in js]

        def fill_view(b, f):
            return misc[fills[f] % 2][:, :].bitcast(BF16).rearrange("p (a r t) -> p a r t", a=2, r=2)

        block = ctx.enter_context(nc.Block())

        @block.sync
        def _(sp):
            sp.dma_start(x[:, 0:TT, :], x_in[0].rearrange("(n p) c -> p n c", p=P)).then_inc(ld_x[0], 16)
            for i, w in enumerate((Wq, Wk, Wv)):
                sp.dma_start(w_nat[:, i, :], w[:, 0:HD, 0:HC]).then_inc(ld_w, 16)
            sp.dma_start(r0w[:, :, :], r0_w.rearrange("(k p) e -> p k e", p=P)).then_inc(ld_w, 16)
            sp.dma_start(rb0[:, :], r0_b.partition_broadcast(P)).then_inc(ld_w, 16)
            for b in range(1, NB):
                sp.dma_start(x[:, TT * b:TT * (b + 1), :],
                             x_in[b].rearrange("(n p) c -> p n c", p=P)).then_inc(ld_x[b], 16)
            later = [(m.e0w[:, :, :], e0_w.rearrange("(k p) c -> p k c", p=P)), (m.e0b[:, :], e0_b.partition_broadcast(P)),
                     (m.w1_nat[:, :, :], W1.rearrange("(n p) c -> p n c", p=P)),
                     (m.b1[:, :], b1.rearrange("(n p) -> p n", p=P)),
                     (m.rms[:, :], rms_w.rearrange("(k p) -> p k", p=P)),
                     (m.r1w[:, :, :], r1_w.rearrange("(k p) e -> p k e", p=P)),
                     (m.wg[:, 0, :, :], sw_gate.rearrange("(k p) f -> p k f", p=P)),
                     (m.wu[:, 0, :, :], sw_up.rearrange("(k p) f -> p k f", p=P)), (m.wd[:, 0, :], sw_down),
                     (m.wg[:, 1:, :, :], w_gate.rearrange("e (k p) f -> p e k f", p=P)),
                     (m.wu[:, 1:, :, :], w_up.rearrange("e (k p) f -> p e k f", p=P)),
                     (m.wd[:, 1:, :], w_down.rearrange("e f c -> f e c"))]
            for dst, src in later:
                sp.dma_start(dst, src, allow_slow_non_contiguous=True).then_inc(ld_later, 16)
            for b in range(NB):
                sp.wait_ge(nmT_sb, b + 1)
                for par in range(2):
                    sp.dma_start(qT[64 * par + KS:64 * par + KM, b % 2, par, :, :],
                                 nmT[24 * par:24 * par + 24, :]
                                 ).then_inc(nm_rows, 16)
            sp.wait_ge(ld_later, 16 * len(later))

        N_LDW = 16 * (3 + 2)

        @block.gpsimd
        def _(pool):
            pool.memset(ident[:, :], 0.0).then_inc(pool_c, 1)
            pool.memset(ident_b[:, :], 0.0).then_inc(pool_c, 1)
            pool.memset(causal[:, :, :], 0.0).then_inc(pool_c, 1)
            pool.memset(half_neg[:, :], -0.5).then_inc(pool_c, 1)
            pool.wait_ge(pool_c, 4)
            for one in (ident, ident_b):
                pool.affine_select(out=one[:, :], in_=one[:, :], compare_op=ALU.not_equal, fill=1.0, base=0,
                                   pattern=[[-1, P]], channel_multiplier=1).then_inc(consts, 1)
            pool.affine_select(out=causal[:, :, :], in_=causal[:, :, :], compare_op=ALU.is_ge, fill=NEG, base=0,
                               pattern=[[0, 4], [-1, P]], channel_multiplier=1).then_inc(consts, 1)

            pool.memset(m.ones[:, :], 1.0).then_inc(pool_c, 1)
            pool.memset(m.same[:, 0, :], 0.0).then_inc(masks, 1)
            for c in range(NB):
                pool.wait_ge(masks, c + 1)
                pool.affine_select(out=m.same[:, 0, :], in_=m.same[:, 0, :], compare_op=ALU.not_equal, fill=1.0,
                                   base=-E0 * c, pattern=[[-1, E0]], channel_multiplier=1).then_inc(masks, 1)
            pool.wait_ge(masks, NB + 1)
            pool.tensor_copy(m.same[:, 1:, :], m.same[:, 0:1, :].to_broadcast([P, NB - 1, E0])).then_inc(masks, 1)
            pool.wait_ge(masks, NB + 2)
            pool.affine_select(out=m.before[:, :, :], in_=m.same[:, :, :], compare_op=ALU.is_gt, fill=0.0, base=0,
                               pattern=[[E0, NB], [0, E0]], channel_multiplier=-1).then_inc(masks, 1)

            def cut(b, u, lo, hi):
                pool.wait_ge(b_exp, 12 * b + 6 * u + hi)
                w = P if lo == 0 else T
                part = probs[:, u, lo:hi, :].rearrange("p c (h t) -> p (c h) t", t=w)[:, :, 0:P]
                pool.affine_select(out=part, in_=part, compare_op=ALU.is_ge, fill=0.0, base=0,
                                   pattern=[[0, 8], [1, P]], channel_multiplier=-1).then_inc(b_cut, 1)

            def add_attn(b):
                for t in range(TT):
                    pool.wait_ge(o_div, TT * b + t + 1)
                    xv = x[:, TT * b + t, 0:HC].rearrange("p (r a d) -> p a r d", a=2, d=HD)
                    pool.tensor_tensor(xv, xv, attn[:, t, :, :, :], ALU.add).then_inc(added, 1)

            def scales(b):
                pool.wait_ge(ln_mv, b + 1)
                at_least(pool, ln_x, TT * b)
                pool.tensor_tensor(rstd[:, :], mv[:, :, 1], half_neg[:, 0:TT], ALU.pow).then_inc(ln_rs, 1)
                pool.wait_ge(ln_rs, 2 * b + 1)
                pool.tensor_tensor(shift[:, :], mv[:, :, 0], rstd[:, :], ALU.mult).then_inc(ln_rs, 1)

            for s in range(-1, NB + 2):
                nxt, cur, prev = 0 <= s + 1 < NB, 0 <= s - 1 < NB, 0 <= s - 2 < NB
                if prev:
                    add_attn(s - 2)
                if cur:
                    cut(s - 1, 0, 0, 2)
                if prev:
                    scales(s - 2)
                if cur:
                    cut(s - 1, 0, 2, 6)
                    cut(s - 1, 1, 0, 2)
                    cut(s - 1, 1, 2, 6)
        N_CONST = 3

        @block.scalar
        def _(act):
            act.wait_ge(wT_ps, 1)
            act.copy(wT[:, :], misc[0][:, 0:3 * P]).then_inc(wT_sb, 1)

            def nmT_out(b):
                act.wait_ge(nmT_ps, b + 1)
                at_least(act, nm_rows, 32 * b)
                act.copy(nmT[:, :], misc[NMT % 2][:, :].bitcast(BF16)[0:48, 0:T]).then_inc(nmT_sb, 1)

            def inT_out(b):
                act.wait_ge(inT_ps, b + 1)
                act.copy(in_T[:, b % 2, :], misc[INT % 2][:, 0:T]).then_inc(inT_sb, 1)

            def qkv_out(b, t):
                act.wait_ge(qkv_ps, TT * b + t + 1)
                bank = misc[(QKV0 + t) % 2]
                if b == 0 and t == 0:
                    act.wait_ge(filled, 6)
                if b >= 3 and t == 0:
                    act.wait_ge(pv_ps, 2 * (b - 2))
                act.copy(vaug[:, b % 3, t, :, 0:HD],
                         bank[:, 2 * P:3 * P].rearrange("p (h d) -> p h d", d=HD)).then_inc(act_c, 1)
                if b >= 1 and t == 0:
                    act.wait_ge(fill_ps, 4 * b)
                act.copy(stack[:, :, t, :, 0:HD],
                         bank[:, 0:2 * P].rearrange("p (a h d) -> p a h d", a=2, d=HD)).then_inc(part_a, 1)

            def exps(b, k):
                n = 12 * b + k
                u = k // 6
                act.wait_ge(b_ps, n + 1)
                if k % 6 == 0:
                    at_least(act, pv_ps, 2 * b + u - 1)
                act.activation(probs[:, u, k % 6, :], bbank[n % 3][:, :], ACT.Exp, scale=SCALE).then_inc(b_exp, 1)

            def o_out(b, u):
                act.wait_ge(pv_ps, 2 * b + u + 1)
                if u == 0:
                    at_least(act, ot_ps, TT * (b - 1))
                act.copy(oT[:, b % 2, u, :, :], obank[:, :].rearrange("p (a t) -> p a t", a=2)).then_inc(o_sb, 1)

            def xT_out(b):
                act.wait_ge(xT_ps, b + 1)
                act.copy(xT[:, :, b * T:(b + 1) * T],
                         misc[XT % 2][:, :].rearrange("p (k t) -> p k t", k=2)).then_inc(xT_sb, 1)

            def fill_out(b, f):
                act.wait_ge(fill_ps, 4 * b + f + 1)
                if b >= 2:
                    act.wait_ge(b_ps, 12 * (b - 2) + 6 * (f // 2) + 6)
                act.copy(kT[:, b % 2, 2 * f:2 * f + 2, :], fill_view(b, f)[:, 1]).then_inc(k_sb, 1)

            def normalise(b):
                act.wait_ge(ln_rs, 2 * b + 2)
                for t in range(TT):
                    xv = x[:, TT * b + t, :]
                    act.activation(xv, xv, ACT.Identity, bias=shift[:, t:t + 1], scale=rstd[:, t:t + 1]
                                   ).then_inc(ln_x, 1)

            def lg_out(b):
                act.wait_ge(lg_sub, b + 1)
                act.activation(sg[:, TT * b:TT * (b + 1), :], lg[:, :, :], ACT.Exp).then_inc(lg_exp, 1)

            for s in range(-1, NB + 2):
                nxt, now, cur, prev = 0 <= s + 1 < NB, 0 <= s < NB, 0 <= s - 1 < NB, 0 <= s - 2 < NB
                if cur:
                    nmT_out(s - 1)
                if now:
                    fill_out(s, 2)
                if prev:
                    o_out(s - 2, 1)
                if now:
                    fill_out(s, 3)
                for k in range(3, 12):
                    if cur:
                        exps(s - 1, k - 3)
                    if nxt and k == 3:
                        inT_out(s + 1)
                    if nxt and k in (4, 5):
                        qkv_out(s + 1, k - 4)
                    if prev and k == 8:
                        normalise(s - 2)
                    if nxt and k in (10, 11):
                        fill_out(s + 1, k - 10)
                if cur:
                    exps(s - 1, 9)
                    o_out(s - 1, 0)
                if prev:
                    xT_out(s - 2)
                if cur:
                    exps(s - 1, 10)
                    exps(s - 1, 11)
                if prev:
                    lg_out(s - 2)

        @block.vector
        def _(dve):
            ticks = [0]

            def tick(ins):
                ticks[0] += 1
                ins.then_inc(dve_c, 1)
                return ticks[0]

            dve.memset(vaug[:, :, :, :, :].rearrange("p a t h d -> p (a t h) d"), 0.0).then_inc(filled, 1)
            for par in range(2):
                other = slice(64 - 64 * par, P - 64 * par)
                dve.memset(qT[other, :, par, :, :].bitcast(F32), 0.0).then_inc(filled, 1)
            dve.memset(stack[:, :, :, :, :].rearrange("p a t h d -> p (a t h) d"), 0.0).then_inc(filled, 1)
            dve.wait_ge(filled, 4)
            dve.memset(vaug[:, :, :, :, HD:HD + 1].rearrange("p a t h d -> p (a t h) d"), 1.0).then_inc(filled, 1)
            dve.memset(stack[:, 1, :, :, KS:KM].rearrange("p t h d -> p (t h) d"), 1.0).then_inc(filled, 1)

            def maxima(b, k):
                n = 12 * b + k
                u, c, par, pairs = chunk(k)
                t = 0 if c < 2 else 1
                dve.wait_ge(a_ps, n + 1)
                if k == 0:
                    at_least(dve, nm_tok, b)
                dve.tensor_reduce(mx[:, t, par, pairs[0]:pairs[-1] + 1],
                                  abank[n % 2][:, :].rearrange("p (h s) -> p h s", h=len(pairs)), AX.X,
                                  ALU.max).then_inc(a_max, 1)

            def neg_max(b):
                dve.wait_ge(a_max, 12 * (b + 1))
                at_least(dve, nmT_ps, b)
                v = tick(dve.tensor_scalar(nm[:, :, :, 0, :], mx[:, :, :, :], -1.0, None, ALU.mult))
                for i in range(2):
                    dve.wait_ge(dve_c, v)
                    src = mx if i == 0 else nmr
                    v = tick(dve.scalar_tensor_tensor(
                        nmr[:, :, :, :].rearrange("p t a r -> p (t a) r"),
                        src[:, :, :, :].rearrange("p t a r -> p (t a) r"), -1.0 if i == 0 else 1.0,
                        nm[:, :, :, i, :].rearrange("p t a r -> p (t a) r"), ALU.mult, ALU.subtract))
                    dve.wait_ge(dve_c, v)
                    w = dve.tensor_copy(nm[:, :, :, i + 1, :], nmr[:, :, :, :])
                    if i == 0:
                        v = tick(w)
                    else:
                        w.then_inc(nm_tok, 1)

            def qk_rest(b, t):
                dve.wait_ge(part_a, TT * b + t + 1)
                at_least(dve, parts, TT * (b - 1) + t + 1)
                dve.tensor_tensor(rest[:, t, :].rearrange("p (a h d) -> p a h d", a=2, d=HD),
                                  misc[(QKV0 + t) % 2][:, 0:2 * P].rearrange("p (a h d) -> p a h d", a=2, d=HD),
                                  stack[:, :, t, :, 0:HD], ALU.subtract).then_inc(part_r, 1)

            def qk_parts(b, t):
                q, k = stack[:, 0, t, :, :], stack[:, 1, t, :, :]
                first = stack[:, :, t, :, 0:HD]
                dve.wait_ge(part_r, TT * b + t + 1)
                dve.tensor_copy(rest_b[:, t, :], rest[:, t, :]).then_inc(part_b, 1)
                dve.tensor_copy(q[:, :, HD:3 * HD].rearrange("p h (i d) -> p h i d", i=2),
                                     first[:, 0].unsqueeze(2).to_broadcast([P, NH, 2, HD]))
                dve.tensor_copy(k[:, :, 3 * HD:4 * HD], first[:, 1])
                dve.tensor_copy(k[:, :, 5 * HD:6 * HD], first[:, 1])
                dve.wait_ge(part_b, TT * b + t + 1)
                sec = rest_b[:, t, :].rearrange("p (a h d) -> p a h d", a=2, d=HD)
                rst = rest[:, t, :].rearrange("p (a h d) -> p a h d", a=2, d=HD)
                dve.tensor_copy(stack[:, :, t, :, 4 * HD:5 * HD], sec)
                dve.tensor_copy(q[:, :, 3 * HD:4 * HD], sec[:, 0])
                dve.tensor_copy(k[:, :, HD:2 * HD], sec[:, 1])
                dve.tensor_tensor(q[:, :, 5 * HD:6 * HD], rst[:, 0], sec[:, 0], ALU.subtract)
                dve.tensor_tensor(k[:, :, 2 * HD:3 * HD], rst[:, 1], sec[:, 1], ALU.subtract).then_inc(parts, 1)

            def fill_out(b, f):
                dve.wait_ge(fill_ps, 4 * b + f + 1)
                if b >= 2:
                    dve.wait_ge(b_ps, 12 * (b - 2) + 6 * (f // 2) + 6)
                for par in range(2):
                    rows = slice(64 * par, 64 * par + 64)
                    dve.wait_ge(k_sb, 4 * b + f + 1)
                    dve.tensor_copy(qT[rows, b % 2, par, 2 * f:2 * f + 2, :], fill_view(b, f)[rows, 0]
                                    ).then_inc(q_sb, 1)

            def residual(b, t):
                tile = TT * b + t
                o = misc[(OT0 + t) % 2][:, :].rearrange("p (g w) -> p g w", w=VW)
                dve.wait_ge(ot_ps, tile + 1)
                at_least(dve, o_div, tile)
                v = tick(dve.reciprocal(rden[:, :], o[:, :, HD]))
                dve.wait_ge(dve_c, v)
                at_least(dve, added, tile - 1)
                dve.tensor_tensor(attn[:, t, :, :, :].rearrange("p a r d -> p (a r) d"), o[:, :, 0:HD],
                                  rden[:, :].unsqueeze(2).to_broadcast([P, NH, HD]), ALU.mult
                                  ).then_inc(o_div, 1)

            def statistics(b):
                for t in range(TT):
                    dve.wait_ge(added, TT * b + t + 1)
                    v = tick(dve.bn_stats(bst[:, t, :], x[:, TT * b + t, :]))
                at_least(dve, ln_x, TT * b)
                for t in range(TT):
                    dve.wait_ge(dve_c, v)
                    v = tick(dve.bn_aggr(mv[:, t, :], bst[:, t, :]))
                dve.wait_ge(dve_c, v)
                tick(dve.tensor_scalar(mv[:, :, 0], mv[:, :, 0], -1.0, None, ALU.mult))
                dve.tensor_scalar(mv[:, :, 1], mv[:, :, 1], LN_EPS, None, ALU.add).then_inc(ln_mv, 1)

            def softmax_a(b):
                dve.wait_ge(lg_ps, b + 1)
                at_least(dve, lg_exp, b)
                dve.tensor_tensor(lg[:, :, :], misc[LG % 2][:, 0:TT * E0].rearrange("p (t e) -> p t e", e=E0),
                                  rb0[:, :].unsqueeze(1).to_broadcast([P, TT, E0]), ALU.add
                                  ).then_inc(lg_in, 1)
                dve.wait_ge(lg_in, b + 1)
                v = tick(dve.tensor_reduce(lgm[:, :], lg[:, :, :], AX.X, ALU.max))
                dve.wait_ge(dve_c, v)
                dve.tensor_tensor(lg[:, :, :], lg[:, :, :], lgm[:, :].unsqueeze(2).to_broadcast([P, TT, E0]),
                                  ALU.subtract).then_inc(lg_sub, 1)

            def softmax_b(b):
                dve.wait_ge(lg_exp, b + 1)
                sv = sg[:, TT * b:TT * (b + 1), :]
                v = tick(dve.tensor_reduce(lgm[:, :], sv, AX.X, ALU.add))
                dve.wait_ge(dve_c, v)
                v = tick(dve.reciprocal(lgm[:, :], lgm[:, :]))
                dve.wait_ge(dve_c, v)
                dve.tensor_tensor(sv, sv, lgm[:, :].unsqueeze(2).to_broadcast([P, TT, E0]), ALU.mult
                                  ).then_inc(s_tok, 1)

            for s in range(-1, NB + 2):
                nxt, now, prev = 0 <= s + 1 < NB, 0 <= s < NB, 0 <= s - 2 < NB
                for k in range(12):
                    if now:
                        maxima(s, k)
                    if now and k in (0, 1):
                        fill_out(s, 2 + k)
                    if prev and k in (2, 3):
                        residual(s - 2, k - 2)
                    if nxt and k in (4, 5):
                        qk_rest(s + 1, k - 4)
                    if prev and k == 5:
                        statistics(s - 2)
                    if nxt and k in (6, 7):
                        qk_parts(s + 1, k - 6)
                    if nxt and k in (10, 11):
                        fill_out(s + 1, k - 10)
                if now:
                    neg_max(s)
                if prev:
                    softmax_a(s - 2)
                    softmax_b(s - 2)

        @block.tensor
        def _(pe):
            pe.wait_ge(consts, N_CONST)
            pe.wait_ge(ld_w, N_LDW)
            for i in range(3):
                mm = pe.transpose(misc[0][:, i * P:(i + 1) * P], w_nat[:, i, :], ident[:, :])
            mm.then_inc(wT_ps, 1)
            pe.wait_ge(wT_sb, 1)

            def scores_a(b, k):
                n = 12 * b + k
                u, c, par, pairs = chunk(k)
                bank = abank[n % 2]
                if c == 0:
                    pe.wait_ge(k_sb, 4 * b + 2 * u + 2)
                    pe.wait_ge(q_sb, 8 * b + 4 * u + 4)
                at_least(pe, a_max, n - 1)
                w = P if c < 2 else T
                t = 0 if c < 2 else 1
                pe.matmul(bank[:, :].rearrange("p (h s) -> p h s", h=len(pairs))[:, :, w - P:w], ident_b[:, :],
                          causal[:, 0:len(pairs), :], start=True, stop=False, skip_group_check=True)
                for j, pair in enumerate(pairs):
                    mm = pe.matmul(bank[:, j * w:(j + 1) * w], qT[:, b % 2, par, pair, t * P:(t + 1) * P],
                                   kT[:, b % 2, pair, 0:w], start=False, stop=True, skip_group_check=True)
                mm.then_inc(a_ps, 1)

            def scores_b(b, k):
                n = 12 * b + k
                u, c, par, pairs = chunk(k)
                bank = bbank[n % 3]
                if k == 0:
                    pe.wait_ge(nm_rows, 32 * (b + 1))
                at_least(pe, b_exp, n - 2)
                w, t0, s0 = (P, P, P) if c < 2 else (T, 0, 0)
                for j, pair in enumerate(pairs):
                    mm = pe.matmul(bank[:, j * w:(j + 1) * w], kT[:, b % 2, pair, s0:s0 + P],
                                   qT[:, b % 2, par, pair, t0:T], start=True, stop=True)
                mm.then_inc(b_ps, 1)

            def values(b, u):
                pe.wait_ge(b_cut, 4 * b + 2 * u + 2)
                at_least(pe, o_sb, 2 * b + u)
                for par in range(2):
                    for j in range(4):
                        h = 8 * u + 2 * j + par
                        pe.matmul(obank[32 * j:32 * j + 32, par * T:(par + 1) * T], vaug[:, b % 3, 0, h, :],
                                  probs[:, u, 2 + 2 * (j // 2) + par, (j % 2) * T:(j % 2 + 1) * T],
                                  start=True, stop=False)
                    for j in range(4):
                        h = 8 * u + 2 * j + par
                        mm = pe.matmul(obank[32 * j:32 * j + 32, par * T + P:(par + 1) * T], vaug[:, b % 3, 1, h, :],
                                       probs[:, u, par, j * P:(j + 1) * P], start=False, stop=True)
                mm.then_inc(pv_ps, 1)

            def free_bank(s, n):
                if (s, n) in ((-1, INT), (-1, QKV0)):
                    return pe.wait_ge(wT_sb, 1)
                a, m = max((a, m) for a in (s - 1, s) for m in range(n % 2, MISC, 2) if uses(a)[m] and (a, m) < (s, n))
                ahead, read, per_sequence, nth = emptied[m]
                pe.wait_ge(read, per_sequence * (a + ahead) + nth)

            def nm_rows_T(b):
                free_bank(b + 1, NMT)
                pe.wait_ge(nm_tok, b + 1)
                for t in range(TT):
                    mm = pe.transpose(misc[NMT % 2][:, :].bitcast(BF16)[0:48, t * P:(t + 1) * P],
                                      nm[:, t, :, :, :].rearrange("p a i r -> p (a i r)"), ident_b[:, :])
                mm.then_inc(nmT_ps, 1)

            def o_T(b, t):
                free_bank(b + 2, OT0 + t)
                if t == 0:
                    pe.wait_ge(o_sb, 2 * (b + 1))
                for par in range(2):
                    for u in range(2):
                        g = par * 2 + u
                        mm = pe.transpose(misc[(OT0 + t) % 2][:, g * P:(g + 1) * P],
                                          oT[:, b % 2, u, par, t * P:(t + 1) * P], ident[:, :])
                mm.then_inc(ot_ps, 1)

            def in_tr(b):
                free_bank(b - 1, INT)
                pe.wait_ge(ld_x[b], 16)
                for t in range(TT):
                    mm = pe.transpose(misc[INT % 2][:, t * P:(t + 1) * P], x[:, TT * b + t, 0:HC], ident[:, :])
                mm.then_inc(inT_ps, 1)

            def qkv(b, t):
                free_bank(b - 1, QKV0 + t)
                pe.wait_ge(inT_sb, b + 1)
                pe.matmul(misc[(QKV0 + t) % 2][:, 0:3 * P], in_T[:, b % 2, t * P:(t + 1) * P], wT[:, :],
                          start=True, stop=True).then_inc(qkv_ps, 1)

            def fill(b, f):
                free_bank(b - 1 if f < 2 else b, fills[f])
                pe.wait_ge(parts, TT * (b + 1))
                view = misc[fills[f] % 2][:, :].bitcast(BF16).rearrange("p (a r t n) -> p a r t n", a=2, r=2, t=TT)
                for a in range(2):
                    for r in range(2):
                        for t in range(TT):
                            pair = 2 * f + r
                            mm = pe.transpose(view[:, a, r, t, :],
                                              stack[:, a, t, 2 * pair:2 * pair + 2, :].rearrange("p h d -> p (h d)"),
                                              ident_b[:, :])
                mm.then_inc(fill_ps, 1)

            def x_T(b):
                free_bank(b + 2, XT)
                pe.wait_ge(ln_x, TT * (b + 1))
                for k in range(2):
                    for t in range(TT):
                        mm = pe.transpose(misc[XT % 2][:, (k * TT + t) * P:(k * TT + t + 1) * P],
                                          x[:, TT * b + t, k * P:(k + 1) * P], ident[:, :])
                mm.then_inc(xT_ps, 1)

            def logits(b):
                free_bank(b + 2, LG)
                pe.wait_ge(xT_sb, b + 1)
                for t in range(TT):
                    for k in range(2):
                        mm = pe.matmul(misc[LG % 2][:, t * E0:(t + 1) * E0],
                                       xT[:, k, (TT * b + t) * P:(TT * b + t + 1) * P], r0w[:, k, :],
                                       start=(k == 0), stop=(k == 1))
                mm.then_inc(lg_ps, 1)

            for s in range(-1, NB + 2):
                nxt, now, cur, prev = 0 <= s + 1 < NB, 0 <= s < NB, 0 <= s - 1 < NB, 0 <= s - 2 < NB
                for k in range(12):
                    if now:
                        scores_a(s, k)
                    if cur and k >= 3:
                        scores_b(s - 1, k - 3)
                    if cur and k == 0:
                        nm_rows_T(s - 1)
                    if prev and k == 0:
                        values(s - 2, 1)
                    if now and k in (0, 1):
                        fill(s, 2 + k)
                    if prev and k in (1, 2):
                        o_T(s - 2, k - 1)
                    if nxt and k == 3:
                        in_tr(s + 1)
                    if nxt and k in (4, 5):
                        qkv(s + 1, k - 4)
                    if nxt and k in (10, 11):
                        fill(s + 1, k - 10)
                if cur:
                    scores_b(s - 1, 9)
                    values(s - 1, 0)
                if prev:
                    x_T(s - 2)
                if cur:
                    scores_b(s - 1, 10)
                    scores_b(s - 1, 11)
                if prev:
                    logits(s - 2)


def rest_of_layers(nc, m, out):
    with ExitStack() as ctx:
        x, xT, sg, ident, half_neg = m.x, m.xT, m.sg, m.ident, m.half_neg

        def sb(name, shape, dt=F32):
            return ctx.enter_context(nc.sbuf_tensor(name, shape, dt))

        def psum(name, shape, dt=F32):
            return ctx.enter_context(nc.psum_tensor(name, shape, dt))

        def sem(name):
            return ctx.enter_context(nc.semaphore(name))

        def at_least(eng, s, n):
            if n > 0:
                eng.wait_ge(s, n)

        prob = sb("prob", [P, 2, P])
        over = sb("over", [P, 2, P])
        tie = sb("tie", [P, 2, P])
        nth = sb("nth", [P, 2, P])
        cand = sb("cand", [P, 1], I32)
        flip = sb("flip", [P, 1], I32)
        cnt = sb("cnt", [P, 3])
        lim = sb("lim", [P, 2])
        tot = sb("tot", [P, 5])
        gsum = sb("gsum", [P, NT])
        y0 = sb("y0", [P, NT, C])
        w1T = sb("w1T", [P, 2, 2 * C])
        b1h = sb("b1h", [P, 2])
        gate = sb("gate", [P, 2, NB * T])
        val = sb("val", [P, 2, NB * T])
        hid = sb("hid", [P, 2, NB * T])
        bst = sb("bst2", [P, NT, 6])
        mv = sb("mv2", [P, NT, 2])
        rstd = sb("rstd2", [P, NT])
        shift = sb("shift2", [P, NT])
        sq = sb("sq", [P, C])
        ss = sb("ss", [P, NT])
        rr = sb("rr", [P, NT])
        xr = sb("xr", [P, QT, C])
        hT = sb("hT", [P, 2, NB * T])
        lg1 = sb("lg1", [P, QT, E1])
        red = sb("red", [P, QT])
        p1 = sb("p1", [P, QT, E1])
        top = sb("top", [P, QT, E1])
        w1 = sb("w1", [P, NT, E1])
        half = sb("half", [P, 2, QN])
        act_in = sb("act_in", [P, 2, QN])

        tr = [psum(f"tr{i}", [P, 512]) for i in range(2)]
        mm = [psum(f"mm{i}", [P, 512]) for i in range(4)]
        zb, gb, ub = mm[0:2], mm[2], mm[3]
        dn = [psum(f"dn{i}", [P, 512]) for i in range(2)]

        y0_ok = sem("y0_ok")
        pr_ps, pr_sb, w1_ps, w1_sb = sem("pr_ps"), sem("pr_sb"), sem("w1_ps"), sem("w1_sb")
        cand_ok, counted, totals = sem("cand_ok"), sem("counted"), sem("totals")
        y0_ps, y0_sb = sem("y0_ps"), sem("y0_sb")
        chosen, g_ps, g_sb = sem("chosen"), sem("g_ps"), sem("g_sb")
        ln_mv = [sem(f"ln{i}_mv") for i in range(3)]
        ln_rs = [sem(f"ln{i}_rs") for i in range(3)]
        rr_ok = sem("rr_ok")
        ln_dve = [sem(f"ln{i}_dve") for i in range(3)]
        ln_act = [sem(f"ln{i}_act") for i in range(3)]
        x2_ps, x2_sb = sem("x2_ps"), sem("x2_sb")
        z_ps, z_sb, g_ok, scanned, h_ps, h_add = (sem("z_ps"), sem("z_sb"), sem("g_ok"), sem("scanned"),
                                                  sem("h_ps"), sem("h_add"))
        sq_ok, ms_ok, xr_ok, xr_ps, hT_ok = sem("sq_ok"), sem("ms_ok"), sem("xr_ok"), sem("xr_ps"), sem("hT_ok")
        lg_ps, lg_rd, lg_sub, lg_exp, w_ok = sem("lg1_ps"), sem("lg1_rd"), sem("lg1_sub"), sem("lg1_exp"), sem("w_ok")
        gu_ps, sil_ok, act_ok, dn_ps, dn_add = sem("gu_ps"), sem("sil_ok"), sem("act_ok"), sem("dn_ps"), sem("dn_add")
        dve_c, act_c, pool_c = sem("dve_c2"), sem("act_c2"), sem("pool_c2")
        stored = sem("stored")
        mul_ok = sem("mul_ok")
        EX = E1 + 1

        (ADD, NORM, TURN, LIN0, LIN1, SCAN, HID, NORM1, RMS, TURN1, ROUTE0, ROUTE1) = range(12)
        STAGES = 12
        steps = []
        for t in range(FIRST_EXPERT + Q * EX + 1):
            stages = [(t - b, q) for q, b in enumerate(BEGIN) if 0 <= t - b < STAGES]
            steps.append((t - FIRST_EXPERT, stages))
        tr_uses = []
        for _, stages in steps:
            for g, q in stages:
                if g in (TURN, HID, TURN1, ROUTE0):
                    tr_uses.append((g, q))
        tr_read = {TURN: x2_sb, HID: h_add, TURN1: hT_ok}

        block = ctx.enter_context(nc.Block())

        def tr_free(pe, g, q, i):
            k = tr_uses.index((g, q))
            if k == 0:
                return pe.wait_ge(g_sb, 1)
            before = tr_uses[:k] if i == 0 else [u for u in tr_uses[:k] if u[0] != ROUTE0]
            if not before:
                return pe.wait_ge(g_sb, 1)
            pg, pq = before[-1]
            if pg == ROUTE0:
                pe.wait_ge(lg_sub, pq + 1)
            else:
                pe.wait_ge(tr_read[pg], 2 * pq + i + 1)

        def follow(emit_stage, emit_expert):
            for i, stages in steps:
                if 0 <= i <= Q * EX:
                    emit_expert(i, lambda: [emit_stage(g, q) for g, q in stages])
                else:
                    for g, q in stages:
                        emit_stage(g, q)

        def normalise(eng, i, q, tiles):
            eng.wait_ge(ln_rs[i], 2 * (q + 1))
            for n in tiles:
                n += QT * q
                if eng is nc.scalar:
                    w = nc.scalar.activation(x[:, n, :], x[:, n, :], ACT.Identity, bias=shift[:, n:n + 1],
                                             scale=rstd[:, n:n + 1])
                else:
                    w = eng.tensor_scalar(x[:, n, :], x[:, n, :], rstd[:, n:n + 1], shift[:, n:n + 1], ALU.mult,
                                          ALU.add)
                w.then_inc((ln_act if eng is nc.scalar else ln_dve)[i], 1)

        def normed(eng, i, q):
            eng.wait_ge(ln_dve[i], ON_DVE * (q + 1))
            eng.wait_ge(ln_act[i], (QT - ON_DVE) * (q + 1))

        @block.sync
        def _(sp):
            for q in range(Q):
                normed(sp, 2, q)
                for h in range(2):
                    sp.dma_start(out[2 * q + h].rearrange("(n p) c -> p n c", p=P),
                                 x[:, QT * q + TT * h:QT * q + TT * (h + 1), :]).then_inc(stored, 16)
            sp.wait_ge(stored, 16 * NB)

        @block.gpsimd
        def _(pool):
            for i in range(NT // 2):
                pool.wait_ge(y0_sb, i + 1)
                yv = y0[:, 2 * i:2 * i + 2, :]
                pool.tensor_tensor(yv, yv, m.e0b[:, :].unsqueeze(1).to_broadcast([P, 2, C]), ALU.add
                                   ).then_inc(y0_ok, 1)

            def scales(i, q):
                n0, n1 = QT * q, QT * (q + 1)
                pool.wait_ge(ln_mv[i], q + 1)
                if i > 0:
                    normed(pool, i - 1, q)
                pool.tensor_tensor(rstd[:, n0:n1], mv[:, n0:n1, 1], half_neg[:, 0:QT], ALU.pow
                                   ).then_inc(ln_rs[i], 1)
                pool.wait_ge(ln_rs[i], 2 * q + 1)
                pool.tensor_tensor(shift[:, n0:n1], mv[:, n0:n1, 0], rstd[:, n0:n1], ALU.mult).then_inc(ln_rs[i], 1)

            def sigmoid(q, k):
                pool.wait_ge(z_sb, 4 * q + 2 * k + 1)
                gv = gate[:, k, QN * q:QN * (q + 1)]
                pool.tensor_scalar(gv, gv, 0.5, 0.5, ALU.mult, ALU.add).then_inc(g_ok, 1)

            def over_rms(q):
                n0, n1 = QT * q, QT * (q + 1)
                pool.wait_ge(ms_ok, q + 1)
                pool.tensor_tensor(rr[:, n0:n1], ss[:, n0:n1], half_neg[:, 0:QT], ALU.pow).then_inc(rr_ok, 1)

            def stage(g, q):
                if g == ADD:
                    scales(0, q)
                elif g in (LIN0, LIN1):
                    sigmoid(q, g - LIN0)
                elif g == HID:
                    scales(1, q)
                elif g == RMS:
                    over_rms(q)

            def expert(i, side):
                if i > 0 and i % EX == 0:
                    scales(2, i // EX - 1)
                side()

            follow(stage, expert)

        @block.scalar
        def _(act):
            for k in range(2):
                act.wait_ge(w1_ps, k + 1)
                act.copy(w1T[:, k, :], mm[k][:, :]).then_inc(w1_sb, 1)
            act.mul(b1h[:, :], m.b1[:, 0:2], 0.5).then_inc(act_c, 1)
            for i in range(NT // 2):
                act.wait_ge(y0_ps, i + 1)
                act.copy(y0[:, 2 * i:2 * i + 2, :], mm[i % 4][:, :].rearrange("p (n c) -> p n c", n=2)
                         ).then_inc(y0_sb, 1)
            act.wait_ge(act_c, 1)

            def x2_out(q):
                for k in range(2):
                    act.wait_ge(x2_ps, 2 * q + k + 1)
                    act.copy(xT[:, k, QN * q:QN * (q + 1)], tr[k][:, :]).then_inc(x2_sb, 1)

            def squash(q, k):
                act.wait_ge(z_ps, 4 * q + 2 * k + 1)
                act.activation(gate[:, k, QN * q:QN * (q + 1)], zb[0][:, :], ACT.Tanh, bias=b1h[:, k:k + 1],
                               scale=0.5).then_inc(z_sb, 1)
                act.wait_ge(z_ps, 4 * q + 2 * k + 2)
                act.activation(val[:, k, QN * q:QN * (q + 1)], zb[1][:, :], ACT.Tanh,
                               bias=m.b1[:, 2 + k:3 + k]).then_inc(z_sb, 1)

            def squares(q):
                normed(act, 1, q)
                for n in range(QT * q, QT * (q + 1)):
                    at_least(act, sq_ok, n)
                    act.activation(sq[:, :], x[:, n, :], ACT.Square, accum_out=ss[:, n:n + 1]).then_inc(sq_ok, 1)

            def hT_out(q):
                for k in range(2):
                    act.wait_ge(xr_ps, 2 * q + k + 1)
                    act.activation(hT[:, k, QN * q:QN * (q + 1)], tr[k][:, :], ACT.Copy,
                                   scale=m.rms[:, k:k + 1]).then_inc(hT_ok, 1)

            def lg_out(q):
                act.wait_ge(lg_sub, q + 1)
                act.activation(p1[:, :, :], lg1[:, :, :], ACT.Exp).then_inc(lg_exp, 1)

            def stage(g, q):
                if g == NORM:
                    normalise(act, 0, q, range(ON_DVE, QT))
                elif g == TURN:
                    x2_out(q)
                elif g in (LIN0, LIN1):
                    squash(q, g - LIN0)
                elif g == NORM1:
                    normalise(act, 1, q, range(ON_DVE, QT))
                    squares(q)
                elif g == TURN1:
                    hT_out(q)
                elif g == ROUTE0:
                    lg_out(q)

            def expert(i, side):
                if i < Q * EX:
                    act.wait_ge(gu_ps, 2 * i + 1)
                    at_least(act, act_ok, i - 1)
                    act.activation(half[:, i % 2, :], gb[:, :], ACT.Tanh, scale=0.5).then_inc(sil_ok, 1)
                if i > 0 and i % EX == 0:
                    normalise(act, 2, i // EX - 1, range(ON_DVE, QT))
                side()

            follow(stage, expert)

        @block.vector
        def _(dve):
            ticks = [0]

            def tick(ins):
                ticks[0] += 1
                ins.then_inc(dve_c, 1)
                return ticks[0]

            dve.wait_ge(pr_ps, 1)
            dve.tensor_copy(prob[:, :, :], tr[0][:, 0:2 * P].rearrange("p (j t) -> p j t", j=2)).then_inc(pr_sb, 1)
            dve.memset(cand[:, :], 1 << (BITS - 1)).then_inc(cand_ok, 1)
            dve.wait_ge(pr_sb, 1)
            for r in range(BITS):
                bit = 1 << (BITS - 1 - r)
                dve.wait_ge(cand_ok, r + 1)
                at_least(dve, totals, r)
                dve.tensor_scalar(over[:, :, :].rearrange("p j t -> p (j t)"),
                                  prob[:, :, :].rearrange("p j t -> p (j t)"), cand[:, :].bitcast(F32), None,
                                  ALU.is_ge, ALU.add, accum_out=cnt[:, 0:1]).then_inc(counted, 1)
                dve.wait_ge(totals, r + 1)
                v = tick(dve.tensor_scalar(flip[:, :], tr[1][:, r % 2:r % 2 + 1], float(TOP), float(bit), ALU.is_lt,
                                           ALU.mult))
                dve.wait_ge(dve_c, v)
                dve.scalar_tensor_tensor(cand[:, :], flip[:, :], bit >> 1, cand[:, :], ALU.bitwise_xor,
                                         ALU.bitwise_xor).then_inc(cand_ok, 1)
            dve.wait_ge(cand_ok, BITS + 1)
            dve.tensor_scalar(over[:, :, :].rearrange("p j t -> p (j t)"),
                              prob[:, :, :].rearrange("p j t -> p (j t)"), cand[:, :].bitcast(F32), None, ALU.is_gt,
                              ALU.add, accum_out=cnt[:, 0:1])
            for j in range(2):
                w = dve.tensor_scalar(tie[:, j, :], prob[:, j, :], cand[:, :].bitcast(F32), None, ALU.is_equal,
                                      ALU.add, accum_out=cnt[:, 1 + j:2 + j])
            w.then_inc(counted, 1)
            dve.wait_ge(counted, BITS + 1)
            for j in range(2):
                v = tick(dve.tensor_tensor_scan(nth[:, j, :], m.ones[:, :], tie[:, j, :], 0.0, ALU.mult, ALU.add))
            dve.wait_ge(totals, BITS + 1)
            v = tick(dve.tensor_copy(tot[:, :], tr[1][:, 2:7]))
            dve.wait_ge(dve_c, v)
            v = tick(dve.tensor_scalar(lim[:, 0:1], tot[:, 0:1], -1.0, float(TOP), ALU.mult, ALU.add))
            dve.wait_ge(dve_c, v)
            v = tick(dve.tensor_tensor(lim[:, 1:2], lim[:, 0:1], tot[:, 1:2], ALU.subtract))
            dve.wait_ge(dve_c, v)
            v = tick(dve.tensor_tensor(lim[:, :], lim[:, :], tot[:, 3:5], ALU.subtract))
            dve.wait_ge(dve_c, v)
            for j in range(2):
                v = tick(dve.scalar_tensor_tensor(tie[:, j, :], nth[:, j, :], lim[:, j:j + 1], tie[:, j, :],
                                                  ALU.is_le, ALU.mult))
            dve.wait_ge(dve_c, v)
            v = tick(dve.tensor_tensor(over[:, :, :], over[:, :, :], tie[:, :, :], ALU.add))
            dve.wait_ge(dve_c, v)
            dve.tensor_tensor(over[:, :, :], over[:, :, :], prob[:, :, :], ALU.mult).then_inc(chosen, 1)
            dve.wait_ge(g_ps, 1)
            dve.tensor_reduce(gsum[:, :].rearrange("p (j c) -> p j c", j=2),
                              tr[0][:, 0:2 * P].rearrange("p (j c e) -> p j c e", j=2, e=E0), AX.X, ALU.add
                              ).then_inc(g_sb, 1)
            dve.wait_ge(g_sb, 1)

            def statistics(i, q):
                n0, n1 = QT * q, QT * (q + 1)
                for n in range(n0, n1):
                    v = tick(dve.bn_stats(bst[:, n, :], x[:, n, :]))
                dve.wait_ge(dve_c, v)
                for n in range(n0, n1):
                    v = tick(dve.bn_aggr(mv[:, n, :], bst[:, n, :]))
                dve.wait_ge(dve_c, v)
                tick(dve.tensor_scalar(mv[:, n0:n1, 0], mv[:, n0:n1, 0], -1.0, None, ALU.mult))
                dve.tensor_scalar(mv[:, n0:n1, 1], mv[:, n0:n1, 1], LN_EPS, None, ALU.add).then_inc(ln_mv[i], 1)

            def add_experts(q):
                dve.wait_ge(y0_ok, QT // 2 * (q + 1))
                for n in range(QT * q, QT * (q + 1)):
                    v = tick(dve.scalar_tensor_tensor(x[:, n, :], y0[:, n, :], gsum[:, n:n + 1], x[:, n, :],
                                                      ALU.mult, ALU.add))
                dve.wait_ge(dve_c, v)
                statistics(0, q)

            def recur(q):
                for k in range(2):
                    dve.wait_ge(g_ok, 2 * q + k + 1)
                    dve.wait_ge(z_sb, 4 * q + 2 * k + 2)
                    for h in range(2):
                        at = slice(QN * q + T * h, QN * q + T * (h + 1))
                        w = dve.tensor_tensor_scan(hid[:, k, at], gate[:, k, at], val[:, k, at], 0.0, ALU.mult,
                                                   ALU.add)
                    w.then_inc(scanned, 1)

            def add_hidden(q):
                for i in range(2):
                    dve.wait_ge(h_ps, 2 * q + i + 1)
                    xv = x[:, QT * q + 2 * i:QT * q + 2 * i + 2, :]
                    dve.tensor_tensor(xv, xv, tr[i][:, :].rearrange("p (n c) -> p n c", n=2), ALU.add
                                      ).then_inc(h_add, 1)
                dve.wait_ge(h_add, 2 * (q + 1))
                statistics(1, q)

            def mean_square(q):
                n0, n1 = QT * q, QT * (q + 1)
                dve.wait_ge(sq_ok, n1)
                dve.tensor_scalar(ss[:, n0:n1], ss[:, n0:n1], 1.0 / C, RMS_EPS, ALU.mult, ALU.add).then_inc(ms_ok, 1)

            def over_rms(q):
                dve.wait_ge(rr_ok, q + 1)
                at_least(dve, xr_ps, 2 * q)
                for t in range(QT):
                    n = QT * q + t
                    dve.tensor_scalar(xr[:, t, :], x[:, n, :], rr[:, n:n + 1], None, ALU.mult).then_inc(xr_ok, 1)

            wide = [P, QT, E1]

            def route_in(q):
                dve.wait_ge(lg_ps, q + 1)
                at_least(dve, w_ok, q)
                z = tr[0][:, 0:QT * E1].rearrange("p (n e) -> p n e", e=E1)
                v = tick(dve.tensor_reduce(red[:, :], z, AX.X, ALU.max))
                dve.wait_ge(dve_c, v)
                dve.tensor_tensor(lg1[:, :, :], z, red[:, :].unsqueeze(2).to_broadcast(wide), ALU.subtract
                                  ).then_inc(lg_sub, 1)

            def route_out(q):
                dve.wait_ge(lg_exp, q + 1)
                v = tick(dve.tensor_reduce(red[:, :], p1[:, :, :], AX.X, ALU.add))
                dve.wait_ge(dve_c, v)
                v = tick(dve.reciprocal(red[:, :], red[:, :]))
                dve.wait_ge(dve_c, v)
                v = tick(dve.tensor_tensor(p1[:, :, :], p1[:, :, :], red[:, :].unsqueeze(2).to_broadcast(wide),
                                           ALU.mult))
                dve.wait_ge(dve_c, v)
                for n in range(QT):
                    v = tick(dve.max(top[:, n, :], p1[:, n, :]))
                dve.wait_ge(dve_c, v)
                v = tick(dve.tensor_tensor(red[:, :], top[:, :, 0], top[:, :, 1], ALU.add))
                v = tick(dve.memset(top[:, :, TOP1:], -1.0))
                dve.wait_ge(dve_c, v)
                v = tick(dve.reciprocal(red[:, :], red[:, :]))
                wv = w1[:, QT * q:QT * (q + 1), :]
                for n in range(QT):
                    v = tick(dve.match_replace(out=w1[:, QT * q + n, :], in_to_replace=top[:, n, :],
                                               in_values=p1[:, n, :], imm_value=0.0))
                dve.wait_ge(dve_c, v)
                v = tick(dve.tensor_tensor(wv, p1[:, :, :], wv, ALU.subtract))
                dve.wait_ge(dve_c, v)
                dve.scalar_tensor_tensor(wv, wv, 0.5, red[:, :].unsqueeze(2).to_broadcast(wide), ALU.mult, ALU.mult
                                         ).then_inc(w_ok, 1)

            def stage(g, q):
                if g == ADD:
                    add_experts(q)
                elif g == NORM:
                    normalise(dve, 0, q, range(ON_DVE))
                elif g == SCAN:
                    recur(q)
                elif g == HID:
                    add_hidden(q)
                elif g == NORM1:
                    normalise(dve, 1, q, range(ON_DVE))
                elif g == RMS:
                    mean_square(q)
                elif g == TURN1:
                    over_rms(q)
                elif g == ROUTE0:
                    route_in(q)
                elif g == ROUTE1:
                    route_out(q)

            def gated(i):
                h = half[:, i % 2, :]
                dve.wait_ge(sil_ok, i + 1)
                dve.scalar_tensor_tensor(h, h, 1.0, gb[:, :], ALU.add, ALU.mult).then_inc(mul_ok, 1)
                dve.wait_ge(gu_ps, 2 * (i + 1))
                at_least(dve, dn_ps, 2 * (i - 1))
                dve.wait_ge(mul_ok, i + 1)
                dve.tensor_tensor(act_in[:, i % 2, :], h, ub[:, :], ALU.mult).then_inc(act_ok, 1)

            def add_down(i):
                q, e = divmod(i, EX)
                if e == 1:
                    dve.wait_ge(w_ok, q + 1)
                for t in range(QT):
                    n = QT * q + t
                    if t % 2 == 0:
                        dve.wait_ge(dn_ps, 2 * i + t // 2 + 1)
                    if e > 0:
                        dve.wait_ge(dn_add, QT * (i - 1) + t + 1)
                    d = dn[t // 2][:, (t % 2) * C:(t % 2 + 1) * C]
                    share = 0.5 if e == 0 else w1[:, n, e - 1:e]
                    dve.scalar_tensor_tensor(x[:, n, :], d, share, x[:, n, :], ALU.mult, ALU.add
                                             ).then_inc(dn_add, 1)

            def expert(i, side):
                if i < Q * EX:
                    gated(i)
                if i > 0:
                    add_down(i - 1)
                if i > 0 and i % EX == 0:
                    dve.wait_ge(dn_add, QT * i)
                    statistics(2, i // EX - 1)
                    normalise(dve, 2, i // EX - 1, range(ON_DVE))
                side()

            follow(stage, expert)

        @block.tensor
        def _(pe):
            for j in range(2):
                w = pe.transpose(tr[0][:, j * P:(j + 1) * P],
                                 sg[:, NB * j:NB * (j + 1), :].rearrange("p c e -> p (c e)"), ident[:, :])
            w.then_inc(pr_ps, 1)
            for k in range(2):
                for d in range(4):
                    w = pe.transpose(mm[k][:, d * P:(d + 1) * P], m.w1_nat[:, d, k * P:(k + 1) * P], ident[:, :])
                w.then_inc(w1_ps, 1)

            def y0_piece(k):
                n, part = divmod(k, 2)
                i = n // 2
                if n % 2 == 0 and part == 0:
                    pe.wait_ge(w1_sb, 2)
                    at_least(pe, y0_sb, i - 3)
                w = pe.matmul(mm[i % 4][:, (n % 2) * C:(n % 2 + 1) * C], xT[:, part, n * P:(n + 1) * P],
                              m.e0w[:, part, :], start=(part == 0), stop=(part == 1))
                if part == 1 and n % 2 == 1:
                    w.then_inc(y0_ps, 1)

            same = m.same[:, :, :].rearrange("p c e -> p (c e)")
            before = m.before[:, :, :].rearrange("p c e -> p (c e)")
            for r in range(BITS):
                pe.wait_ge(counted, r + 1)
                at_least(pe, cand_ok, r)
                pe.matmul(tr[1][:, r % 2:r % 2 + 1], same, cnt[:, 0:1], start=True, stop=True).then_inc(totals, 1)
                for k in range(2 * NT * r // BITS, 2 * NT * (r + 1) // BITS):
                    y0_piece(k)
            pe.wait_ge(counted, BITS + 1)
            pe.matmul(tr[1][:, 2:5], same, cnt[:, :], start=True, stop=True)
            pe.matmul(tr[1][:, 5:7], before, cnt[:, 1:3], start=True, stop=True).then_inc(totals, 1)
            pe.wait_ge(chosen, 1)
            for j in range(2):
                w = pe.transpose(tr[0][:, j * P:(j + 1) * P], over[:, j, :], ident[:, :])
            w.then_inc(g_ps, 1)
            pe.wait_ge(y0_sb, NT // 2)

            def x2_T(q):
                normed(pe, 0, q)
                for k in range(2):
                    tr_free(pe, TURN, q, k)
                    for t in range(QT):
                        w = pe.transpose(tr[k][:, t * P:(t + 1) * P], x[:, QT * q + t, k * P:(k + 1) * P],
                                         ident[:, :])
                    w.then_inc(x2_ps, 1)

            def linear(q, k):
                for j in range(2):
                    d = 2 * j + k
                    at_least(pe, z_sb, 4 * q + 2 * k + j - 1)
                    for c in range(2):
                        if k == 0 and j == 0:
                            pe.wait_ge(x2_sb, 2 * q + c + 1)
                        w = pe.matmul(zb[j][:, :], w1T[:, c, d * P:(d + 1) * P], xT[:, c, QN * q:QN * (q + 1)],
                                      start=(c == 0), stop=(c == 1))
                    w.then_inc(z_ps, 1)

            def hidden_T(q):
                pe.wait_ge(scanned, 2 * (q + 1))
                for i in range(2):
                    tr_free(pe, HID, q, i)
                    for t in range(2):
                        for k in range(2):
                            n = QT * q + 2 * i + t
                            w = pe.transpose(tr[i][:, (2 * t + k) * P:(2 * t + k + 1) * P],
                                             hid[:, k, n * P:(n + 1) * P], ident[:, :])
                    w.then_inc(h_ps, 1)

            def h_T(q):
                pe.wait_ge(xr_ok, QT * (q + 1))
                for k in range(2):
                    tr_free(pe, TURN1, q, k)
                    for t in range(QT):
                        w = pe.transpose(tr[k][:, t * P:(t + 1) * P], xr[:, t, k * P:(k + 1) * P], ident[:, :])
                    w.then_inc(xr_ps, 1)

            def logits(q):
                pe.wait_ge(hT_ok, 2 * (q + 1))
                tr_free(pe, ROUTE0, q, 0)
                for t in range(QT):
                    for k in range(2):
                        n = QT * q + t
                        w = pe.matmul(tr[0][:, t * E1:(t + 1) * E1], hT[:, k, n * P:(n + 1) * P], m.r1w[:, k, :],
                                      start=(k == 0), stop=(k == 1))
                w.then_inc(lg_ps, 1)

            def stage(g, q):
                if g == TURN:
                    x2_T(q)
                elif g in (LIN0, LIN1):
                    linear(q, g - LIN0)
                elif g == HID:
                    hidden_T(q)
                elif g == TURN1:
                    h_T(q)
                elif g == ROUTE0:
                    logits(q)

            def gate_up(i):
                q, e = divmod(i, EX)
                if e == 0:
                    pe.wait_ge(hT_ok, 2 * (q + 1))
                for j, (bank, weights, free) in enumerate(((gb, m.wg, mul_ok), (ub, m.wu, act_ok))):
                    at_least(pe, free, i)
                    for k in range(2):
                        w = pe.matmul(bank[:, :], weights[:, e, k, :], hT[:, k, QN * q:QN * (q + 1)],
                                      start=(k == 0), stop=(k == 1))
                    w.then_inc(gu_ps, 1)

            def down(i):
                e = i % EX
                pe.wait_ge(act_ok, i + 1)
                for t in range(QT):
                    if t % 2 == 0:
                        at_least(pe, dn_add, QT * (i - 1) + t + 2)
                    w = pe.matmul(dn[t // 2][:, (t % 2) * C:(t % 2 + 1) * C], act_in[:, i % 2, t * P:(t + 1) * P],
                                  m.wd[:, e, :], start=True, stop=True)
                    if t % 2 == 1:
                        w.then_inc(dn_ps, 1)

            def expert(i, side):
                if i < Q * EX:
                    gate_up(i)
                if i > 0:
                    down(i - 1)
                side()

            follow(stage, expert)



INPUTS = ["L0_attn_x", "L0_attn_Wq", "L0_attn_Wk", "L0_attn_Wv", "L0_ffn_router_w", "L0_ffn_router_b",
          "L0_ffn_expert_w", "L0_ffn_expert_b", "L1_attn_W", "L1_attn_b", "L1_ffn_rms_weight", "L1_ffn_router_w",
          "L1_ffn_w_gate", "L1_ffn_w_up", "L1_ffn_w_down", "L1_ffn_sw_gate", "L1_ffn_sw_up", "L1_ffn_sw_down"]


def kernel(**inputs):
    import numpy as np
    import concourse.bacc as bacc
    from concourse.bass_utils import run_bass_kernel_spmd

    nc = bacc.Bacc("TRN2", target_bir_lowering=False, num_devices=1)
    arrays, args = {}, []
    for name in INPUTS:
        a = np.ascontiguousarray(inputs[name])
        arrays[f"in_{name}"] = a
        args.append(nc.dram_tensor(f"in_{name}", a.shape, mybir.dt.from_np(a.dtype), kind="ExternalInput").ap())
    out = nc.dram_tensor("out", (NB, T, C), F32, kind="ExternalOutput").ap()
    program(nc, *args, out)
    return run_bass_kernel_spmd(nc, [arrays], core_ids=[0]).results[0]["out"]
```

```python
from contextlib import ExitStack

import concourse.bass as bass
from concourse import mybir

F32 = mybir.dt.float32
BF16 = mybir.dt.bfloat16
I32 = mybir.dt.int32
F32R = mybir.dt.float32r
ACT = mybir.ActivationFunctionType
ALU = mybir.AluOpType
AX = mybir.AxisListType

P = 128
NB, T, C = 8, 256, 256
TT = T // P
NT = NB * TT
HC = 128
NH, HD = 16, 8
PAIRS = NH // 2
SLOTS = 6
KS = SLOTS * HD
KM = KS + 3
NMT_SLOT = 0
STAT_SLOT = 0
REST_SLOTS = (1, 2)
NORM_SLOT = 2
V1_SLOTS = (4, 5)
PART_SLOTS = (2, 5)
XT_SLOT = 5
LG_SLOT = 6
OT_SLOTS = (6, 7)
SOFT_SLOT = 7
RES_SLOTS = (7, 8)
SOFTB_SLOT = 9
FILL_SLOTS = (9, 10)
Q_LATE = 1
VB = 4
LAG = 3
VW = 32
NEG = -1.0e30
SCALE = float(HD) ** -0.5
LN_EPS = 1e-5
E0 = 16
TOP = NB * T // E0
BITS = 30
E1, TOP1 = 8, 2
FF = 128
RMS_EPS = 1e-6
Q = 4
QT = NT // Q
QN = QT * P
ON_DVE = 3
BEGIN = (0, 1, 3, 5)
FIRST_EXPERT = 13
MISC = 12


def program(nc, x_in, Wq, Wk, Wv, r0_w, r0_b, e0_w, e0_b, W1, b1, rms_w, r1_w, w_gate, w_up, w_down,
            sw_gate, sw_up, sw_down, out):
    with ExitStack() as whole:
        def keep(name, shape, dt=F32):
            return whole.enter_context(nc.sbuf_tensor(name, shape, dt))

        m = Kept()
        m.x = keep("x", [P, NT, C])
        m.xT = keep("xT", [P, 2, NB * T])
        m.sg = keep("sg", [P, NT, E0])
        m.ident = keep("ident", [P, P])
        m.half_neg = keep("half_neg", [P, NT])
        m.same = keep("same", [P, NB, E0], BF16)
        m.before = keep("before", [P, NB, E0], BF16)
        m.ones = keep("ones", [P, P])
        m.e0w = keep("e0w", [P, 2, C])
        m.e0b = keep("e0b", [P, C])
        m.w1_nat = keep("w1_nat", [P, 4, C])
        m.b1 = keep("b1s", [P, 4])
        m.rms = keep("rms", [P, 2])
        m.r1w = keep("r1w", [P, 2, E1])
        with nc.sbuf_tensor("w", [P, 3, E1 + 1, 2, FF], F32) as m.w:
            attention(nc, m, x_in, Wq, Wk, Wv, r0_w, r0_b, e0_w, e0_b, W1, b1, rms_w, r1_w, w_gate, w_up, w_down,
                      sw_gate, sw_up, sw_down)
        rest_of_layers(nc, m, out)


class Kept:
    pass


def attention(nc, m, x_in, Wq, Wk, Wv, r0_w, r0_b, e0_w, e0_b, W1, b1, rms_w, r1_w, w_gate, w_up, w_down,
              sw_gate, sw_up, sw_down):
    with ExitStack() as ctx:
        x, xT, sg, ident, half_neg = m.x, m.xT, m.sg, m.ident, m.half_neg

        def sb(name, shape, dt=F32):
            return ctx.enter_context(nc.sbuf_tensor(name, shape, dt))

        def psum(name, shape, dt=F32):
            return ctx.enter_context(nc.psum_tensor(name, shape, dt))

        def sem(name):
            return ctx.enter_context(nc.semaphore(name))

        def at_least(eng, s, n):
            if n > 0:
                eng.wait_ge(s, n)

        w_nat = sb("w_nat", [P, 3, P])
        wT = sb("wT", [P, 3 * P])
        ident_b = sb("ident_b", [P, P], BF16)
        causal = sb("causal", [P, 4, P], BF16)
        in_T = sb("in_T", [P, 2, T])
        stacks = sb("stacks", [P, 2, 2, TT, NH, 64], BF16)
        rest = sb("rest", [P, TT, 2 * P])
        rest_b = sb("rest_b", [P, TT, 2 * P], BF16)
        kT = sb("kT", [P, 2, PAIRS, T], BF16)
        qT = sb("qT", [P, 2, 2, PAIRS, T], BF16)
        vaug = sb("vaug", [P, VB, TT, NH, VW])
        mx = sb("mx", [P, TT, 2, PAIRS])
        nmr = sb("nmr", [P, TT, 2, PAIRS])
        nm = sb("nm", [P, TT, 2, 3, PAIRS], BF16)
        nmT = sb("nmT", [2 * 3 * PAIRS, T], BF16)
        probs = sb("probs", [P, 2, 6, 512])
        oT = sb("oT", [P, 2, 2, 2, T])
        rden = sb("rden", [P, NH])
        attn = sb("attn", [P, TT, 2, PAIRS, HD])
        bst = sb("bst", [P, TT, 6])
        mv = sb("mv", [P, TT, 2])
        rstd = sb("rstd", [P, TT])
        shift = sb("shift", [P, TT])
        rb0 = sb("rb0", [P, E0])
        r0w = sb("r0w", [P, 2, E0])
        lg = sb("lg", [P, TT, E0])
        lgm = sb("lgm", [P, TT])

        misc = [psum(f"misc{i}", [P, 512]) for i in range(2)]
        abank = [psum(f"abank{i}", [P, 512]) for i in range(2)]
        bbank = [psum(f"bbank{i}", [P, 512]) for i in range(3)]
        obank = psum("obank", [P, 512])

        ld_w = sem("ld_w")
        ld_x = [sem(f"ld_x{b}") for b in range(NB)]
        consts = sem("consts")
        wT_ps, wT_sb = sem("wT_ps"), sem("wT_sb")
        inT_ps, inT_sb = sem("inT_ps"), sem("inT_sb")
        qkv_ps, part_a, part_r, part_b, parts = sem("qkv_ps"), sem("part_a"), sem("part_r"), sem("part_b"), sem("parts")
        fill_ps, k_sb, q_sb = sem("fill_ps"), sem("k_sb"), sem("q_sb")
        a_ps, a_max = sem("a_ps"), sem("a_max")
        nm_tok, nmT_ps, nmT_sb, nm_rows = sem("nm_tok"), sem("nmT_ps"), sem("nmT_sb"), sem("nm_rows")
        b_ps, b_exp, b_cut, pv_ps, o_sb = sem("b_ps"), sem("b_exp"), sem("b_cut"), sem("pv_ps"), sem("o_sb")
        ot_ps = sem("ot_ps")
        ln_mv, ln_rs, ln_x = sem("ln_mv"), sem("ln_rs"), sem("ln_x")
        xT_ps, xT_sb = sem("xT_ps"), sem("xT_sb")
        lg_ps, lg_in, lg_sub, lg_exp, s_tok = sem("lg_ps"), sem("lg_in"), sem("lg_sub"), sem("lg_exp"), sem("s_tok")
        o_div, added, filled = sem("o_div"), sem("added"), sem("filled")
        v_fixed, q_zero = sem("v_fixed"), sem("q_zero")
        dve_c, act_c, pool_c = sem("dve_c"), sem("act_c"), sem("pool_c")
        ld_later, masks = sem("ld_later"), sem("masks")

        def uses(s):
            return [0 <= s + ahead[n] < NB for n in range(MISC)]

        NMT, QKV0, QKV1, FILL2, FILL3, XT, LG, OT0, OT1, FILL0, FILL1, INT = range(MISC)
        ahead = {NMT: -1, QKV0: 1, QKV1: 1, FILL2: 0, FILL3: 0, XT: -3, LG: -3, OT0: -2, OT1: -2, FILL0: 1,
                 FILL1: 1, INT: 2}
        fills = [FILL0, FILL1, FILL2, FILL3]
        emptied = {NMT: (nmT_sb, 1, 1), OT0: (o_div, 2, 1), OT1: (o_div, 2, 2), INT: (inT_sb, 1, 1),
                   QKV0: (part_r, 2, 1), QKV1: (part_r, 2, 2), XT: (xT_sb, 1, 1),
                   LG: (lg_in, 1, 1), FILL0: (q_sb, 8, 2), FILL1: (q_sb, 8, 4),
                   FILL2: (q_sb, 8, 6), FILL3: (q_sb, 8, 8)}

        def chunk(k):
            u, c = divmod(k, 6)
            js = range(4) if c < 2 else (range(0, 2) if c < 4 else range(2, 4))
            return u, c, c % 2, [4 * u + j for j in js]

        def fill_view(b, f):
            return misc[fills[f] % 2][:, :].bitcast(BF16).rearrange("p (a r t) -> p a r t", a=2, r=2)

        block = ctx.enter_context(nc.Block())

        @block.sync
        def _(sp):
            sp.dma_start(x[:, 0:TT, :], x_in[0].rearrange("(n p) c -> p n c", p=P)).then_inc(ld_x[0], 16)
            for i, w in enumerate((Wq, Wk, Wv)):
                sp.dma_start(w_nat[:, i, :], w[:, 0:HD, 0:HC]).then_inc(ld_w, 16)
            sp.dma_start(r0w[:, :, :], r0_w.rearrange("(k p) e -> p k e", p=P)).then_inc(ld_w, 16)
            sp.dma_start(rb0[:, :], r0_b.partition_broadcast(P)).then_inc(ld_w, 16)
            for b in range(1, NB):
                sp.dma_start(x[:, TT * b:TT * (b + 1), :],
                             x_in[b].rearrange("(n p) c -> p n c", p=P)).then_inc(ld_x[b], 16)
            later = [(m.e0w[:, :, :], e0_w.rearrange("(k p) c -> p k c", p=P)), (m.e0b[:, :], e0_b.partition_broadcast(P)),
                     (m.w1_nat[:, :, :], W1.rearrange("(n p) c -> p n c", p=P)),
                     (m.b1[:, :], b1.rearrange("(n p) -> p n", p=P)),
                     (m.rms[:, :], rms_w.rearrange("(k p) -> p k", p=P)),
                     (m.r1w[:, :, :], r1_w.rearrange("(k p) e -> p k e", p=P)),
                     (m.w[:, 0, 0], sw_gate.rearrange("(k p) f -> p k f", p=P)),
                     (m.w[:, 1, 0], sw_up.rearrange("(k p) f -> p k f", p=P)), (m.w[:, 2, 0], sw_down.rearrange("f (k d) -> f k d", k=2)),
                     (m.w[:, 0, 1:], w_gate.rearrange("e (k p) f -> p e k f", p=P)),
                     (m.w[:, 1, 1:], w_up.rearrange("e (k p) f -> p e k f", p=P)),
                     (m.w[:, 2, 1:], w_down.rearrange("e f (k d) -> f e k d", k=2))]
            for dst, src in later:
                sp.dma_start(dst, src, allow_slow_non_contiguous=True).then_inc(ld_later, 16)
            for b in range(NB):
                sp.wait_ge(nmT_sb, b + 1)
                for par in range(2):
                    sp.dma_start(qT[64 * par + KS:64 * par + KM, b % 2, par, :, :],
                                 nmT[24 * par:24 * par + 24, :]
                                 ).then_inc(nm_rows, 16)
            sp.wait_ge(ld_later, 16 * len(later))

        N_LDW = 16 * (3 + 2)

        @block.gpsimd
        def _(pool):
            pool.memset(ident[:, :], 0.0).then_inc(pool_c, 1)
            pool.memset(ident_b[:, :], 0.0).then_inc(pool_c, 1)
            pool.memset(causal[:, :, :], 0.0).then_inc(pool_c, 1)
            pool.memset(half_neg[:, :], -0.5).then_inc(pool_c, 1)
            pool.wait_ge(pool_c, 4)
            for one in (ident, ident_b):
                pool.affine_select(out=one[:, :], in_=one[:, :], compare_op=ALU.not_equal, fill=1.0, base=0,
                                   pattern=[[-1, P]], channel_multiplier=1).then_inc(consts, 1)
            pool.affine_select(out=causal[:, :, :], in_=causal[:, :, :], compare_op=ALU.is_ge, fill=NEG, base=0,
                               pattern=[[0, 4], [-1, P]], channel_multiplier=1).then_inc(consts, 1)

            beside = vaug[:, :, :, :, HD:].rearrange("p b t h d -> p (b t h) d")
            pool.memset(beside, 0.0).then_inc(v_fixed, 1)
            pool.wait_ge(v_fixed, 1)
            pool.memset(beside[:, :, 0:1], 1.0).then_inc(v_fixed, 1)
            for par in range(2):
                other = slice(64 - 64 * par, P - 64 * par)
                pool.wait_ge(*((v_fixed, 2) if par == 0 else (q_zero, 1)))
                pool.memset(qT[other, :, par, :, :].bitcast(F32), 0.0).then_inc(q_zero, 1)
            pool.wait_ge(q_zero, 2)

            pool.memset(m.ones[:, :], 1.0).then_inc(pool_c, 1)
            pool.memset(m.same[:, 0, :], 0.0).then_inc(masks, 1)
            for c in range(NB):
                pool.wait_ge(masks, c + 1)
                pool.affine_select(out=m.same[:, 0, :], in_=m.same[:, 0, :], compare_op=ALU.not_equal, fill=1.0,
                                   base=-E0 * c, pattern=[[-1, E0]], channel_multiplier=1).then_inc(masks, 1)
            pool.wait_ge(masks, NB + 1)
            pool.tensor_copy(m.same[:, 1:, :], m.same[:, 0:1, :].to_broadcast([P, NB - 1, E0])).then_inc(masks, 1)
            pool.wait_ge(masks, NB + 2)
            pool.affine_select(out=m.before[:, :, :], in_=m.same[:, :, :], compare_op=ALU.is_gt, fill=0.0, base=0,
                               pattern=[[E0, NB], [0, E0]], channel_multiplier=-1).then_inc(masks, 1)

            def cut(b, u, lo, hi):
                pool.wait_ge(b_exp, 12 * b + 6 * u + hi)
                w = P if lo == 0 else T
                part = probs[:, u, lo:hi, :].rearrange("p c (h t) -> p (c h) t", t=w)[:, :, 0:P]
                pool.affine_select(out=part, in_=part, compare_op=ALU.is_ge, fill=0.0, base=0,
                                   pattern=[[0, 8], [1, P]], channel_multiplier=-1).then_inc(b_cut, 1)

            def add_attn(b):
                for t in range(TT):
                    pool.wait_ge(o_div, TT * b + t + 1)
                    xv = x[:, TT * b + t, 0:HC].rearrange("p (r a d) -> p a r d", a=2, d=HD)
                    pool.tensor_tensor(xv, xv, attn[:, t, :, :, :], ALU.add).then_inc(added, 1)

            def scales(b):
                pool.wait_ge(ln_mv, b + 1)
                at_least(pool, ln_x, TT * b)
                pool.tensor_tensor(rstd[:, :], mv[:, :, 1], half_neg[:, 0:TT], ALU.pow).then_inc(ln_rs, 1)
                pool.wait_ge(ln_rs, 2 * b + 1)
                pool.tensor_tensor(shift[:, :], mv[:, :, 0], rstd[:, :], ALU.mult).then_inc(ln_rs, 1)

            for s in range(-2, NB + 3):
                cur, prev = 0 <= s - 1 < NB, 0 <= s - 2 < NB
                if 0 <= s - 3 < NB:
                    scales(s - 3)
                if prev:
                    cut(s - 2, 1, 2, 6)
                if cur:
                    cut(s - 1, 0, 0, 2)
                    cut(s - 1, 0, 2, 6)
                if prev:
                    add_attn(s - 2)
                if cur:
                    cut(s - 1, 1, 0, 2)
        N_CONST = 3

        @block.scalar
        def _(act):
            act.wait_ge(wT_ps, 1)
            act.copy(wT[:, :], misc[0][:, 0:3 * P]).then_inc(wT_sb, 1)

            def nmT_out(b):
                act.wait_ge(nmT_ps, b + 1)
                at_least(act, nm_rows, 32 * b)
                act.copy(nmT[:, :], misc[NMT % 2][:, :].bitcast(BF16)[0:48, 0:T]).then_inc(nmT_sb, 1)

            def inT_out(b):
                act.wait_ge(inT_ps, b + 1)
                act.copy(in_T[:, b % 2, :], misc[INT % 2][:, 0:T]).then_inc(inT_sb, 1)

            def qkv_out(b, t):
                act.wait_ge(qkv_ps, TT * b + t + 1)
                bank = misc[(QKV0 + t) % 2]
                if b == 0 and t == 0:
                    act.wait_ge(v_fixed, 2)
                    act.wait_ge(filled, 3)
                if b >= VB and t == 0:
                    act.wait_ge(pv_ps, 2 * (b - VB + 1))
                act.copy(vaug[:, b % VB, t, :, 0:HD],
                         bank[:, 2 * P:3 * P].rearrange("p (h d) -> p h d", d=HD)).then_inc(act_c, 1)
                if b >= 2 and t == 0:
                    act.wait_ge(fill_ps, 4 * (b - 1))
                act.copy(stacks[:, b % 2, :, t, :, 0:HD],
                         bank[:, 0:2 * P].rearrange("p (a h d) -> p a h d", a=2, d=HD)).then_inc(part_a, 1)

            def exps(b, k):
                n = 12 * b + k
                u = k // 6
                act.wait_ge(b_ps, n + 1)
                if k % 6 == 0:
                    at_least(act, pv_ps, 2 * b + u - 1)
                act.activation(probs[:, u, k % 6, :], bbank[n % 3][:, :], ACT.Exp, scale=SCALE).then_inc(b_exp, 1)

            def o_out(b, u):
                act.wait_ge(pv_ps, 2 * b + u + 1)
                if u == 0:
                    at_least(act, ot_ps, TT * (b - 1))
                act.copy(oT[:, b % 2, u, :, :], obank[:, :].rearrange("p (a t) -> p a t", a=2)).then_inc(o_sb, 1)

            def xT_out(b):
                act.wait_ge(xT_ps, b + 1)
                act.copy(xT[:, :, b * T:(b + 1) * T],
                         misc[XT % 2][:, :].rearrange("p (k t) -> p k t", k=2)).then_inc(xT_sb, 1)

            def fill_out(b, f):
                act.wait_ge(fill_ps, 4 * b + f + 1)
                if b >= 2:
                    act.wait_ge(b_ps, 12 * (b - 2) + 6 * (f // 2) + 6)
                act.copy(kT[:, b % 2, 2 * f:2 * f + 2, :], fill_view(b, f)[:, 1]).then_inc(k_sb, 1)

            def normalise(b):
                act.wait_ge(ln_rs, 2 * b + 2)
                for t in range(TT):
                    xv = x[:, TT * b + t, :]
                    act.activation(xv, xv, ACT.Identity, bias=shift[:, t:t + 1], scale=rstd[:, t:t + 1]
                                   ).then_inc(ln_x, 1)

            def lg_out(b):
                act.wait_ge(lg_sub, b + 1)
                act.activation(sg[:, TT * b:TT * (b + 1), :], lg[:, :, :], ACT.Exp).then_inc(lg_exp, 1)

            for s in range(-2, NB + 3):
                def has(n):
                    return uses(s)[n]
                for k in range(12):
                    if k == NMT_SLOT and has(NMT):
                        nmT_out(s - 1)
                    if k in (1, 2) and has(QKV0):
                        qkv_out(s + 1, k - 1)
                    if k in (3, 4) and has(FILL2):
                        fill_out(s, k - 1)
                    if k == XT_SLOT and has(XT):
                        xT_out(s - 3)
                    if k in FILL_SLOTS and has(FILL0):
                        fill_out(s + 1, FILL_SLOTS.index(k))
                    elif k == 11 and has(INT):
                        inT_out(s + 2)
                    b, kb = (s - 2, k + 12 - LAG) if k < LAG else (s - 1, k - LAG)
                    if 0 <= b < NB:
                        exps(b, kb)
                    if k == NORM_SLOT and has(XT):
                        normalise(s - 3)
                    if k == V1_SLOTS[1] and has(OT0):
                        o_out(s - 2, 1)
                    if k == 11 and has(NMT):
                        o_out(s - 1, 0)
                    if k == SOFT_SLOT + 1 and has(LG):
                        lg_out(s - 3)

        @block.vector
        def _(dve):
            ticks = [0]

            def tick(ins):
                ticks[0] += 1
                ins.then_inc(dve_c, 1)
                return ticks[0]

            below = stacks[:, :, :, :, :, KS:].rearrange("p b a t h d -> p (b a t h) d")
            dve.memset(below, 0.0).then_inc(filled, 1)
            dve.wait_ge(filled, 1)
            for i in range(2):
                dve.memset(stacks[:, i, 1, :, :, KS:KM].rearrange("p t h d -> p (t h) d"), 1.0).then_inc(filled, 1)

            def maxima(b, k):
                n = 12 * b + k
                u, c, par, pairs = chunk(k)
                t = 0 if c < 2 else 1
                dve.wait_ge(a_ps, n + 1)
                if k == 0:
                    at_least(dve, nm_tok, b)
                dve.tensor_reduce(mx[:, t, par, pairs[0]:pairs[-1] + 1],
                                  abank[n % 2][:, :].rearrange("p (h s) -> p h s", h=len(pairs)), AX.X,
                                  ALU.max).then_inc(a_max, 1)

            def neg_max(b):
                dve.wait_ge(a_max, 12 * (b + 1))
                at_least(dve, nmT_ps, b)
                v = tick(dve.tensor_scalar(nm[:, :, :, 0, :], mx[:, :, :, :], -1.0, None, ALU.mult))
                for i in range(2):
                    dve.wait_ge(dve_c, v)
                    src = mx if i == 0 else nmr
                    v = tick(dve.scalar_tensor_tensor(
                        nmr[:, :, :, :].rearrange("p t a r -> p (t a) r"),
                        src[:, :, :, :].rearrange("p t a r -> p (t a) r"), -1.0 if i == 0 else 1.0,
                        nm[:, :, :, i, :].rearrange("p t a r -> p (t a) r"), ALU.mult, ALU.subtract))
                    dve.wait_ge(dve_c, v)
                    w = dve.tensor_copy(nm[:, :, :, i + 1, :], nmr[:, :, :, :])
                    if i == 0:
                        v = tick(w)
                    else:
                        w.then_inc(nm_tok, 1)

            def qk_rest(b, t):
                dve.wait_ge(part_a, TT * b + t + 1)
                at_least(dve, parts, TT * (b - 1) + t + 1)
                dve.tensor_tensor(rest[:, t, :].rearrange("p (a h d) -> p a h d", a=2, d=HD),
                                  misc[(QKV0 + t) % 2][:, 0:2 * P].rearrange("p (a h d) -> p a h d", a=2, d=HD),
                                  stacks[:, b % 2, :, t, :, 0:HD], ALU.subtract).then_inc(part_r, 1)

            def qk_parts(b, t):
                stack = stacks[:, b % 2]
                q, k = stack[:, 0, t, :, :], stack[:, 1, t, :, :]
                first = stack[:, :, t, :, 0:HD]
                dve.wait_ge(part_r, TT * b + t + 1)
                dve.tensor_copy(rest_b[:, t, :], rest[:, t, :]).then_inc(part_b, 1)
                dve.tensor_copy(q[:, :, HD:3 * HD].rearrange("p h (i d) -> p h i d", i=2),
                                     first[:, 0].unsqueeze(2).to_broadcast([P, NH, 2, HD]))
                dve.tensor_copy(k[:, :, 3 * HD:4 * HD], first[:, 1])
                dve.tensor_copy(k[:, :, 5 * HD:6 * HD], first[:, 1])
                dve.wait_ge(part_b, TT * b + t + 1)
                sec = rest_b[:, t, :].rearrange("p (a h d) -> p a h d", a=2, d=HD)
                rst = rest[:, t, :].rearrange("p (a h d) -> p a h d", a=2, d=HD)
                dve.tensor_copy(stack[:, :, t, :, 4 * HD:5 * HD], sec)
                dve.tensor_copy(q[:, :, 3 * HD:4 * HD], sec[:, 0])
                dve.tensor_copy(k[:, :, HD:2 * HD], sec[:, 1])
                dve.tensor_tensor(q[:, :, 5 * HD:6 * HD], rst[:, 0], sec[:, 0], ALU.subtract)
                dve.tensor_tensor(k[:, :, 2 * HD:3 * HD], rst[:, 1], sec[:, 1], ALU.subtract).then_inc(parts, 1)

            def fill_out(b, f):
                dve.wait_ge(fill_ps, 4 * b + f + 1)
                if b >= 2:
                    dve.wait_ge(b_ps, 12 * (b - 2) + 6 * (f // 2) + 6)
                for par in range(2):
                    rows = slice(64 * par, 64 * par + 64)
                    dve.wait_ge(k_sb, 4 * b + f + 1)
                    dve.tensor_copy(qT[rows, b % 2, par, 2 * f:2 * f + 2, :], fill_view(b, f)[rows, 0]
                                    ).then_inc(q_sb, 1)

            def residual(b, t):
                tile = TT * b + t
                o = misc[(OT0 + t) % 2][:, :].rearrange("p (g w) -> p g w", w=VW)
                dve.wait_ge(ot_ps, tile + 1)
                at_least(dve, o_div, tile)
                v = tick(dve.reciprocal(rden[:, :], o[:, :, HD]))
                dve.wait_ge(dve_c, v)
                at_least(dve, added, tile - 1)
                dve.tensor_tensor(attn[:, t, :, :, :].rearrange("p a r d -> p (a r) d"), o[:, :, 0:HD],
                                  rden[:, :].unsqueeze(2).to_broadcast([P, NH, HD]), ALU.mult
                                  ).then_inc(o_div, 1)

            def statistics(b):
                for t in range(TT):
                    dve.wait_ge(added, TT * b + t + 1)
                    v = tick(dve.bn_stats(bst[:, t, :], x[:, TT * b + t, :]))
                at_least(dve, ln_x, TT * b)
                for t in range(TT):
                    dve.wait_ge(dve_c, v)
                    v = tick(dve.bn_aggr(mv[:, t, :], bst[:, t, :]))
                dve.wait_ge(dve_c, v)
                tick(dve.tensor_scalar(mv[:, :, 0], mv[:, :, 0], -1.0, None, ALU.mult))
                dve.tensor_scalar(mv[:, :, 1], mv[:, :, 1], LN_EPS, None, ALU.add).then_inc(ln_mv, 1)

            def softmax_a(b):
                dve.wait_ge(lg_ps, b + 1)
                at_least(dve, lg_exp, b)
                dve.tensor_tensor(lg[:, :, :], misc[LG % 2][:, 0:TT * E0].rearrange("p (t e) -> p t e", e=E0),
                                  rb0[:, :].unsqueeze(1).to_broadcast([P, TT, E0]), ALU.add
                                  ).then_inc(lg_in, 1)
                dve.wait_ge(lg_in, b + 1)
                v = tick(dve.tensor_reduce(lgm[:, :], lg[:, :, :], AX.X, ALU.max))
                dve.wait_ge(dve_c, v)
                dve.tensor_tensor(lg[:, :, :], lg[:, :, :], lgm[:, :].unsqueeze(2).to_broadcast([P, TT, E0]),
                                  ALU.subtract).then_inc(lg_sub, 1)

            def softmax_b(b):
                dve.wait_ge(lg_exp, b + 1)
                sv = sg[:, TT * b:TT * (b + 1), :]
                v = tick(dve.tensor_reduce(lgm[:, :], sv, AX.X, ALU.add))
                dve.wait_ge(dve_c, v)
                v = tick(dve.reciprocal(lgm[:, :], lgm[:, :]))
                dve.wait_ge(dve_c, v)
                dve.tensor_tensor(sv, sv, lgm[:, :].unsqueeze(2).to_broadcast([P, TT, E0]), ALU.mult
                                  ).then_inc(s_tok, 1)

            for s in range(-2, NB + 3):
                def has(n):
                    return uses(s)[n]
                for k in range(12):
                    if k == 0 and has(NMT):
                        neg_max(s - 1)
                    if k in (4, 5) and has(FILL2):
                        fill_out(s, k - 2)
                    if k - Q_LATE in FILL_SLOTS and has(FILL0):
                        fill_out(s + 1, FILL_SLOTS.index(k - Q_LATE))
                    if k == SOFT_SLOT and has(LG):
                        softmax_a(s - 3)
                    if 0 <= s < NB:
                        maxima(s, k)
                    if k in REST_SLOTS and has(QKV0):
                        qk_rest(s + 1, REST_SLOTS.index(k))
                    if k in PART_SLOTS and has(QKV0):
                        qk_parts(s + 1, PART_SLOTS.index(k))
                    if k in RES_SLOTS and has(OT0):
                        residual(s - 2, RES_SLOTS.index(k))
                    if k == SOFTB_SLOT and has(LG):
                        softmax_b(s - 3)
                    if k == STAT_SLOT and has(XT):
                        statistics(s - 3)

        @block.tensor
        def _(pe):
            pe.wait_ge(consts, N_CONST)
            pe.wait_ge(ld_w, N_LDW)
            for i in range(3):
                mm = pe.transpose(misc[0][:, i * P:(i + 1) * P], w_nat[:, i, :], ident[:, :])
            mm.then_inc(wT_ps, 1)
            pe.wait_ge(wT_sb, 1)

            def scores_a(b, k):
                n = 12 * b + k
                u, c, par, pairs = chunk(k)
                bank = abank[n % 2]
                if n == 0:
                    pe.wait_ge(q_zero, 2)
                if c == 0:
                    pe.wait_ge(k_sb, 4 * b + 2 * u + 2)
                    pe.wait_ge(q_sb, 8 * b + 4 * u + 4)
                at_least(pe, a_max, n - 1)
                w = P if c < 2 else T
                t = 0 if c < 2 else 1
                pe.matmul(bank[:, :].rearrange("p (h s) -> p h s", h=len(pairs))[:, :, w - P:w], ident_b[:, :],
                          causal[:, 0:len(pairs), :], start=True, stop=False, skip_group_check=True)
                for j, pair in enumerate(pairs):
                    mm = pe.matmul(bank[:, j * w:(j + 1) * w], qT[:, b % 2, par, pair, t * P:(t + 1) * P],
                                   kT[:, b % 2, pair, 0:w], start=False, stop=True, skip_group_check=True)
                mm.then_inc(a_ps, 1)

            def scores_b(b, k):
                n = 12 * b + k
                u, c, par, pairs = chunk(k)
                bank = bbank[n % 3]
                if k == 0:
                    pe.wait_ge(nm_rows, 32 * (b + 1))
                at_least(pe, b_exp, n - 2)
                w, t0, s0 = (P, P, P) if c < 2 else (T, 0, 0)
                for j, pair in enumerate(pairs):
                    mm = pe.matmul(bank[:, j * w:(j + 1) * w], kT[:, b % 2, pair, s0:s0 + P],
                                   qT[:, b % 2, par, pair, t0:T], start=True, stop=True)
                mm.then_inc(b_ps, 1)

            def values(b, u, par):
                if par == 0:
                    pe.wait_ge(b_cut, 4 * b + 2 * u + 2)
                    at_least(pe, o_sb, 2 * b + u)
                for j in range(4):
                    h = 8 * u + 2 * j + par
                    pe.matmul(obank[32 * j:32 * j + 32, par * T:(par + 1) * T], vaug[:, b % VB, 0, h, :],
                              probs[:, u, 2 + 2 * (j // 2) + par, (j % 2) * T:(j % 2 + 1) * T],
                              start=True, stop=False)
                for j in range(4):
                    h = 8 * u + 2 * j + par
                    mm = pe.matmul(obank[32 * j:32 * j + 32, par * T + P:(par + 1) * T], vaug[:, b % VB, 1, h, :],
                                   probs[:, u, par, j * P:(j + 1) * P], start=False, stop=True)
                if par == 1:
                    mm.then_inc(pv_ps, 1)

            def free_bank(s, n):
                if (s, n) in ((-2, INT), (-1, QKV1)):
                    return pe.wait_ge(wT_sb, 1)
                a, m = max((a, m) for a in (s - 1, s) for m in range(n % 2, MISC, 2) if uses(a)[m] and (a, m) < (s, n))
                read, per_sequence, nth = emptied[m]
                pe.wait_ge(read, per_sequence * (a + ahead[m]) + nth)

            def nm_rows_T(b):
                free_bank(b - ahead[NMT], NMT)
                pe.wait_ge(nm_tok, b + 1)
                for t in range(TT):
                    mm = pe.transpose(misc[NMT % 2][:, :].bitcast(BF16)[0:48, t * P:(t + 1) * P],
                                      nm[:, t, :, :, :].rearrange("p a i r -> p (a i r)"), ident_b[:, :])
                mm.then_inc(nmT_ps, 1)

            def o_T(b, t):
                free_bank(b - ahead[OT0], OT0 + t)
                if t == 0:
                    pe.wait_ge(o_sb, 2 * (b + 1))
                for par in range(2):
                    for u in range(2):
                        g = par * 2 + u
                        mm = pe.transpose(misc[(OT0 + t) % 2][:, g * P:(g + 1) * P],
                                          oT[:, b % 2, u, par, t * P:(t + 1) * P], ident[:, :])
                mm.then_inc(ot_ps, 1)

            def in_tr(b):
                free_bank(b - ahead[INT], INT)
                pe.wait_ge(ld_x[b], 16)
                for t in range(TT):
                    mm = pe.transpose(misc[INT % 2][:, t * P:(t + 1) * P], x[:, TT * b + t, 0:HC], ident[:, :])
                mm.then_inc(inT_ps, 1)

            def qkv(b, t):
                free_bank(b - ahead[QKV0], QKV0 + t)
                pe.wait_ge(inT_sb, b + 1)
                pe.matmul(misc[(QKV0 + t) % 2][:, 0:3 * P], in_T[:, b % 2, t * P:(t + 1) * P], wT[:, :],
                          start=True, stop=True).then_inc(qkv_ps, 1)

            def fill(b, f):
                free_bank(b - ahead[fills[f]], fills[f])
                pe.wait_ge(parts, TT * (b + 1))
                view = misc[fills[f] % 2][:, :].bitcast(BF16).rearrange("p (a r t n) -> p a r t n", a=2, r=2, t=TT)
                for a in range(2):
                    for r in range(2):
                        for t in range(TT):
                            pair = 2 * f + r
                            mm = pe.transpose(view[:, a, r, t, :],
                                              stacks[:, b % 2, a, t, 2 * pair:2 * pair + 2, :].rearrange("p h d -> p (h d)"),
                                              ident_b[:, :])
                mm.then_inc(fill_ps, 1)

            def x_T(b):
                free_bank(b - ahead[XT], XT)
                pe.wait_ge(ln_x, TT * (b + 1))
                for k in range(2):
                    for t in range(TT):
                        mm = pe.transpose(misc[XT % 2][:, (k * TT + t) * P:(k * TT + t + 1) * P],
                                          x[:, TT * b + t, k * P:(k + 1) * P], ident[:, :])
                mm.then_inc(xT_ps, 1)

            def logits(b):
                free_bank(b - ahead[LG], LG)
                pe.wait_ge(xT_sb, b + 1)
                for t in range(TT):
                    for k in range(2):
                        mm = pe.matmul(misc[LG % 2][:, t * E0:(t + 1) * E0],
                                       xT[:, k, (TT * b + t) * P:(TT * b + t + 1) * P], r0w[:, k, :],
                                       start=(k == 0), stop=(k == 1))
                mm.then_inc(lg_ps, 1)

            for s in range(-2, NB + 3):
                def has(n):
                    return uses(s)[n]
                for k in range(12):
                    if 0 <= s < NB:
                        scores_a(s, k)
                    if k == NMT_SLOT and has(NMT):
                        nm_rows_T(s - 1)
                    if k in (1, 2) and has(QKV0):
                        qkv(s + 1, k - 1)
                    if k in (3, 4) and has(FILL2):
                        fill(s, k - 1)
                    if k == XT_SLOT and has(XT):
                        x_T(s - 3)
                    if k == LG_SLOT and has(LG):
                        logits(s - 3)
                    if k in OT_SLOTS and has(OT0):
                        o_T(s - 2, OT_SLOTS.index(k))
                    if k in FILL_SLOTS and has(FILL0):
                        fill(s + 1, FILL_SLOTS.index(k))
                    if k == 11 and has(INT):
                        in_tr(s + 2)
                    b, kb = (s - 2, k + 12 - LAG) if k < LAG else (s - 1, k - LAG)
                    if 0 <= b < NB:
                        scores_b(b, kb)
                    if k in V1_SLOTS and has(OT0):
                        values(s - 2, 1, k - V1_SLOTS[0])
                    if k in (10, 11) and has(NMT):
                        values(s - 1, 0, k - 10)


def rest_of_layers(nc, m, out):
    with ExitStack() as ctx:
        x, xT, sg, ident, half_neg = m.x, m.xT, m.sg, m.ident, m.half_neg

        def sb(name, shape, dt=F32):
            return ctx.enter_context(nc.sbuf_tensor(name, shape, dt))

        def psum(name, shape, dt=F32):
            return ctx.enter_context(nc.psum_tensor(name, shape, dt))

        def sem(name):
            return ctx.enter_context(nc.semaphore(name))

        def at_least(eng, s, n):
            if n > 0:
                eng.wait_ge(s, n)

        w_lo = sb("w_lo", [P, 3, E1 + 1, 2, FF])
        w_hi = sb("w_hi", [P, 3, E1 + 1, 2, FF])
        r1_hi = sb("r1_hi", [P, 2, E1])
        r1_lo = sb("r1_lo", [P, 2, E1])
        prob = sb("prob", [P, 2, P])
        over = sb("over", [P, 2, P])
        tie = sb("tie", [P, 2, P])
        nth = sb("nth", [P, 2, P])
        cand = sb("cand", [P, 1], I32)
        flip = sb("flip", [P, 1], I32)
        cnt = sb("cnt", [P, 3], BF16)
        lim = sb("lim", [P, 2])
        tot = sb("tot", [P, 5])
        gsum = sb("gsum", [P, NT])
        y0 = sb("y0", [P, NT, C])
        w1T_hi = sb("w1T_hi", [P, 2, 2 * C])
        w1T_lo = sb("w1T_lo", [P, 2, 2 * C])
        x2_hi = sb("x2_hi", [P, 2, 2, QN])
        x2_lo = sb("x2_lo", [P, 2, 2, QN])
        b1h = sb("b1h", [P, 2])
        hid = y0[:, :, :].rearrange("p (q n) c -> p q (n c)", q=Q).rearrange("p q (k t) -> p q k t", k=2)
        with ExitStack() as first:
            gate = first.enter_context(nc.sbuf_tensor("gate", [P, Q, 2, QN], F32))
            val = first.enter_context(nc.sbuf_tensor("val", [P, Q, 2, QN], F32))
        hT_hi = sb("hT_hi", [P, Q, 2, QN])
        hT_lo = sb("hT_lo", [P, Q, 2, QN])
        bst = sb("bst2", [P, NT, 6])
        mv = sb("mv2", [P, NT, 2])
        rstd = sb("rstd2", [P, NT])
        shift = sb("shift2", [P, NT])
        sq = sb("sq", [P, C])
        ss = sb("ss", [P, NT])
        rr = sb("rr", [P, NT])
        xr = sb("xr", [P, QT, C])
        lg1 = sb("lg1", [P, QT, E1])
        red = sb("red", [P, QT])
        p1 = sb("p1", [P, QT, E1])
        top = sb("top", [P, QT, E1])
        w1 = sb("w1", [P, NT, E1])
        half = sb("half", [P, 2, QN])
        act_in = sb("act_in", [P, 2, QN])
        act_hi = sb("act_hi", [P, 2, QN])
        act_lo = sb("act_lo", [P, 2, QN])

        tr = [psum(f"tr{i}", [P, 512]) for i in range(2)]
        mm = [psum(f"mm{i}", [P, 512]) for i in range(4)]
        zb, gb, ub = mm[0:2], mm[2], mm[3]
        dn = [psum(f"dn{i}", [P, 512]) for i in range(2)]

        y0_ok = sem("y0_ok")
        pr_ps, pr_sb, w1_ps, w1_sb = sem("pr_ps"), sem("pr_sb"), sem("w1_ps"), sem("w1_sb")
        cand_ok, counted, totals = sem("cand_ok"), sem("counted"), sem("totals")
        y0_ps, y0_sb = sem("y0_ps"), sem("y0_sb")
        chosen, g_ps, g_sb = sem("chosen"), sem("g_ps"), sem("g_sb")
        ln_mv = [sem(f"ln{i}_mv") for i in range(3)]
        ln_rs = [sem(f"ln{i}_rs") for i in range(3)]
        rr_ok = sem("rr_ok")
        ln_dve = [sem(f"ln{i}_dve") for i in range(3)]
        ln_act = [sem(f"ln{i}_act") for i in range(3)]
        x2_ps, x2_sb = sem("x2_ps"), sem("x2_sb")
        z_ps, z_sb, g_ok, scanned, h_ps, h_add = (sem("z_ps"), sem("z_sb"), sem("g_ok"), sem("scanned"),
                                                  sem("h_ps"), sem("h_add"))
        sq_ok, ms_ok, xr_ok, xr_ps, hT_ok = sem("sq_ok"), sem("ms_ok"), sem("xr_ok"), sem("xr_ps"), sem("hT_ok")
        lg_ps, lg_sub, lg_exp, w_ok = sem("lg1_ps"), sem("lg1_sub"), sem("lg1_exp"), sem("w_ok")
        gu_ps, sil_ok, act_ok, dn_ps, dn_add = sem("gu_ps"), sem("sil_ok"), sem("act_ok"), sem("dn_ps"), sem("dn_add")
        dve_c, act_c = sem("dve_c2"), sem("act_c2")
        stored = sem("stored")
        x2_low, w1_low = sem("x2_low"), sem("w1_low")
        mul_ok, hi_ok, lo_ok = sem("mul_ok"), sem("hi_ok"), sem("lo_ok")
        whi_ok, wlo_ok, hlo_ok, r1_ok = sem("whi_ok"), sem("wlo_ok"), sem("hlo_ok"), sem("r1_ok")
        EX = E1 + 1


        def row(weights, r):
            return weights[:, r % 3, r // 3].rearrange("p k f -> p (k f)")

        (ADD, NORM, TURN, LIN0, LIN1, SCAN, HID, NORM1, RMS, SCALE1, TURN1, ROUTE0, ROUTE1) = range(13)
        STAGES = 13
        steps = []
        for t in range(FIRST_EXPERT + Q * EX + 2):
            stages = [(t - b, q) for q, b in enumerate(BEGIN) if 0 <= t - b < STAGES]
            steps.append((t - FIRST_EXPERT, stages))
        tr_uses = []
        for _, stages in steps:
            for g, q in stages:
                if g in (TURN, HID, TURN1, ROUTE0):
                    tr_uses.append((g, q))
        tr_read = {TURN: x2_low, HID: h_add, TURN1: hlo_ok}

        block = ctx.enter_context(nc.Block())

        def tr_free(pe, g, q, i):
            k = tr_uses.index((g, q))
            if k == 0:
                return pe.wait_ge(g_sb, 1)
            before = tr_uses[:k] if i == 0 else [u for u in tr_uses[:k] if u[0] != ROUTE0]
            if not before:
                return pe.wait_ge(g_sb, 1)
            pg, pq = before[-1]
            if pg == ROUTE0:
                pe.wait_ge(lg_sub, pq + 1)
            else:
                pe.wait_ge(tr_read[pg], 2 * pq + i + 1)

        def follow(emit_stage, emit_expert):
            for i, stages in steps:
                if 0 <= i <= Q * EX + 1:
                    emit_expert(i, lambda: [emit_stage(g, q) for g, q in stages])
                else:
                    for g, q in stages:
                        emit_stage(g, q)

        def normalise(eng, i, q, tiles):
            eng.wait_ge(ln_rs[i], 2 * (q + 1))
            for n in tiles:
                n += QT * q
                if eng is nc.scalar:
                    w = nc.scalar.activation(x[:, n, :], x[:, n, :], ACT.Identity, bias=shift[:, n:n + 1],
                                             scale=rstd[:, n:n + 1])
                else:
                    w = eng.tensor_scalar(x[:, n, :], x[:, n, :], rstd[:, n:n + 1], shift[:, n:n + 1], ALU.mult,
                                          ALU.add)
                w.then_inc((ln_act if eng is nc.scalar else ln_dve)[i], 1)

        def normed(eng, i, q):
            eng.wait_ge(ln_dve[i], ON_DVE * (q + 1))
            eng.wait_ge(ln_act[i], (QT - ON_DVE) * (q + 1))

        @block.sync
        def _(sp):
            for q in range(Q):
                normed(sp, 2, q)
                for h in range(2):
                    sp.dma_start(out[2 * q + h].rearrange("(n p) c -> p n c", p=P),
                                 x[:, QT * q + TT * h:QT * q + TT * (h + 1), :]).then_inc(stored, 16)
            sp.wait_ge(stored, 16 * NB)

        @block.gpsimd
        def _(pool):
            def add_bias(i):
                pool.wait_ge(y0_sb, i + 1)
                yv = y0[:, 2 * i:2 * i + 2, :]
                pool.tensor_tensor(yv, yv, m.e0b[:, :].unsqueeze(1).to_broadcast([P, 2, C]), ALU.add
                                   ).then_inc(y0_ok, 1)

            for r in range(BITS):
                if r < 3 * EX:
                    pool.wait_ge(whi_ok, r + 1)
                    pool.tensor_tensor(row(w_lo, r).bitcast(F32R), row(m.w, r), row(w_hi, r), ALU.subtract
                                       ).then_inc(wlo_ok, 1)
                for i in range(NT // 2 * r // BITS, NT // 2 * (r + 1) // BITS):
                    add_bias(i)

            def scales(i, q):
                n0, n1 = QT * q, QT * (q + 1)
                pool.wait_ge(ln_mv[i], q + 1)
                if i > 0:
                    normed(pool, i - 1, q)
                pool.tensor_tensor(rstd[:, n0:n1], mv[:, n0:n1, 1], half_neg[:, 0:QT], ALU.pow
                                   ).then_inc(ln_rs[i], 1)
                pool.wait_ge(ln_rs[i], 2 * q + 1)
                pool.tensor_tensor(shift[:, n0:n1], mv[:, n0:n1, 0], rstd[:, n0:n1], ALU.mult).then_inc(ln_rs[i], 1)

            def sigmoid(q, k):
                pool.wait_ge(z_sb, 4 * q + 2 * k + 1)
                gv = gate[:, q, k, :]
                pool.tensor_scalar(gv, gv, 0.5, 0.5, ALU.mult, ALU.add).then_inc(g_ok, 1)

            def over_rms(q):
                n0, n1 = QT * q, QT * (q + 1)
                pool.wait_ge(ms_ok, q + 1)
                pool.tensor_tensor(rr[:, n0:n1], ss[:, n0:n1], half_neg[:, 0:QT], ALU.pow).then_inc(rr_ok, 1)

            def stage(g, q):
                if g == ADD:
                    scales(0, q)
                elif g in (LIN0, LIN1):
                    sigmoid(q, g - LIN0)
                elif g == HID:
                    scales(1, q)
                elif g == RMS:
                    over_rms(q)

            def expert(i, side):
                if i < Q * EX:
                    pool.wait_ge(hi_ok, i + 1)
                    at_least(pool, dn_ps, 2 * (i - 1))
                    for h in range(2):
                        at = slice(h * QN // 2, (h + 1) * QN // 2)
                        pool.tensor_tensor(act_lo[:, i % 2, at].bitcast(F32R), act_in[:, i % 2, at], act_hi[:, i % 2, at],
                                           ALU.subtract).then_inc(lo_ok, 1)
                if i > 0 and i % EX == 0:
                    scales(2, i // EX - 1)
                side()

            follow(stage, expert)

        @block.scalar
        def _(act):
            for k in range(2):
                act.wait_ge(w1_ps, k + 1)
                act.copy(w1T_hi[:, k, :].bitcast(F32R), mm[k][:, :]).then_inc(w1_sb, 1)
            act.mul(b1h[:, :], m.b1[:, 0:2], 0.5).then_inc(act_c, 1)
            for i in range(NT // 2):
                act.wait_ge(y0_ps, i + 1)
                act.copy(y0[:, 2 * i:2 * i + 2, :], mm[i % 4][:, :].rearrange("p (n c) -> p n c", n=2)
                         ).then_inc(y0_sb, 1)
            act.wait_ge(act_c, 1)

            def x2_out(q):
                for k in range(2):
                    act.wait_ge(x2_ps, 2 * q + k + 1)
                    at_least(act, z_ps, 4 * (q - 1))
                    act.copy(x2_hi[:, q % 2, k, :].bitcast(F32R), tr[k][:, :]).then_inc(x2_sb, 1)

            def squash(q, k):
                act.wait_ge(z_ps, 4 * q + 2 * k + 1)
                act.activation(gate[:, q, k, :], zb[0][:, :], ACT.Tanh, bias=b1h[:, k:k + 1],
                               scale=0.5).then_inc(z_sb, 1)
                act.wait_ge(z_ps, 4 * q + 2 * k + 2)
                act.activation(val[:, q, k, :], zb[1][:, :], ACT.Tanh,
                               bias=m.b1[:, 2 + k:3 + k]).then_inc(z_sb, 1)

            def squares(q):
                normed(act, 1, q)
                for n in range(QT * q, QT * (q + 1)):
                    at_least(act, sq_ok, n)
                    act.activation(sq[:, :], x[:, n, :], ACT.Square, accum_out=ss[:, n:n + 1]).then_inc(sq_ok, 1)

            def hT_out(q):
                for k in range(2):
                    act.wait_ge(xr_ps, 2 * q + k + 1)
                    act.activation(hT_hi[:, q, k, :].bitcast(F32R), tr[k][:, :], ACT.Copy,
                                   scale=m.rms[:, k:k + 1]).then_inc(hT_ok, 1)

            def lg_out(q):
                act.wait_ge(lg_sub, q + 1)
                act.activation(p1[:, :, :], lg1[:, :, :], ACT.Exp).then_inc(lg_exp, 1)

            def stage(g, q):
                if g == NORM:
                    normalise(act, 0, q, range(ON_DVE, QT))
                elif g == TURN:
                    x2_out(q)
                elif g in (LIN0, LIN1):
                    squash(q, g - LIN0)
                elif g == NORM1:
                    normalise(act, 1, q, range(ON_DVE, QT))
                    squares(q)
                elif g == TURN1:
                    hT_out(q)
                elif g == ROUTE0:
                    lg_out(q)

            def expert(i, side):
                if 0 < i <= Q * EX:
                    j = i - 1
                    act.wait_ge(act_ok, j + 1)
                    at_least(act, dn_ps, 2 * (j - 1))
                    act.copy(act_hi[:, j % 2, :].bitcast(F32R), act_in[:, j % 2, :]).then_inc(hi_ok, 1)
                if i < Q * EX:
                    act.wait_ge(gu_ps, 2 * i + 1)
                    at_least(act, act_ok, i - 1)
                    act.activation(half[:, i % 2, :], gb[:, :], ACT.Tanh, scale=0.5).then_inc(sil_ok, 1)
                if i > 1 and i % EX == 1:
                    normalise(act, 2, i // EX - 1, range(ON_DVE, QT))
                side()

            follow(stage, expert)

        @block.vector
        def _(dve):
            ticks = [0]

            def tick(ins):
                ticks[0] += 1
                ins.then_inc(dve_c, 1)
                return ticks[0]

            dve.wait_ge(pr_ps, 1)
            dve.tensor_copy(prob[:, :, :], tr[0][:, 0:2 * P].rearrange("p (j t) -> p j t", j=2)).then_inc(pr_sb, 1)
            dve.memset(cand[:, :], 1 << (BITS - 1)).then_inc(cand_ok, 1)
            for k in range(2):
                dve.wait_ge(w1_sb, k + 1)
                dve.tensor_tensor(w1T_lo[:, k, :].bitcast(F32R), mm[k][:, :], w1T_hi[:, k, :], ALU.subtract
                                  ).then_inc(w1_low, 1)
            dve.wait_ge(pr_sb, 1)
            for r in range(BITS):
                bit = 1 << (BITS - 1 - r)
                dve.wait_ge(cand_ok, r + 1)
                at_least(dve, totals, r)
                dve.tensor_scalar(over[:, :, :].rearrange("p j t -> p (j t)"),
                                  prob[:, :, :].rearrange("p j t -> p (j t)"), cand[:, :].bitcast(F32), None,
                                  ALU.is_ge, ALU.add, accum_out=cnt[:, 0:1]).then_inc(counted, 1)
                if r < 3 * (E1 + 1):
                    dve.tensor_copy(row(w_hi, r).bitcast(F32R), row(m.w, r)).then_inc(whi_ok, 1)
                elif r == 3 * (E1 + 1):
                    dve.tensor_copy(r1_hi[:, :, :].bitcast(F32R), m.r1w[:, :, :]).then_inc(r1_ok, 1)
                elif r == 3 * (E1 + 1) + 1:
                    dve.wait_ge(r1_ok, 1)
                    dve.tensor_tensor(r1_lo[:, :, :].bitcast(F32R), m.r1w[:, :, :], r1_hi[:, :, :], ALU.subtract
                                      ).then_inc(r1_ok, 1)
                dve.wait_ge(totals, r + 1)
                v = tick(dve.tensor_scalar(flip[:, :], tr[1][:, r % 2:r % 2 + 1], float(TOP), float(bit), ALU.is_lt,
                                           ALU.mult))
                dve.wait_ge(dve_c, v)
                dve.scalar_tensor_tensor(cand[:, :], flip[:, :], bit >> 1, cand[:, :], ALU.bitwise_xor,
                                         ALU.bitwise_xor).then_inc(cand_ok, 1)
            dve.wait_ge(cand_ok, BITS + 1)
            dve.tensor_scalar(over[:, :, :].rearrange("p j t -> p (j t)"),
                              prob[:, :, :].rearrange("p j t -> p (j t)"), cand[:, :].bitcast(F32), None, ALU.is_gt,
                              ALU.add, accum_out=cnt[:, 0:1])
            for j in range(2):
                w = dve.tensor_scalar(tie[:, j, :], prob[:, j, :], cand[:, :].bitcast(F32), None, ALU.is_equal,
                                      ALU.add, accum_out=cnt[:, 1 + j:2 + j])
            w.then_inc(counted, 1)
            dve.wait_ge(counted, BITS + 1)
            for j in range(2):
                v = tick(dve.tensor_tensor_scan(nth[:, j, :], m.ones[:, :], tie[:, j, :], 0.0, ALU.mult, ALU.add))
            dve.wait_ge(totals, BITS + 1)
            v = tick(dve.tensor_copy(tot[:, :], tr[1][:, 2:7]))
            dve.wait_ge(dve_c, v)
            v = tick(dve.tensor_scalar(lim[:, 0:1], tot[:, 0:1], -1.0, float(TOP), ALU.mult, ALU.add))
            dve.wait_ge(dve_c, v)
            v = tick(dve.tensor_tensor(lim[:, 1:2], lim[:, 0:1], tot[:, 1:2], ALU.subtract))
            dve.wait_ge(dve_c, v)
            v = tick(dve.tensor_tensor(lim[:, :], lim[:, :], tot[:, 3:5], ALU.subtract))
            dve.wait_ge(dve_c, v)
            for j in range(2):
                v = tick(dve.scalar_tensor_tensor(tie[:, j, :], nth[:, j, :], lim[:, j:j + 1], tie[:, j, :],
                                                  ALU.is_le, ALU.mult))
            dve.wait_ge(dve_c, v)
            v = tick(dve.tensor_tensor(over[:, :, :], over[:, :, :], tie[:, :, :], ALU.add))
            dve.wait_ge(dve_c, v)
            dve.tensor_tensor(over[:, :, :], over[:, :, :], prob[:, :, :], ALU.mult).then_inc(chosen, 1)
            dve.wait_ge(g_ps, 1)
            dve.tensor_reduce(gsum[:, :].rearrange("p (j c) -> p j c", j=2),
                              tr[0][:, 0:2 * P].rearrange("p (j c e) -> p j c e", j=2, e=E0), AX.X, ALU.add
                              ).then_inc(g_sb, 1)
            dve.wait_ge(g_sb, 1)

            def statistics(i, q):
                n0, n1 = QT * q, QT * (q + 1)
                for n in range(n0, n1):
                    v = tick(dve.bn_stats(bst[:, n, :], x[:, n, :]))
                dve.wait_ge(dve_c, v)
                for n in range(n0, n1):
                    v = tick(dve.bn_aggr(mv[:, n, :], bst[:, n, :]))
                dve.wait_ge(dve_c, v)
                tick(dve.tensor_scalar(mv[:, n0:n1, 0], mv[:, n0:n1, 0], -1.0, None, ALU.mult))
                dve.tensor_scalar(mv[:, n0:n1, 1], mv[:, n0:n1, 1], LN_EPS, None, ALU.add).then_inc(ln_mv[i], 1)

            def add_experts(q):
                dve.wait_ge(y0_ok, QT // 2 * (q + 1))
                for n in range(QT * q, QT * (q + 1)):
                    v = tick(dve.scalar_tensor_tensor(x[:, n, :], y0[:, n, :], gsum[:, n:n + 1], x[:, n, :],
                                                      ALU.mult, ALU.add))
                dve.wait_ge(dve_c, v)
                statistics(0, q)

            def recur(q):
                for k in range(2):
                    dve.wait_ge(g_ok, 2 * q + k + 1)
                    dve.wait_ge(z_sb, 4 * q + 2 * k + 2)
                    for h in range(2):
                        at = slice(T * h, T * (h + 1))
                        w = dve.tensor_tensor_scan(hid[:, q, k, at], gate[:, q, k, at], val[:, q, k, at], 0.0,
                                                   ALU.mult, ALU.add)
                    w.then_inc(scanned, 1)

            def add_hidden(q):
                for i in range(2):
                    dve.wait_ge(h_ps, 2 * q + i + 1)
                    xv = x[:, QT * q + 2 * i:QT * q + 2 * i + 2, :]
                    dve.tensor_tensor(xv, xv, tr[i][:, :].rearrange("p (n c) -> p n c", n=2), ALU.add
                                      ).then_inc(h_add, 1)
                dve.wait_ge(h_add, 2 * (q + 1))
                statistics(1, q)

            def mean_square(q):
                n0, n1 = QT * q, QT * (q + 1)
                dve.wait_ge(sq_ok, n1)
                dve.tensor_scalar(ss[:, n0:n1], ss[:, n0:n1], 1.0 / C, RMS_EPS, ALU.mult, ALU.add).then_inc(ms_ok, 1)

            def over_rms(q):
                dve.wait_ge(rr_ok, q + 1)
                at_least(dve, xr_ps, 2 * q)
                for t in range(QT):
                    n = QT * q + t
                    dve.tensor_scalar(xr[:, t, :], x[:, n, :], rr[:, n:n + 1], None, ALU.mult).then_inc(xr_ok, 1)

            def h_low(q):
                for k in range(2):
                    dve.wait_ge(hT_ok, 2 * q + k + 1)
                    dve.scalar_tensor_tensor(hT_lo[:, q, k, :].bitcast(F32R), tr[k][:, :], m.rms[:, k:k + 1],
                                             hT_hi[:, q, k, :], ALU.mult, ALU.subtract).then_inc(hlo_ok, 1)

            wide = [P, QT, E1]

            def route_in(q):
                dve.wait_ge(lg_ps, q + 1)
                at_least(dve, w_ok, q)
                z = tr[0][:, 0:QT * E1].rearrange("p (n e) -> p n e", e=E1)
                v = tick(dve.tensor_reduce(red[:, :], z, AX.X, ALU.max))
                dve.wait_ge(dve_c, v)
                dve.tensor_tensor(lg1[:, :, :], z, red[:, :].unsqueeze(2).to_broadcast(wide), ALU.subtract
                                  ).then_inc(lg_sub, 1)

            def route_out(q):
                dve.wait_ge(lg_exp, q + 1)
                v = tick(dve.tensor_reduce(red[:, :], p1[:, :, :], AX.X, ALU.add))
                dve.wait_ge(dve_c, v)
                v = tick(dve.reciprocal(red[:, :], red[:, :]))
                dve.wait_ge(dve_c, v)
                v = tick(dve.tensor_tensor(p1[:, :, :], p1[:, :, :], red[:, :].unsqueeze(2).to_broadcast(wide),
                                           ALU.mult))
                dve.wait_ge(dve_c, v)
                for n in range(QT):
                    v = tick(dve.max(top[:, n, :], p1[:, n, :]))
                dve.wait_ge(dve_c, v)
                v = tick(dve.tensor_tensor(red[:, :], top[:, :, 0], top[:, :, 1], ALU.add))
                v = tick(dve.memset(top[:, :, TOP1:], -1.0))
                dve.wait_ge(dve_c, v)
                v = tick(dve.reciprocal(red[:, :], red[:, :]))
                wv = w1[:, QT * q:QT * (q + 1), :]
                for n in range(QT):
                    v = tick(dve.match_replace(out=w1[:, QT * q + n, :], in_to_replace=top[:, n, :],
                                               in_values=p1[:, n, :], imm_value=0.0))
                dve.wait_ge(dve_c, v)
                v = tick(dve.tensor_tensor(wv, p1[:, :, :], wv, ALU.subtract))
                dve.wait_ge(dve_c, v)
                dve.scalar_tensor_tensor(wv, wv, 0.5, red[:, :].unsqueeze(2).to_broadcast(wide), ALU.mult, ALU.mult
                                         ).then_inc(w_ok, 1)

            def stage(g, q):
                if g == ADD:
                    add_experts(q)
                elif g == NORM:
                    normalise(dve, 0, q, range(ON_DVE))
                elif g == TURN:
                    for k in range(2):
                        dve.wait_ge(x2_sb, 2 * q + k + 1)
                        at_least(dve, z_ps, 4 * (q - 1))
                        dve.tensor_tensor(x2_lo[:, q % 2, k, :].bitcast(F32R), tr[k][:, :], x2_hi[:, q % 2, k, :],
                                          ALU.subtract).then_inc(x2_low, 1)
                elif g == SCAN:
                    recur(q)
                elif g == HID:
                    add_hidden(q)
                elif g == NORM1:
                    normalise(dve, 1, q, range(ON_DVE))
                elif g == RMS:
                    mean_square(q)
                elif g == SCALE1:
                    over_rms(q)
                elif g == TURN1:
                    h_low(q)
                elif g == ROUTE0:
                    route_in(q)
                elif g == ROUTE1:
                    route_out(q)

            def gated(i):
                h = half[:, i % 2, :]
                dve.wait_ge(sil_ok, i + 1)
                dve.scalar_tensor_tensor(h, h, 1.0, gb[:, :], ALU.add, ALU.mult).then_inc(mul_ok, 1)
                dve.wait_ge(gu_ps, 2 * (i + 1))
                dve.wait_ge(mul_ok, i + 1)
                at_least(dve, lo_ok, 2 * (i - 1))
                dve.tensor_tensor(act_in[:, i % 2, :], h, ub[:, :], ALU.mult
                                  ).then_inc(act_ok, 1)

            def add_down(i):
                q, e = divmod(i, EX)
                if e == 1:
                    dve.wait_ge(w_ok, q + 1)
                for t in range(QT):
                    n = QT * q + t
                    if t % 2 == 0:
                        dve.wait_ge(dn_ps, 2 * i + t // 2 + 1)
                    if e > 0:
                        dve.wait_ge(dn_add, QT * (i - 1) + t + 1)
                    d = dn[t // 2][:, (t % 2) * C:(t % 2 + 1) * C]
                    share = 0.5 if e == 0 else w1[:, n, e - 1:e]
                    dve.scalar_tensor_tensor(x[:, n, :], d, share, x[:, n, :], ALU.mult, ALU.add
                                             ).then_inc(dn_add, 1)

            def expert(i, side):
                if i < Q * EX:
                    gated(i)
                if i > 1 and i % EX == 1:
                    normalise(dve, 2, i // EX - 1, range(ON_DVE))
                if 0 < i <= Q * EX:
                    add_down(i - 1)
                if i > 0 and i % EX == 0:
                    dve.wait_ge(dn_add, QT * i)
                    statistics(2, i // EX - 1)
                side()

            follow(stage, expert)

        @block.tensor
        def _(pe):
            for j in range(2):
                w = pe.transpose(tr[0][:, j * P:(j + 1) * P],
                                 sg[:, NB * j:NB * (j + 1), :].rearrange("p c e -> p (c e)"), ident[:, :])
            w.then_inc(pr_ps, 1)
            for k in range(2):
                for d in range(4):
                    w = pe.transpose(mm[k][:, d * P:(d + 1) * P], m.w1_nat[:, d, k * P:(k + 1) * P], ident[:, :])
                w.then_inc(w1_ps, 1)

            def y0_piece(k):
                n, part = divmod(k, 2)
                i = n // 2
                if n % 2 == 0 and part == 0:
                    pe.wait_ge(w1_low, 2)
                    at_least(pe, y0_sb, i - 3)
                w = pe.matmul(mm[i % 4][:, (n % 2) * C:(n % 2 + 1) * C], xT[:, part, n * P:(n + 1) * P],
                              m.e0w[:, part, :], start=(part == 0), stop=(part == 1))
                if part == 1 and n % 2 == 1:
                    w.then_inc(y0_ps, 1)

            same = m.same[:, :, :].rearrange("p c e -> p (c e)")
            before = m.before[:, :, :].rearrange("p c e -> p (c e)")
            for r in range(BITS):
                pe.wait_ge(counted, r + 1)
                at_least(pe, cand_ok, r)
                pe.matmul(tr[1][:, r % 2:r % 2 + 1], same, cnt[:, 0:1], start=True, stop=True).then_inc(totals, 1)
                for k in range(2 * NT * r // BITS, 2 * NT * (r + 1) // BITS):
                    y0_piece(k)
            pe.wait_ge(counted, BITS + 1)
            pe.matmul(tr[1][:, 2:5], same, cnt[:, :], start=True, stop=True)
            pe.matmul(tr[1][:, 5:7], before, cnt[:, 1:3], start=True, stop=True).then_inc(totals, 1)
            pe.wait_ge(chosen, 1)
            for j in range(2):
                w = pe.transpose(tr[0][:, j * P:(j + 1) * P], over[:, j, :], ident[:, :])
            w.then_inc(g_ps, 1)
            pe.wait_ge(y0_sb, NT // 2)

            def x2_T(q):
                normed(pe, 0, q)
                for k in range(2):
                    tr_free(pe, TURN, q, k)
                    for t in range(QT):
                        w = pe.transpose(tr[k][:, t * P:(t + 1) * P], x[:, QT * q + t, k * P:(k + 1) * P],
                                         ident[:, :])
                    w.then_inc(x2_ps, 1)

            def three_passes(dst, a, b, first=True, last=True):
                for n, (u, v) in enumerate(((0, 0), (0, 1), (1, 0))):
                    w = pe.matmul(dst, a[u].bitcast(F32R), b[v].bitcast(F32R), start=first and n == 0,
                                  stop=last and n == 2)
                return w

            def linear(q, k):
                for j in range(2):
                    d = 2 * j + k
                    at_least(pe, z_sb, 4 * q + 2 * k + j - 1)
                    for c in range(2):
                        if k == 0 and j == 0:
                            pe.wait_ge(x2_low, 2 * q + c + 1)
                        at = slice(d * P, (d + 1) * P)
                        w = three_passes(zb[j][:, :], (w1T_hi[:, c, at], w1T_lo[:, c, at]),
                                         (x2_hi[:, q % 2, c, :], x2_lo[:, q % 2, c, :]), c == 0, c == 1)
                    w.then_inc(z_ps, 1)

            def hidden_T(q):
                pe.wait_ge(scanned, 2 * (q + 1))
                for i in range(2):
                    tr_free(pe, HID, q, i)
                    for t in range(2):
                        for k in range(2):
                            n = 2 * i + t
                            w = pe.transpose(tr[i][:, (2 * t + k) * P:(2 * t + k + 1) * P],
                                             hid[:, q, k, n * P:(n + 1) * P], ident[:, :])
                    w.then_inc(h_ps, 1)

            def h_T(q):
                pe.wait_ge(xr_ok, QT * (q + 1))
                for k in range(2):
                    tr_free(pe, TURN1, q, k)
                    for t in range(QT):
                        w = pe.transpose(tr[k][:, t * P:(t + 1) * P], xr[:, t, k * P:(k + 1) * P], ident[:, :])
                    w.then_inc(xr_ps, 1)

            def logits(q):
                pe.wait_ge(hlo_ok, 2 * (q + 1))
                pe.wait_ge(r1_ok, 2)
                tr_free(pe, ROUTE0, q, 0)
                for t in range(QT):
                    for k in range(2):
                        at = slice(t * P, (t + 1) * P)
                        w = three_passes(tr[0][:, t * E1:(t + 1) * E1], (hT_hi[:, q, k, at], hT_lo[:, q, k, at]),
                                         (r1_hi[:, k, :], r1_lo[:, k, :]), k == 0, k == 1)
                w.then_inc(lg_ps, 1)

            def stage(g, q):
                if g == TURN:
                    x2_T(q)
                elif g in (LIN0, LIN1):
                    linear(q, g - LIN0)
                elif g == HID:
                    hidden_T(q)
                elif g == TURN1:
                    h_T(q)
                elif g == ROUTE0:
                    logits(q)

            def gate_up(i):
                q, e = divmod(i, EX)
                if e == 0:
                    pe.wait_ge(hlo_ok, 2 * (q + 1))
                if q == 0:
                    pe.wait_ge(wlo_ok, 3 * (e + 1))
                for j, (bank, free) in enumerate(((gb, mul_ok), (ub, act_ok))):
                    at_least(pe, free, i)
                    for k in range(2):
                        w = three_passes(bank[:, :], (w_hi[:, j, e, k, :], w_lo[:, j, e, k, :]),
                                         (hT_hi[:, q, k, :], hT_lo[:, q, k, :]), k == 0, k == 1)
                    w.then_inc(gu_ps, 1)

            def down(i):
                e = i % EX
                pe.wait_ge(hi_ok, i + 1)
                for t in range(QT):
                    if t % 2 == 0:
                        pe.wait_ge(lo_ok, 2 * i + t // 2 + 1)
                        at_least(pe, dn_add, QT * (i - 1) + t + 2)
                    at = slice(t * P, (t + 1) * P)
                    w = three_passes(dn[t // 2][:, (t % 2) * C:(t % 2 + 1) * C],
                                     (act_hi[:, i % 2, at], act_lo[:, i % 2, at]),
                                     (w_hi[:, 2, e].rearrange("p k f -> p (k f)"),
                                      w_lo[:, 2, e].rearrange("p k f -> p (k f)")))
                    if t % 2 == 1:
                        w.then_inc(dn_ps, 1)

            def expert(i, side):
                if i < Q * EX:
                    gate_up(i)
                if 0 < i <= Q * EX:
                    down(i - 1)
                side()

            follow(stage, expert)



INPUTS = ["L0_attn_x", "L0_attn_Wq", "L0_attn_Wk", "L0_attn_Wv", "L0_ffn_router_w", "L0_ffn_router_b",
          "L0_ffn_expert_w", "L0_ffn_expert_b", "L1_attn_W", "L1_attn_b", "L1_ffn_rms_weight", "L1_ffn_router_w",
          "L1_ffn_w_gate", "L1_ffn_w_up", "L1_ffn_w_down", "L1_ffn_sw_gate", "L1_ffn_sw_up", "L1_ffn_sw_down"]


def kernel(**inputs):
    import numpy as np
    import concourse.bacc as bacc
    from concourse.bass_utils import run_bass_kernel_spmd

    nc = bacc.Bacc("TRN2", target_bir_lowering=False, num_devices=1)
    arrays, args = {}, []
    for name in INPUTS:
        a = np.ascontiguousarray(inputs[name])
        arrays[f"in_{name}"] = a
        args.append(nc.dram_tensor(f"in_{name}", a.shape, mybir.dt.from_np(a.dtype), kind="ExternalInput").ap())
    out = nc.dram_tensor("out", (NB, T, C), F32, kind="ExternalOutput").ap()
    program(nc, *args, out)
    return run_bass_kernel_spmd(nc, [arrays], core_ids=[0]).results[0]["out"]
```
